# Optimizing a Trainium2 kernel written in Bass

```python
import numpy as np
import jax
import jax.numpy as jnp

def _softmax(x, axis=-1):
    return jax.nn.softmax(x, axis=axis)

def _gelu(x):
    return jax.nn.gelu(x, approximate=True)

def _silu(x):
    return jax.nn.silu(x)

def _sigmoid(x):
    return jax.nn.sigmoid(x)

def _layernorm(x, axis=-1, eps=1e-05):
    m = jnp.mean(x, axis=axis, keepdims=True)
    v = jnp.var(x, axis=axis, keepdims=True)
    return (x - m) / jnp.sqrt(v + eps)

def _scatter_add(tgt, idx, src, axis=0):
    return tgt.at[idx].add(src)

def _segment_sum(src, seg, n):
    return jax.ops.segment_sum(src, seg, n)
kernel_name = 'mk_audio_tower_d4_tok_audfeat512_r4_1c1fd8'

def setup_inputs(seed: int=0):
    np.random.seed(seed)
    _w = jnp.asarray

    def _rec_inputs():
        import jax
        import jax.numpy as jnp
        _rk = jax.random.key(seed)
        x = -0.0003702 + 0.999946 * jax.random.normal(jax.random.fold_in(_rk, 1), (16, 64, 750), jnp.float32)
        return x
    x = _rec_inputs()

    def _L0_tok_setup():
        import jax, jax.numpy as jnp
        import numpy as np
        PATCH_SIZE = 200
        EMBED_DIM = 128
        IN_FEATURES = 2 * (PATCH_SIZE // 2 + 1)
        HIDDEN = 4 * IN_FEATURES
        key = jax.random.key(seed)
        k_x, k_w1, k_b1, k_w2, k_b2 = jax.random.split(key, 5)
        scale1 = 1.0 / np.sqrt(IN_FEATURES)
        scale2 = 1.0 / np.sqrt(HIDDEN)
        return {'x': jax.random.normal(k_x, (64, 64, 1000), dtype=jnp.float32), 'w1': jax.random.normal(k_w1, (IN_FEATURES, HIDDEN), dtype=jnp.float32) * scale1, 'b1': jax.random.normal(k_b1, (HIDDEN,), dtype=jnp.float32) * scale1, 'w2': jax.random.normal(k_w2, (HIDDEN, EMBED_DIM), dtype=jnp.float32) * scale2, 'b2': jax.random.normal(k_b2, (EMBED_DIM,), dtype=jnp.float32) * scale2}
    _L0_tok_all = _L0_tok_setup()
    _L0_tok_in = {k: v for k, v in _L0_tok_all.items() if k in ('w1', 'b1', 'w2', 'b2')}
    del _L0_tok_all

    def _L0_attn_setup():
        import jax, jax.numpy as jnp
        import numpy as np
        W_WIN = 20
        HOP = 10
        NHEAD = 8

        def _layernorm(x, g, b, eps=1e-05):
            m = x.mean(-1, keepdims=True)
            v = x.var(-1, keepdims=True)
            return (x - m) / jnp.sqrt(v + eps) * g + b

        def _mha(x, w_in, b_in, w_out, b_out):
            Bn, W, E = x.shape
            hd = E // NHEAD
            qkv = x @ w_in.T + b_in
            q, k, v = jnp.split(qkv, 3, axis=-1)
            q = q.reshape(Bn, W, NHEAD, hd)
            k = k.reshape(Bn, W, NHEAD, hd)
            v = v.reshape(Bn, W, NHEAD, hd)
            scores = jnp.einsum('bqhd,bkhd->bhqk', q, k) / jnp.sqrt(jnp.asarray(hd, x.dtype))
            attn = jax.nn.softmax(scores, axis=-1)
            out = jnp.einsum('bhqk,bkhd->bqhd', attn, v).reshape(Bn, W, E)
            return out @ w_out.T + b_out
        key = jax.random.key(seed)
        ks = jax.random.split(key, 4)
        B, L, C = (8, 1024, 128)
        x = jax.random.normal(ks[0], (B, L, C), dtype=jnp.float32)
        ln_g = jnp.ones((C,), jnp.float32)
        ln_b = jnp.zeros((C,), jnp.float32)
        w_in = jax.random.normal(ks[1], (3 * C, C), dtype=jnp.float32) * 0.02
        b_in = jnp.zeros((3 * C,), jnp.float32)
        w_out = jax.random.normal(ks[2], (C, C), dtype=jnp.float32) * 0.02
        b_out = jnp.zeros((C,), jnp.float32)
        return {'x': x, 'ln_g': ln_g, 'ln_b': ln_b, 'w_in': w_in, 'b_in': b_in, 'w_out': w_out, 'b_out': b_out}
    _L0_attn_all = _L0_attn_setup()
    _L0_attn_in = {k: v for k, v in _L0_attn_all.items() if k in ('ln_g', 'ln_b', 'w_in', 'b_in', 'w_out', 'b_out')}
    del _L0_attn_all

    def _L0_ffn_setup():
        import jax, jax.numpy as jnp
        import numpy as np
        B, S, D, H, E = (4, 512, 128, 8, 8)
        FF = 4 * D
        HD = D // H
        EPS = 1e-05

        def _layernorm(x, g, b):
            mu = jnp.mean(x, axis=-1, keepdims=True)
            var = jnp.mean((x - mu) ** 2, axis=-1, keepdims=True)
            return (x - mu) * jax.lax.rsqrt(var + EPS) * g + b
        key = jax.random.key(seed)
        ks = jax.random.split(key, 16)
        s = 0.02
        return {'x': jax.random.normal(ks[0], (B, S, D), dtype=jnp.float32), 'ln1_g': jnp.ones((D,), jnp.float32), 'ln1_b': jnp.zeros((D,), jnp.float32), 'Wq': jax.random.normal(ks[1], (D, D), jnp.float32) * s, 'bq': jnp.zeros((D,), jnp.float32), 'Wk': jax.random.normal(ks[2], (D, D), jnp.float32) * s, 'bk': jnp.zeros((D,), jnp.float32), 'Wv': jax.random.normal(ks[3], (D, D), jnp.float32) * s, 'bv': jnp.zeros((D,), jnp.float32), 'Wo': jax.random.normal(ks[4], (D, D), jnp.float32) * s, 'bo': jnp.zeros((D,), jnp.float32), 'gate_W': jax.random.normal(ks[5], (D, E), jnp.float32) * s, 'gate_b': jnp.zeros((E,), jnp.float32), 'W1': jax.random.normal(ks[6], (E, D, FF), jnp.float32) * s, 'b1': jnp.zeros((E, FF), jnp.float32), 'W2': jax.random.normal(ks[7], (E, FF, D), jnp.float32) * s, 'b2': jnp.zeros((E, D), jnp.float32)}
    _L0_ffn_all = _L0_ffn_setup()
    _L0_ffn_in = {k: v for k, v in _L0_ffn_all.items() if k in ('ln1_g', 'ln1_b', 'Wq', 'bq', 'Wk', 'bk', 'Wv', 'bv', 'Wo', 'bo', 'gate_W', 'gate_b', 'W1', 'b1', 'W2', 'b2')}
    del _L0_ffn_all

    def _L1_attn_setup():
        import jax, jax.numpy as jnp
        import numpy as np
        import math
        D_MODEL = 128
        NUM_HEADS = 8
        D_HEAD = D_MODEL // NUM_HEADS
        key = jax.random.key(seed)
        ks = jax.random.split(key, 8)
        B, S = (2, 512)
        x = jax.random.normal(ks[0], (B, S, D_MODEL), dtype=jnp.float32)
        s = 1.0 / math.sqrt(D_MODEL)
        Wq = jax.random.normal(ks[1], (NUM_HEADS, D_MODEL, D_HEAD), dtype=jnp.float32) * s
        Wk = jax.random.normal(ks[2], (NUM_HEADS, D_MODEL, D_HEAD), dtype=jnp.float32) * s
        Wv = jax.random.normal(ks[3], (NUM_HEADS, D_MODEL, D_HEAD), dtype=jnp.float32) * s
        bq = jax.random.normal(ks[4], (NUM_HEADS, D_HEAD), dtype=jnp.float32) * 0.02
        bk = jax.random.normal(ks[5], (NUM_HEADS, D_HEAD), dtype=jnp.float32) * 0.02
        bv = jax.random.normal(ks[6], (NUM_HEADS, D_HEAD), dtype=jnp.float32) * 0.02
        Wo = jax.random.normal(ks[7], (D_MODEL, D_MODEL), dtype=jnp.float32) * s
        bo = jnp.zeros((D_MODEL,), dtype=jnp.float32)
        return {'x': x, 'Wq': Wq, 'Wk': Wk, 'Wv': Wv, 'bq': bq, 'bk': bk, 'bv': bv, 'Wo': Wo, 'bo': bo}
    _L1_attn_all = _L1_attn_setup()
    _L1_attn_in = {k: v for k, v in _L1_attn_all.items() if k in ('Wq', 'Wk', 'Wv', 'bq', 'bk', 'bv', 'Wo', 'bo')}
    del _L1_attn_all

    def _L1_ffn_setup():
        import jax, jax.numpy as jnp
        import numpy as np
        EPS = 1e-05

        def _bitlinear(x, w):
            w_scale = jnp.clip(jnp.mean(jnp.abs(w)), EPS, None)
            w_q = jnp.clip(jnp.round(w / w_scale), -1.0, 1.0) * w_scale
            w_eff = w + jax.lax.stop_gradient(w_q - w)
            x_scale = 127.0 / jnp.clip(jnp.max(jnp.abs(x), axis=-1, keepdims=True), EPS, None)
            x_q = jnp.clip(jnp.round(x * x_scale), -128.0, 127.0) / x_scale
            x_eff = x + jax.lax.stop_gradient(x_q - x)
            return jnp.einsum('bsi,oi->bso', x_eff, w_eff)

        def _ste_round_clamp_int8(h):
            h_q = jnp.clip(jnp.round(h), -128.0, 127.0)
            return h + jax.lax.stop_gradient(h_q - h)
        key = jax.random.key(seed)
        k1, k2, k3 = jax.random.split(key, 3)
        B, S, D, F = (8, 2048, 128, 512)
        x = jax.random.normal(k1, (B, S, D), dtype=jnp.float32)
        w_up = jax.random.normal(k2, (F, D), dtype=jnp.float32) * (1.0 / np.sqrt(D))
        w_down = jax.random.normal(k3, (D, F), dtype=jnp.float32) * (1.0 / np.sqrt(F))
        return {'x': x, 'w_up': w_up, 'w_down': w_down}
    _L1_ffn_all = _L1_ffn_setup()
    _L1_ffn_in = {k: v for k, v in _L1_ffn_all.items() if k in ('w_up', 'w_down')}
    del _L1_ffn_all

    def _L2_attn_setup():
        import jax, jax.numpy as jnp
        from jax import lax
        import numpy as np

        def make_hippo_matrix(N):
            P = np.sqrt(1 + 2 * np.arange(N))
            A = P[:, None] * P[None, :]
            A = np.tril(A) - np.diag(np.arange(N))
            return jnp.asarray(-A, dtype=jnp.float32)
        key = jax.random.key(seed)
        k1, k2, k3, k4, k5 = jax.random.split(key, 5)
        Bsz, L, H, N = (16, 512, 128, 64)
        dt_min, dt_max = (0.001, 0.1)
        u = jax.random.normal(k1, (Bsz, L, H), dtype=jnp.float32)
        B_ssm = jax.random.normal(k2, (N, 1), dtype=jnp.float32)
        C_ssm = jax.random.normal(k3, (1, N), dtype=jnp.float32)
        D_skip = jax.random.normal(k4, (1,), dtype=jnp.float32)
        log_dt = jax.random.uniform(k5, (1,), dtype=jnp.float32) * (np.log(dt_max) - np.log(dt_min)) + np.log(dt_min)
        return {'u': u, 'B_ssm': B_ssm, 'C_ssm': C_ssm, 'D_skip': D_skip, 'log_dt': log_dt}
    _L2_attn_all = _L2_attn_setup()
    _L2_attn_in = {k: v for k, v in _L2_attn_all.items() if k in ('B_ssm', 'C_ssm', 'D_skip', 'log_dt')}
    del _L2_attn_all

    def _L2_ffn_setup():
        import jax, jax.numpy as jnp
        import numpy as np
        D = 128
        E = 8
        K = 2
        EXP = 4
        LN_EPS = 1e-05
        key = jax.random.key(seed)
        ks = jax.random.split(key, 8)
        B, T = (8, 512)
        Dh = D * EXP
        x = jax.random.normal(ks[0], (B, T, D), dtype=jnp.float32)
        ln_g = jnp.ones((D,), dtype=jnp.float32)
        ln_b = jnp.zeros((D,), dtype=jnp.float32)
        lim_r = np.sqrt(6.0 / (D + E)).astype(np.float32)
        w_r = jax.random.uniform(ks[1], (E, D), dtype=jnp.float32, minval=-lim_r, maxval=lim_r)
        b_r = jnp.zeros((E,), dtype=jnp.float32)
        lim1 = np.sqrt(6.0 / (D + Dh)).astype(np.float32)
        W1 = jax.random.uniform(ks[2], (E, D, Dh), dtype=jnp.float32, minval=-lim1, maxval=lim1)
        b1 = jnp.zeros((E, Dh), dtype=jnp.float32)
        W2 = jax.random.uniform(ks[3], (E, Dh, D), dtype=jnp.float32, minval=-lim1, maxval=lim1)
        b2 = jnp.zeros((E, D), dtype=jnp.float32)
        return {'x': x, 'ln_g': ln_g, 'ln_b': ln_b, 'w_r': w_r, 'b_r': b_r, 'W1': W1, 'b1': b1, 'W2': W2, 'b2': b2}
    _L2_ffn_all = _L2_ffn_setup()
    _L2_ffn_in = {k: v for k, v in _L2_ffn_all.items() if k in ('ln_g', 'ln_b', 'w_r', 'b_r', 'W1', 'b1', 'W2', 'b2')}
    del _L2_ffn_all

    def _L3_attn_setup():
        import jax, jax.numpy as jnp
        import numpy as np
        N_HEADS = 8
        D_MODEL = 128
        HEAD_DIM = D_MODEL // N_HEADS
        BATCH = 32
        SEQ = 128
        key = jax.random.key(seed)
        kx, kq, kv = jax.random.split(key, 3)
        x = jax.random.normal(kx, (BATCH, SEQ, D_MODEL), dtype=jnp.float32)
        Q = jax.random.uniform(kq, (N_HEADS, D_MODEL, D_MODEL), dtype=jnp.float32, minval=-0.1, maxval=0.1)
        V = jax.random.uniform(kv, (N_HEADS, D_MODEL, HEAD_DIM), dtype=jnp.float32, minval=-0.1, maxval=0.1)
        return {'input': x, 'Q': Q, 'V': V}
    _L3_attn_all = _L3_attn_setup()
    _L3_attn_in = {k: v for k, v in _L3_attn_all.items() if k in ('Q', 'V')}
    del _L3_attn_all

    def _L3_ffn_setup():
        import jax, jax.numpy as jnp
        import numpy as np
        NUM_EXPERTS = 32
        GROUP_SIZE = 4
        NUM_GROUPS = NUM_EXPERTS // GROUP_SIZE
        C_CAP = 1.0
        key = jax.random.key(seed)
        ks = jax.random.split(key, 5)
        B, S, H = (16, 512, 128)
        D_FF = int(H * 4 * (2.0 / 3.0))
        x = jax.random.normal(ks[0], (B, S, H), dtype=jnp.float32)
        W_router = jax.random.normal(ks[1], (H, NUM_EXPERTS), dtype=jnp.float32) * (1.0 / np.sqrt(H))
        b_router = jnp.zeros((NUM_EXPERTS,), dtype=jnp.float32)
        W_up = jax.random.normal(ks[2], (NUM_GROUPS, H, D_FF), dtype=jnp.float32) * (1.0 / np.sqrt(H))
        b_up = jnp.zeros((NUM_GROUPS, D_FF), dtype=jnp.float32)
        W_down = jax.random.normal(ks[3], (NUM_EXPERTS, D_FF, H), dtype=jnp.float32) * (1.0 / np.sqrt(D_FF))
        b_down = jnp.zeros((NUM_EXPERTS, H), dtype=jnp.float32)
        return {'x': x, 'W_router': W_router, 'b_router': b_router, 'W_up': W_up, 'b_up': b_up, 'W_down': W_down, 'b_down': b_down}
    _L3_ffn_all = _L3_ffn_setup()
    _L3_ffn_in = {k: v for k, v in _L3_ffn_all.items() if k in ('W_router', 'b_router', 'W_up', 'b_up', 'W_down', 'b_down')}
    del _L3_ffn_all
    return {'x': x, 'L0_tok_w1': _L0_tok_in['w1'], 'L0_tok_b1': _L0_tok_in['b1'], 'L0_tok_w2': _L0_tok_in['w2'], 'L0_tok_b2': _L0_tok_in['b2'], 'L0_attn_ln_g': _L0_attn_in['ln_g'], 'L0_attn_ln_b': _L0_attn_in['ln_b'], 'L0_attn_w_in': _L0_attn_in['w_in'], 'L0_attn_b_in': _L0_attn_in['b_in'], 'L0_attn_w_out': _L0_attn_in['w_out'], 'L0_attn_b_out': _L0_attn_in['b_out'], 'L0_ffn_ln1_g': _L0_ffn_in['ln1_g'], 'L0_ffn_ln1_b': _L0_ffn_in['ln1_b'], 'L0_ffn_Wq': _L0_ffn_in['Wq'], 'L0_ffn_bq': _L0_ffn_in['bq'], 'L0_ffn_Wk': _L0_ffn_in['Wk'], 'L0_ffn_bk': _L0_ffn_in['bk'], 'L0_ffn_Wv': _L0_ffn_in['Wv'], 'L0_ffn_bv': _L0_ffn_in['bv'], 'L0_ffn_Wo': _L0_ffn_in['Wo'], 'L0_ffn_bo': _L0_ffn_in['bo'], 'L0_ffn_gate_W': _L0_ffn_in['gate_W'], 'L0_ffn_gate_b': _L0_ffn_in['gate_b'], 'L0_ffn_W1': _L0_ffn_in['W1'], 'L0_ffn_b1': _L0_ffn_in['b1'], 'L0_ffn_W2': _L0_ffn_in['W2'], 'L0_ffn_b2': _L0_ffn_in['b2'], 'L1_attn_Wq': _L1_attn_in['Wq'], 'L1_attn_Wk': _L1_attn_in['Wk'], 'L1_attn_Wv': _L1_attn_in['Wv'], 'L1_attn_bq': _L1_attn_in['bq'], 'L1_attn_bk': _L1_attn_in['bk'], 'L1_attn_bv': _L1_attn_in['bv'], 'L1_attn_Wo': _L1_attn_in['Wo'], 'L1_attn_bo': _L1_attn_in['bo'], 'L1_ffn_w_up': _L1_ffn_in['w_up'], 'L1_ffn_w_down': _L1_ffn_in['w_down'], 'L2_attn_B_ssm': _L2_attn_in['B_ssm'], 'L2_attn_C_ssm': _L2_attn_in['C_ssm'], 'L2_attn_D_skip': _L2_attn_in['D_skip'], 'L2_attn_log_dt': _L2_attn_in['log_dt'], 'L2_ffn_ln_g': _L2_ffn_in['ln_g'], 'L2_ffn_ln_b': _L2_ffn_in['ln_b'], 'L2_ffn_w_r': _L2_ffn_in['w_r'], 'L2_ffn_b_r': _L2_ffn_in['b_r'], 'L2_ffn_W1': _L2_ffn_in['W1'], 'L2_ffn_b1': _L2_ffn_in['b1'], 'L2_ffn_W2': _L2_ffn_in['W2'], 'L2_ffn_b2': _L2_ffn_in['b2'], 'L3_attn_Q': _L3_attn_in['Q'], 'L3_attn_V': _L3_attn_in['V'], 'L3_ffn_W_router': _L3_ffn_in['W_router'], 'L3_ffn_b_router': _L3_ffn_in['b_router'], 'L3_ffn_W_up': _L3_ffn_in['W_up'], 'L3_ffn_b_up': _L3_ffn_in['b_up'], 'L3_ffn_W_down': _L3_ffn_in['W_down'], 'L3_ffn_b_down': _L3_ffn_in['b_down']}

def reference(x, L0_tok_w1, L0_tok_b1, L0_tok_w2, L0_tok_b2, L0_attn_ln_g, L0_attn_ln_b, L0_attn_w_in, L0_attn_b_in, L0_attn_w_out, L0_attn_b_out, L0_ffn_ln1_g, L0_ffn_ln1_b, L0_ffn_Wq, L0_ffn_bq, L0_ffn_Wk, L0_ffn_bk, L0_ffn_Wv, L0_ffn_bv, L0_ffn_Wo, L0_ffn_bo, L0_ffn_gate_W, L0_ffn_gate_b, L0_ffn_W1, L0_ffn_b1, L0_ffn_W2, L0_ffn_b2, L1_attn_Wq, L1_attn_Wk, L1_attn_Wv, L1_attn_bq, L1_attn_bk, L1_attn_bv, L1_attn_Wo, L1_attn_bo, L1_ffn_w_up, L1_ffn_w_down, L2_attn_B_ssm, L2_attn_C_ssm, L2_attn_D_skip, L2_attn_log_dt, L2_ffn_ln_g, L2_ffn_ln_b, L2_ffn_w_r, L2_ffn_b_r, L2_ffn_W1, L2_ffn_b1, L2_ffn_W2, L2_ffn_b2, L3_attn_Q, L3_attn_V, L3_ffn_W_router, L3_ffn_b_router, L3_ffn_W_up, L3_ffn_b_up, L3_ffn_W_down, L3_ffn_b_down):
    import jax
    import jax.numpy as jnp

    def _L0_tok_ref(x, w1, b1, w2, b2):
        import jax, jax.numpy as jnp
        import numpy as np
        PATCH_SIZE = 200
        EMBED_DIM = 128
        IN_FEATURES = 2 * (PATCH_SIZE // 2 + 1)
        HIDDEN = 4 * IN_FEATURES
        B, C, T = x.shape
        P = PATCH_SIZE
        pad = -T % P
        if pad:
            x = jnp.pad(x, ((0, 0), (0, 0), (0, pad)))
            T = T + pad
        S = T // P
        xp = x.reshape(B, C, S, P)
        fr = jnp.fft.rfft(xp, axis=-1)
        feats = jnp.concatenate([jnp.abs(fr), jnp.angle(fr)], axis=-1)
        h = jax.nn.gelu(feats @ w1 + b1, approximate=False)
        out = h @ w2 + b2
        return out.reshape(B, C * S, EMBED_DIM)

    def _L0_attn_ref(x, ln_g, ln_b, w_in, b_in, w_out, b_out):
        import jax, jax.numpy as jnp
        import numpy as np
        W_WIN = 20
        HOP = 10
        NHEAD = 8

        def _layernorm(x, g, b, eps=1e-05):
            m = x.mean(-1, keepdims=True)
            v = x.var(-1, keepdims=True)
            return (x - m) / jnp.sqrt(v + eps) * g + b

        def _mha(x, w_in, b_in, w_out, b_out):
            Bn, W, E = x.shape
            hd = E // NHEAD
            qkv = x @ w_in.T + b_in
            q, k, v = jnp.split(qkv, 3, axis=-1)
            q = q.reshape(Bn, W, NHEAD, hd)
            k = k.reshape(Bn, W, NHEAD, hd)
            v = v.reshape(Bn, W, NHEAD, hd)
            scores = jnp.einsum('bqhd,bkhd->bhqk', q, k) / jnp.sqrt(jnp.asarray(hd, x.dtype))
            attn = jax.nn.softmax(scores, axis=-1)
            out = jnp.einsum('bhqk,bkhd->bqhd', attn, v).reshape(Bn, W, E)
            return out @ w_out.T + b_out
        B, L, C = x.shape
        starts = np.arange(0, L - W_WIN + 1, HOP)
        S = starts.shape[0]
        idx = starts[:, None] + np.arange(W_WIN)
        segs = x[:, idx].reshape(B * S, W_WIN, C)
        normed = _layernorm(segs, ln_g, ln_b)
        segs_out = normed + _mha(normed, w_in, b_in, w_out, b_out)
        chunks = segs_out.reshape(S, B, W_WIN, C)
        vals = chunks.transpose(1, 0, 2, 3).reshape(B, S * W_WIN, C)
        flat_idx = idx.reshape(-1)
        out = jnp.zeros_like(x).at[:, flat_idx].add(vals)
        cnt = jnp.zeros((B, L), x.dtype).at[:, flat_idx].add(1.0)
        return out / jnp.clip(cnt, 1.0)[..., None] + x

    def _L0_ffn_ref(x, ln1_g, ln1_b, Wq, bq, Wk, bk, Wv, bv, Wo, bo, gate_W, gate_b, W1, b1, W2, b2):
        import jax, jax.numpy as jnp
        import numpy as np
        B, S, D, H, E = (4, 512, 128, 8, 8)
        FF = 4 * D
        HD = D // H
        EPS = 1e-05

        def _layernorm(x, g, b):
            mu = jnp.mean(x, axis=-1, keepdims=True)
            var = jnp.mean((x - mu) ** 2, axis=-1, keepdims=True)
            return (x - mu) * jax.lax.rsqrt(var + EPS) * g + b
        b, s, d = x.shape
        q = (x @ Wq + bq).reshape(b, s, H, HD)
        k = (x @ Wk + bk).reshape(b, s, H, HD)
        v = (x @ Wv + bv).reshape(b, s, H, HD)
        scores = jnp.einsum('bqhd,bkhd->bhqk', q, k) / jnp.sqrt(jnp.float32(HD))
        attn = jax.nn.softmax(scores, axis=-1)
        o = jnp.einsum('bhqk,bkhd->bqhd', attn, v).reshape(b, s, d) @ Wo + bo
        h = _layernorm(x + o, ln1_g, ln1_b)
        t = h.reshape(b * s, d)
        probs = jax.nn.softmax(t @ gate_W + gate_b, axis=-1)
        idx = jnp.argmax(probs, axis=-1)
        gw = jnp.max(probs, axis=-1)
        hid = jax.nn.gelu(jnp.einsum('nd,edf->enf', t, W1) + b1[:, None, :])
        out_all = jnp.einsum('enf,efd->end', hid, W2) + b2[:, None, :]
        onehot = jax.nn.one_hot(idx, E, dtype=t.dtype)
        out = jnp.einsum('ne,end->nd', onehot, out_all)
        out = out * gw[:, None]
        return out.reshape(b, s, d)

    def _L1_attn_ref(x, Wq, Wk, Wv, bq, bk, bv, Wo, bo):
        import jax, jax.numpy as jnp
        import numpy as np
        import math
        D_MODEL = 128
        NUM_HEADS = 8
        D_HEAD = D_MODEL // NUM_HEADS
        Q = jnp.einsum('bsd,hde->bhse', x, Wq) + bq[None, :, None, :]
        K = jnp.einsum('bsd,hde->bhse', x, Wk) + bk[None, :, None, :]
        V = jnp.einsum('bsd,hde->bhse', x, Wv) + bv[None, :, None, :]
        scale = 1.0 / math.sqrt(D_HEAD)
        scores = jnp.einsum('bhqe,bhke->bhqk', Q, K) * scale
        attn = jax.nn.softmax(scores, axis=-1)
        out = jnp.einsum('bhqk,bhke->bhqe', attn, V)
        B, H, S, d = out.shape
        concat = out.transpose(0, 2, 1, 3).reshape(B, S, H * d)
        return jnp.einsum('bsd,de->bse', concat, Wo) + bo

    def _L1_ffn_ref(x, w_up, w_down):
        import jax, jax.numpy as jnp
        import numpy as np
        EPS = 1e-05

        def _bitlinear(x, w):
            w_scale = jnp.clip(jnp.mean(jnp.abs(w)), EPS, None)
            w_q = jnp.clip(jnp.round(w / w_scale), -1.0, 1.0) * w_scale
            w_eff = w + jax.lax.stop_gradient(w_q - w)
            x_scale = 127.0 / jnp.clip(jnp.max(jnp.abs(x), axis=-1, keepdims=True), EPS, None)
            x_q = jnp.clip(jnp.round(x * x_scale), -128.0, 127.0) / x_scale
            x_eff = x + jax.lax.stop_gradient(x_q - x)
            return jnp.einsum('bsi,oi->bso', x_eff, w_eff)

        def _ste_round_clamp_int8(h):
            h_q = jnp.clip(jnp.round(h), -128.0, 127.0)
            return h + jax.lax.stop_gradient(h_q - h)
        h = _bitlinear(x, w_up)
        h = jax.nn.relu(h)
        h = _ste_round_clamp_int8(h)
        return _bitlinear(h, w_down)

    def _L2_attn_ref(u, B_ssm, C_ssm, D_skip, log_dt):
        import jax, jax.numpy as jnp
        from jax import lax
        import numpy as np

        def make_hippo_matrix(N):
            P = np.sqrt(1 + 2 * np.arange(N))
            A = P[:, None] * P[None, :]
            A = np.tril(A) - np.diag(np.arange(N))
            return jnp.asarray(-A, dtype=jnp.float32)
        Bsz, L, H = u.shape
        N = B_ssm.shape[0]
        A = make_hippo_matrix(N)
        dt = jnp.exp(log_dt)
        A_bar = jax.scipy.linalg.expm(dt * A)
        B_bar = jnp.linalg.solve(A, (A_bar - jnp.eye(N, dtype=A.dtype)) @ B_ssm)

        def step(power, _):
            kk = (C_ssm @ power)[0, 0]
            return (A_bar @ power, kk)
        _, K = lax.scan(step, B_bar, None, length=L)
        Krev = K[::-1]
        n_fft = 2 * L
        Uf = jnp.fft.rfft(u, n=n_fft, axis=1)
        Kf = jnp.fft.rfft(Krev, n=n_fft)
        y_conv = jnp.fft.irfft(Uf * Kf[None, :, None], n=n_fft, axis=1)[:, :L, :]
        y = y_conv.astype(u.dtype) + D_skip * u
        return y

    def _L2_ffn_ref(x, ln_g, ln_b, w_r, b_r, W1, b1, W2, b2):
        import jax, jax.numpy as jnp
        import numpy as np
        D = 128
        E = 8
        K = 2
        EXP = 4
        LN_EPS = 1e-05
        B, T, d = x.shape
        mu = jnp.mean(x, axis=-1, keepdims=True)
        var = jnp.mean(jnp.square(x - mu), axis=-1, keepdims=True)
        h = (x - mu) * jax.lax.rsqrt(var + LN_EPS) * ln_g + ln_b
        logits = jnp.einsum('btd,ed->bte', h, w_r) + b_r
        topk_vals, topk_idx = jax.lax.top_k(logits, K)
        gates = jax.nn.softmax(topk_vals, axis=-1)
        hf = h.reshape(B * T, d)
        hid = jax.nn.gelu(jnp.einsum('nd,edf->nef', hf, W1) + b1, approximate=False)
        expert_stack = jnp.einsum('nef,efd->ned', hid, W2) + b2
        idx_flat = topk_idx.reshape(B * T, K)
        gates_flat = gates.reshape(B * T, K)
        gathered = jnp.take_along_axis(expert_stack, idx_flat[:, :, None], axis=1)
        mixed = jnp.sum(gathered * gates_flat[:, :, None], axis=1).reshape(B, T, d)
        return x + mixed

    def _L3_attn_ref(input, Q, V):
        import jax, jax.numpy as jnp
        import numpy as np
        N_HEADS = 8
        D_MODEL = 128
        HEAD_DIM = D_MODEL // N_HEADS
        BATCH = 32
        SEQ = 128
        scores = jnp.einsum('bnd,hde,bme->bhnm', input, Q, input)
        w = jax.nn.softmax(scores, axis=-1)
        weighted = jnp.einsum('bhnm,bmd->bhnd', w, input)
        out = jnp.einsum('bhnd,hdk->bhnk', weighted, V)
        B, H, N, K = out.shape
        return out.transpose(0, 2, 1, 3).reshape(B, N, H * K)

    def _L3_ffn_ref(x, W_router, b_router, W_up, b_up, W_down, b_down):
        import jax, jax.numpy as jnp
        import numpy as np
        NUM_EXPERTS = 32
        GROUP_SIZE = 4
        NUM_GROUPS = NUM_EXPERTS // GROUP_SIZE
        C_CAP = 1.0
        B, S, H = x.shape
        bs = B * S
        E = NUM_EXPERTS
        k = min(int(bs * C_CAP) // E, bs)
        xf = x.reshape(bs, H)
        h = xf @ W_router + b_router
        Sm = jax.nn.softmax(h, axis=-1)
        G_ek, idx_ek = jax.lax.top_k(Sm.T, k)
        tokens = xf[idx_ek]
        D_FF = W_up.shape[-1]
        tok_g = tokens.reshape(NUM_GROUPS, GROUP_SIZE, k, H)
        up = jnp.einsum('gjkh,ghf->gjkf', tok_g, W_up) + b_up[:, None, None, :]
        act = jax.nn.silu(up).reshape(E, k, D_FF)
        Eout = jnp.einsum('ekf,efh->ekh', act, W_down) + b_down[:, None, :]
        weighted = G_ek[..., None] * Eout
        y = jnp.zeros((bs, H), dtype=x.dtype).at[idx_ek.reshape(-1)].add(weighted.reshape(-1, H))
        return y.reshape(B, S, H)
    h = _L0_tok_ref(x, L0_tok_w1, L0_tok_b1, L0_tok_w2, L0_tok_b2)
    h = h + _L0_attn_ref(_layernorm(h, axis=-1), L0_attn_ln_g, L0_attn_ln_b, L0_attn_w_in, L0_attn_b_in, L0_attn_w_out, L0_attn_b_out)
    h = h + _L0_ffn_ref(_layernorm(h, axis=-1), L0_ffn_ln1_g, L0_ffn_ln1_b, L0_ffn_Wq, L0_ffn_bq, L0_ffn_Wk, L0_ffn_bk, L0_ffn_Wv, L0_ffn_bv, L0_ffn_Wo, L0_ffn_bo, L0_ffn_gate_W, L0_ffn_gate_b, L0_ffn_W1, L0_ffn_b1, L0_ffn_W2, L0_ffn_b2)
    h = h + _L1_attn_ref(_layernorm(h, axis=-1), L1_attn_Wq, L1_attn_Wk, L1_attn_Wv, L1_attn_bq, L1_attn_bk, L1_attn_bv, L1_attn_Wo, L1_attn_bo)
    h = h + _L1_ffn_ref(_layernorm(h, axis=-1), L1_ffn_w_up, L1_ffn_w_down)
    h = h + _L2_attn_ref(_layernorm(h, axis=-1), L2_attn_B_ssm, L2_attn_C_ssm, L2_attn_D_skip, L2_attn_log_dt)
    h = h + _L2_ffn_ref(_layernorm(h, axis=-1), L2_ffn_ln_g, L2_ffn_ln_b, L2_ffn_w_r, L2_ffn_b_r, L2_ffn_W1, L2_ffn_b1, L2_ffn_W2, L2_ffn_b2)
    h = h + _L3_attn_ref(_layernorm(h, axis=-1), L3_attn_Q, L3_attn_V)
    h = h + _L3_ffn_ref(_layernorm(h, axis=-1), L3_ffn_W_router, L3_ffn_b_router, L3_ffn_W_up, L3_ffn_b_up, L3_ffn_W_down, L3_ffn_b_down)
    return h

_drawn_inputs = setup_inputs


def setup_inputs(seed=0):
    import zlib

    import numpy as np

    out = dict(_drawn_inputs(seed))
    spreads = {'L0_attn_ln_g': (1.0, 0.571),
     'L0_attn_ln_b': (0.0, 0.572),
     'L0_attn_b_in': (0.0, 0.8),
     'L0_attn_b_out': (0.0, 0.601),
     'L0_ffn_ln1_g': (1.0, 0.6),
     'L0_ffn_ln1_b': (0.0, 0.8),
     'L0_ffn_bq': (0.0, 0.8),
     'L0_ffn_bk': (0.0, 2.0),
     'L0_ffn_bv': (0.0, 0.8),
     'L0_ffn_bo': (0.0, 0.8),
     'L0_ffn_gate_b': (0.0, 0.8),
     'L0_ffn_b1': (0.0, 0.8),
     'L0_ffn_b2': (0.0, 0.8),
     'L1_attn_bo': (0.0, 0.601),
     'L2_ffn_ln_g': (1.0, 0.6),
     'L2_ffn_ln_b': (0.0, 0.554),
     'L2_ffn_b_r': (0.0, 0.75),
     'L2_ffn_b1': (0.0, 0.8),
     'L2_ffn_b2': (0.0, 0.8),
     'L3_ffn_b_router': (0.0, 0.8),
     'L3_ffn_b_up': (0.0, 0.8),
     'L3_ffn_b_down': (0.0, 2.0)}
    factors = {'L0_tok_b1': 5.623,
     'L0_tok_b2': 7.781,
     'L0_attn_w_in': 7.898,
     'L0_attn_w_out': 7.233,
     'L0_ffn_Wq': 8.0,
     'L0_ffn_Wk': 8.0,
     'L0_ffn_Wv': 8.0,
     'L0_ffn_Wo': 8.0,
     'L0_ffn_gate_W': 8.0,
     'L0_ffn_W1': 8.0,
     'L0_ffn_W2': 8.0,
     'L1_attn_Wq': 8.0,
     'L1_attn_Wk': 8.0,
     'L1_attn_bq': 8.0,
     'L1_attn_bk': 64.0,
     'L1_attn_bv': 8.0,
     'L3_ffn_W_router': 6.365,
     'L3_ffn_W_up': 6.808,
     'L3_ffn_W_down': 6.229}
    for name, (base, spread) in spreads.items():
        noise = np.random.default_rng([zlib.crc32(name.encode()), seed]).standard_normal(out[name].shape)
        drawn = base * np.exp(spread * noise) if base else spread * noise
        out[name] = jnp.asarray(drawn.astype(out[name].dtype))
    for name, factor in factors.items():
        out[name] = (out[name] * factor).astype(out[name].dtype)
    return out
```

```python
from contextlib import ExitStack

import numpy as np
import concourse.bass as bass
from concourse import mybir
from concourse.alu_op_type import AluOpType as ALU

F32 = mybir.dt.float32
BF16 = mybir.dt.bfloat16
U32 = mybir.dt.uint32
I32 = mybir.dt.int32
ACT = mybir.ActivationFunctionType
AX = mybir.AxisListType

P = 128
NB = 16
L = 256
D = 128
NT = NB * L // P
NH, HD = 8, 16
HV = HD + 1
PATCH, NPATCH, HP = 200, 4, 100
NF = PATCH // 2 + 1
NHID = 8
WIN, HOP = 20, 10
NW = (L - WIN) // HOP + 1
WT = 120
EPS = 1e-5
NE, FF = 8, 512
KF = FF // P
EC, ECF = 32, 341
ECK = NB * L // EC
ECG = 4
ECT = [(0, 128), (128, 128), (256, 85)]
NSTATE = 64
SQUARINGS = 12
MAGIC = 1.5 * 2.0 ** 23
NEG = -1e30
TINY = 1e-37


class NS:
    pass


def window_offset(w):
    return HOP * (w // 2) + WT * (w % 2)


class Sems:

    def __init__(self, nc, ctx, phase, names):
        self.s = {n: ctx.enter_context(nc.semaphore(f"{phase}_{n}")) for n in names.split()}

    def __getitem__(self, name):
        return self.s[name]

    def restart(self, nc):
        with nc.Block() as block:

            @block.gpsimd
            def _(pool):
                for sem in self.s.values():
                    pool.sem_clear(sem)


def ln_scales(nc, t, phase):
    with ExitStack() as ctx:
        s, n = t.ln_sems, t.ln_uses + 1
        t.ln_uses = n
        tmp = ctx.enter_context(nc.sbuf_tensor(f"{phase}_tmp", [P, 4, NT], F32))
        with nc.Block() as block:

            @block.vector
            def _(dve):
                me, mo = t.BN[:, :, 1], t.BN[:, :, 4]
                ve, vo = t.BN[:, :, 2], t.BN[:, :, 5]
                dve.tensor_tensor(tmp[:, 0], me, mo, ALU.subtract)
                dve.tensor_tensor(tmp[:, 1], ve, vo, ALU.add)
                dve.tensor_tensor(t.MEAN[:, :], me, mo, ALU.add)
                dve.drain()
                dve.tensor_tensor(tmp[:, 0], tmp[:, 0], tmp[:, 0], ALU.mult)
                dve.tensor_scalar(tmp[:, 1], tmp[:, 1], 1.0 / D, EPS, ALU.mult, ALU.add)
                dve.tensor_scalar(t.MEAN[:, :], t.MEAN[:, :], 0.5, None, ALU.mult)
                dve.drain()
                dve.scalar_tensor_tensor(tmp[:, 2], tmp[:, 0], 0.25, tmp[:, 1], ALU.mult, ALU.add)\
                   .then_inc(s["var_ready"], 1)
                dve.wait_ge(s["root_ready"], n)
                dve.reciprocal(t.RSTD[:, :], tmp[:, 3])
                dve.drain()
                dve.tensor_tensor(tmp[:, 0], t.RSTD[:, :], t.RSTD[:, :], ALU.mult)
                dve.drain()
                dve.tensor_tensor(tmp[:, 0], tmp[:, 0], tmp[:, 2], ALU.mult)
                dve.drain()
                dve.tensor_scalar(tmp[:, 0], tmp[:, 0], -0.5, 1.5, ALU.mult, ALU.add)
                dve.drain()
                dve.tensor_tensor(t.RSTD[:, :], t.RSTD[:, :], tmp[:, 0], ALU.mult)

            @block.scalar
            def _(act):
                act.wait_ge(s["var_ready"], n)
                act.activation(tmp[:, 3], tmp[:, 2], ACT.Sqrt).then_inc(s["root_ready"], 1)


def setup(nc, t, a, ctx):
    s = Sems(nc, ctx, "setup", "loaded zeroed scratch_zeroed")
    zero = ctx.enter_context(nc.sbuf_tensor("zero_tile", [P, 2048], F32))
    loads = [(t.ident, a["c_ident"]), (t.w1, a["tok_w1"]), (t.b1, a["tok_b1"]), (t.w2, a["tok_w2"]),
             (t.b2, a["tok_b2"]), (t.dft, a["c_dft"])]
    with nc.Block() as block:

        @block.sync
        def _(sp):
            for dst, src in loads:
                sp.dma_start(dst[tuple(slice(None) for _ in dst.shape)], src).then_inc(s["loaded"], 16)
            sp.wait_ge(s["loaded"], 16 * len(loads))

        @block.vector
        def _(dve):
            dve.memset(zero[:, :], 0.0).then_inc(s["zeroed"], 1)

        @block.scalar
        def _(act):
            act.wait_ge(s["zeroed"], 1)
            n = 0
            for buf in (t.XS1, t.XS2):
                rows = buf.rearrange("(p r) c -> p (r c)", p=P)
                for c in range(0, rows.shape[1], 2048):
                    m = min(2048, rows.shape[1] - c)
                    act.dma_start(rows[:, c:c + m], zero[:, 0:m]).then_inc(s["scratch_zeroed"], 16)
                    n += 16
            act.wait_ge(s["scratch_zeroed"], n)


def tokenizer(nc, t, a):
    N = 2 * L
    with ExitStack() as ctx:
        def sb(name, shape, dt=F32):
            return ctx.enter_context(nc.sbuf_tensor(f"tok_{name}", shape, dt))

        s = Sems(nc, ctx, "tok", "w1_doubled padded loaded0 loaded1 tr xt dft squares sum mag ratio atan feat "
                                 "hid_ps hid out_ps stored")
        rows = [sb(f"rows{i}", [P, 2 * NPATCH * HP]) for i in range(2)]
        xt = [sb(f"xt{i}", [HP, 2, P, NPATCH]) for i in range(2)]
        feat = [sb(f"feat{i}", [NF, 2, N]) for i in range(2)]
        sq = [sb(f"sq{i}", [NF, 2, N]) for i in range(2)]
        den = [sb(f"den{i}", [NF, N]) for i in range(2)]
        rat = [sb(f"rat{i}", [NF, N]) for i in range(2)]
        at = [sb(f"at{i}", [NF, N]) for i in range(2)]
        hid = [sb(f"hid{i}", [NF, NHID, N]) for i in range(2)]
        T = a["x"].shape[2]
        x_rows = a["x"].rearrange("b c t -> (b c) t")
        PS = t.PS

        with nc.Block() as block:

            @block.sync
            def _(sp):
                sp.wait_ge(s["padded"], 2)
                with sp.Fori(0, NB // 4) as k:
                    for p in range(2):
                        sp.wait_ge(s["tr"], k * 2 + p + 1)
                        sp.dma_start(rows[p][:, 0:T], x_rows[bass.ds((k * 2 + p) * P, P), :])\
                          .then_inc(s[f"loaded{p}"], 16)

            @block.tensor
            def _(pe):
                pe.wait_ge(s["w1_doubled"], 1)
                pe.nop().then_inc(s["tr"], 2)
                with pe.Fori(0, NB // 4) as k:
                    for p in range(2):
                        pe.wait_ge(s[f"loaded{p}"], k * 16 + 16)
                        for j in range(2 * NPATCH):
                            mm = pe.transpose(PS[0:HP, j % 2, (j // 2) * P:(j // 2 + 1) * P],
                                              rows[p][:, j * HP:(j + 1) * HP], t.ident[:, :])
                        mm.then_inc(s["tr"], 1)
                        pe.wait_ge(s["xt"], (k * 2 + p + 1) * 2)
                        if p == 1:
                            pe.wait_ge(s["feat"], k * 2 + 1)
                        for part in range(2):
                            for half in range(2):
                                mm = pe.matmul(PS[0:NF, 2 + part, :], t.dft[:, half, part, :],
                                               xt[p][:, half].rearrange("h q s -> h (q s)"),
                                               start=(half == 0), stop=(half == 1))
                        mm.then_inc(s["dft"], 1)
                    for p in range(2):
                        pe.wait_ge(s["feat"], k * 2 + p + 1)
                        for m in range(NHID):
                            pe.wait_ge(s["hid"], k * 16 + p * 8 + m + 7)
                            for f in range(2):
                                mm = pe.matmul(PS[0:NF, 4 + m % 2, :], t.w1[:, f, m * NF:(m + 1) * NF],
                                               feat[p][:, f, :], start=(f == 0), stop=(f == 1))
                            mm.then_inc(s["hid_ps"], 1)
                        pe.wait_ge(s["hid"], k * 16 + p * 8 + 16)
                        pe.wait_ge(s["stored"], k * 2 + p + 1)
                        for q in range(4):
                            for m in range(NHID):
                                mm = pe.matmul(PS[:, 6 + p, q * D:(q + 1) * D],
                                               hid[p][:, m, q * P:(q + 1) * P], t.w2[:, m, :],
                                               start=(m == 0), stop=(m == NHID - 1))
                        mm.then_inc(s["out_ps"], 1)

            @block.scalar
            def _(act):
                act.nop().then_inc(s["hid"], 8)
                with act.Fori(0, NB // 4) as k:
                    for p in range(2):
                        act.wait_ge(s["tr"], k * 2 + p + 3)
                        act.activation(xt[p][:, 0].rearrange("h q s -> h s q"),
                                       PS[0:HP, 0, :].rearrange("h (s q) -> h s q", s=NPATCH),
                                       ACT.Copy).then_inc(s["xt"], 1)
                        act.wait_ge(s["dft"], k * 2 + p + 1)
                        act.activation(den[p][:, :], PS[0:NF, 2, :], ACT.Abs)
                        act.activation(sq[p][:, 0], PS[0:NF, 2, :], ACT.Square)
                        act.activation(sq[p][:, 1], PS[0:NF, 3, :], ACT.Square).then_inc(s["squares"], 1)
                        act.wait_ge(s["sum"], k * 2 + p + 1)
                        act.activation(feat[p][:, 0], sq[p][:, 0], ACT.Sqrt).then_inc(s["mag"], 1)
                        act.wait_ge(s["ratio"], k * 2 + p + 1)
                        act.activation(at[p][:, :], rat[p][:, :], ACT.Arctan).then_inc(s["atan"], 1)
                    for p in range(2):
                        for m in range(NHID):
                            act.wait_ge(s["hid_ps"], k * 16 + p * 8 + m + 1)
                            act.activation(hid[p][:, m], PS[0:NF, 4 + m % 2, :], ACT.Gelu,
                                           bias=t.b1[:, m:m + 1]).then_inc(s["hid"], 1)

            @block.vector
            def _(dve):
                for p in range(2):
                    dve.memset(rows[p][:, T:], 0.0).then_inc(s["padded"], 1)
                dve.tensor_scalar(t.w1[:, 1, :], t.w1[:, 1, :], 2.0, None, ALU.mult)\
                   .then_inc(s["w1_doubled"], 1)
                dve.nop().then_inc(s["stored"], 2)
                with dve.Fori(0, NB // 4) as k:
                    for p in range(2):
                        re, im = PS[0:NF, 2, :], PS[0:NF, 3, :]
                        dve.wait_ge(s["tr"], k * 2 + p + 3)
                        dve.tensor_copy(xt[p][:, 1].rearrange("h q s -> h s q"),
                                        PS[0:HP, 1, :].rearrange("h (s q) -> h s q", s=NPATCH))\
                           .then_inc(s["xt"], 1)
                        dve.wait_ge(s["squares"], k * 2 + p + 1)
                        dve.tensor_tensor(sq[p][:, 0], sq[p][:, 0], sq[p][:, 1], ALU.add).then_inc(s["sum"], 1)
                        dve.wait_ge(s["mag"], k * 2 + p + 1)
                        dve.tensor_tensor(den[p][:, :], den[p][:, :], feat[p][:, 0], ALU.add)
                        dve.drain()
                        dve.tensor_scalar(den[p][:, :], den[p][:, :], TINY, None, ALU.max)
                        dve.drain()
                        dve.reciprocal(den[p][:, :], den[p][:, :])
                        dve.drain()
                        dve.tensor_tensor(rat[p][:, :], im, den[p][:, :], ALU.mult).then_inc(s["ratio"], 1)
                        dve.tensor_scalar(sq[p][:, 1], im, 0.0, -0.5, ALU.is_ge, ALU.add)
                        dve.drain()
                        dve.wait_ge(s["atan"], k * 2 + p + 1)
                        dve.scalar_tensor_tensor(sq[p][:, 0], at[p][:, :], -2.0 / np.pi, sq[p][:, 1],
                                                 ALU.mult, ALU.add)
                        dve.drain()
                        dve.scalar_tensor_tensor(sq[p][:, 1], re, 0.0, sq[p][:, 0], ALU.is_lt, ALU.mult)
                        dve.drain()
                        dve.scalar_tensor_tensor(feat[p][:, 1], sq[p][:, 1], float(np.pi), at[p][:, :],
                                                 ALU.mult, ALU.add).then_inc(s["feat"], 1)
                    for p in range(2):
                        dve.wait_ge(s["out_ps"], k * 2 + p + 1)
                        i0 = (k * 2 + p) * 4
                        dve.tensor_tensor(t.H[:, bass.ds(i0, 4), :],
                                          PS[:, 6 + p, :].rearrange("p (q c) -> p q c", q=4),
                                          t.b2[:, :].unsqueeze(1).broadcast_to([P, 4, D]), ALU.add)\
                           .then_inc(s["stored"], 1)
                        dve.drain()
                        for q in range(4):
                            dve.bn_stats(t.BN[:, i0 + q, :], t.H[:, i0 + q, :])


def second_norm(nc, t):
    with nc.Block() as block:

        @block.vector
        def _(dve):
            with dve.Fori(0, NT // 2) as k:
                for p in range(2):
                    i = k * 2 + p
                    dve.tensor_scalar(t.U[:, i, :], t.H[:, i, :], t.MEAN[:, bass.ds(i, 1)],
                                      t.RSTD[:, bass.ds(i, 1)], ALU.subtract, ALU.mult)
                dve.drain()
                for p in range(2):
                    dve.bn_stats(t.BN[:, k * 2 + p, :], t.U[:, k * 2 + p, :])


def load_all(block, pairs, sem):
    @block.sync
    def _(sp):
        for dst, src in pairs:
            sp.dma_start(dst[tuple(slice(None) for _ in dst.shape)], src).then_inc(sem, 16)
        sp.wait_ge(sem, 16 * len(pairs))


def attention_weights(nc, ctx, a, name):
    w = NS()

    def sb(n, shape):
        return ctx.enter_context(nc.sbuf_tensor(f"{name}_{n}", shape, F32))

    w.wq, w.wk, w.wvo = sb("wq", [P, 2, P]), sb("wk", [P, 2, P]), sb("wvo", [P, 2, D])
    w.bqk, w.bvo = sb("bqk", [P, 2, 2]), sb("bvo", [P, 2, D])
    w.loads = [(w.wq, a[name + "_wq"]), (w.wk, a[name + "_wk"]), (w.wvo, a[name + "_wvo"]),
               (w.bqk, a[name + "_bqk"]), (w.bvo, a[name + "_bvo"])]
    return w


def attention_prelude(nc, t, s, w, nm, values, loads):
    with nc.Block() as block:
        load_all(block, loads, s["weights"])

        @block.vector
        def _(dve):
            for p in range(2):
                if nm is not None:
                    dve.memset(nm[p][tuple(slice(None) for _ in nm[p].shape)], 0.0)
                dve.memset(values[p][:, :, :, HD:HV], 1.0)


ATTENTION_SEMS = ("weights u tr ut q_ps q k_ps k v_ps v st_ps mx nt_ps q2 stt_ps exp av_ps norm ot_ps ot "
                  "out_ps stored")


def windowed_attention(nc, t, a, ctx):
    ln_scales(nc, t, "ln_a")
    with ExitStack() as sub:
        def sb(name, shape, dt=F32):
            return sub.enter_context(nc.sbuf_tensor(f"win_{name}", shape, dt))

        t.U = sb("u", [P, NT, D])
        second_norm(nc, t)
        ln_scales(nc, t, "ln_b")
        SEG = nc.dram_tensor("window_out", [NB * NW * WIN, D], F32).ap()
        with ExitStack() as loop:
            def lb(name, shape, dt=F32):
                return loop.enter_context(nc.sbuf_tensor(f"win_{name}", shape, dt))

            s = Sems(nc, loop, "win", ATTENTION_SEMS + " mask sent0 sent1")
            w = attention_weights(nc, loop, a, "win")
            gb, maskf = lb("gb", [P, 2]), lb("maskf", [WT, WT])
            mask, four = lb("mask", [WT, WT], BF16), lb("four", [WT, 4, WT], BF16)
            two = range(2)
            us = [lb(f"us{i}", [P, 2, D]) for i in two]
            ut = [lb(f"ut{i}", [P, L]) for i in two]
            qt, kt = [lb(f"qt{i}", [P, 2, L]) for i in two], [lb(f"kt{i}", [P, 2, L]) for i in two]
            q2 = [lb(f"q2{i}", [P, 2, 4, WT]) for i in two]
            v = [lb(f"v{i}", [WT, 4, NH, HV]) for i in two]
            nm = [lb(f"nm{i}", [WT, 4, 2, 4, 32]) for i in two]
            pt = [lb(f"pt{i}", [WT, NH, 4, WT]) for i in two]
            rc = [lb(f"rc{i}", [WT, 4, NH]) for i in two]
            oc = [lb(f"oc{i}", [WT, 4, NH, HD]) for i in two]
            ot = [lb(f"ot{i}", [P, 4, WT]) for i in two]
            sg = [lb(f"sg{i}", [WT, 4, D]) for i in two]
            attention_prelude(nc, t, s, w, nm, v, w.loads + [(gb, a["win_gb"]), (maskf, a["c_mask"])])
            PS = t.PS
            X = [4, 6]

            with nc.Block() as block:

                @block.tensor
                def _(pe):
                    pe.wait_ge(s["mask"], 1)
                    with pe.Fori(0, NB // 2) as k:

                        def project(p):
                            c = k * 2 + p + 1
                            pe.wait_ge(s["u"], c)
                            for h in range(2):
                                mm = pe.transpose(PS[:, X[p], h * P:(h + 1) * P], us[p][:, h, :], t.ident[:, :])
                            mm.then_inc(s["tr"], 1)
                            pe.wait_ge(s["ut"], c)
                            for g in range(2):
                                mm = pe.matmul(PS[:, X[p] + 1, g * L:(g + 1) * L], w.wq[:, g, :], ut[p][:, :],
                                               start=True, stop=True)
                            mm.then_inc(s["q_ps"], 1)
                            for g in range(2):
                                mm = pe.matmul(PS[:, X[p], g * L:(g + 1) * L], w.wk[:, g, :], ut[p][:, :],
                                               start=True, stop=True)
                            mm.then_inc(s["k_ps"], 1)
                            pe.wait_ge(s["q"], c)
                            for j in range(4):
                                o = window_offset(j)
                                mm = pe.matmul(PS[0:WT, X[p] + 1, j * D:(j + 1) * D], ut[p][:, o:o + WT],
                                               w.wvo[:, 0, :], start=True, stop=True)
                            mm.then_inc(s["v_ps"], 1)

                        def scores(p, n, moving, ready):
                            for h in range(2):
                                g, r = n // 2, 32 * (2 * n % 4 + h)
                                bank = 2 * (n % 2) + h
                                pe.matmul(PS[0:WT, bank, 0:4 * WT], mask[:, :],
                                          four[:, :, :].rearrange("p a b -> p (a b)"), start=True, stop=False)
                                for j in range(4):
                                    o = window_offset(j)
                                    stat, mov = moving(g, r, j, o)
                                    mm = pe.matmul(PS[0:WT, bank, j * WT:(j + 1) * WT], stat, mov,
                                                   start=False, stop=(j == 3))
                            mm.then_inc(ready, 1)

                        def row_scores(p, n):
                            if n < 2:
                                if p == 0:
                                    pe.wait_ge(s["exp"], k * 8 + 7 + n)
                                else:
                                    pe.wait_ge(s["mx"], k * 8 + 3 + n)
                            else:
                                pe.wait_ge(s["mx"], k * 8 + p * 4 + n - 1)
                            scores(p, n, lambda g, r, j, o: (qt[p][r:r + 32, g, o:o + WT],
                                                             kt[p][r:r + 32, g, o:o + WT]), s["st_ps"])

                        def column_scores(p, n):
                            if p == 0 and n < 2:
                                pe.wait_ge(s["mx"], k * 8 + 7 + n)
                            else:
                                pe.wait_ge(s["exp"], 8 + k * 8 + p * 4 + n - 1)
                            scores(p, n, lambda g, r, j, o: (kt[p][r:r + 32, g, o:o + WT],
                                                             q2[p][r:r + 32, g, j, :]), s["stt_ps"])

                        def transpose_maxima(p):
                            pe.wait_ge(s["mx"], k * 8 + p * 4 + 4)
                            for g in range(2):
                                for j in range(4):
                                    mm = pe.transpose(PS[:, X[p] + g, j * WT:(j + 1) * WT],
                                                      nm[p][:, j, g].rearrange("q i r -> q (i r)"),
                                                      t.ident[0:WT, 0:WT])
                            mm.then_inc(s["nt_ps"], 1)

                        for p in range(2):
                            project(p)
                        pe.wait_ge(s["k"], k * 2 + 1)
                        for n in range(4):
                            row_scores(0, n)
                        pe.wait_ge(s["k"], k * 2 + 2)
                        pe.wait_ge(s["v"], k * 2 + 2)
                        for n in range(2):
                            row_scores(1, n)
                        transpose_maxima(0)
                        for n in range(2, 4):
                            row_scores(1, n)
                        pe.wait_ge(s["q2"], k * 2 + 1)
                        for n in range(2):
                            column_scores(0, n)
                        transpose_maxima(1)
                        for n in range(2, 4):
                            column_scores(0, n)
                        pe.wait_ge(s["q2"], k * 2 + 2)
                        for n in range(4):
                            column_scores(1, n)
                        for p in range(2):
                            pe.wait_ge(s["exp"], 8 + k * 8 + p * 4 + 4)
                            for j in range(4):
                                for h in range(NH):
                                    o = (j % 2) * NH * HV + h * HV
                                    mm = pe.matmul(PS[0:WT, X[p] + j // 2, o:o + HV], pt[p][:, h, j, :],
                                                   v[p][:, j, h, :], start=True, stop=True)
                            mm.then_inc(s["av_ps"], 1)
                        for p in range(2):
                            pe.wait_ge(s["norm"], k * 2 + p + 1)
                            for j in range(4):
                                mm = pe.transpose(PS[:, X[p], j * WT:(j + 1) * WT],
                                                  oc[p][:, j].rearrange("q h d -> q (h d)"), t.ident[0:WT, 0:WT])
                            mm.then_inc(s["ot_ps"], 1)
                        for p in range(2):
                            pe.wait_ge(s["ot"], k * 2 + p + 1)
                            for j in range(4):
                                o = window_offset(j)
                                pe.matmul(PS[0:WT, X[p] + 1, j * D:(j + 1) * D], ot[p][:, j, :], w.wvo[:, 1, :],
                                          start=True, stop=False)
                                mm = pe.matmul(PS[0:WT, X[p] + 1, j * D:(j + 1) * D], ut[p][:, o:o + WT],
                                               t.ident[:, :], start=False, stop=True)
                            mm.then_inc(s["out_ps"], 1)

                @block.scalar
                def _(act):
                    act.nop().then_inc(s["exp"], 8)
                    with act.Fori(0, NB // 2) as k:
                        for p in range(2):
                            c = k * 2 + p + 1
                            act.wait_ge(s["tr"], c)
                            act.activation(ut[p][:, :], PS[:, X[p], 0:L], ACT.Identity, scale=gb[:, 0:1],
                                           bias=gb[:, 1:2]).then_inc(s["ut"], 1)
                            act.wait_ge(s["q_ps"], c)
                            for g in range(2):
                                i = act.activation(qt[p][:, g, :], PS[:, X[p] + 1, g * L:(g + 1) * L],
                                                   ACT.Identity, bias=w.bqk[:, 0, g:g + 1])
                            i.then_inc(s["q"], 1)
                            act.wait_ge(s["k_ps"], c)
                            for g in range(2):
                                i = act.activation(kt[p][:, g, :], PS[:, X[p], g * L:(g + 1) * L],
                                                   ACT.Identity, bias=w.bqk[:, 1, g:g + 1])
                            i.then_inc(s["k"], 1)
                        for p in range(2):
                            for n in range(4):
                                act.wait_ge(s["stt_ps"], k * 8 + p * 4 + n + 1)
                                b = 2 * (n % 2)
                                act.activation(pt[p][:, 2 * n:2 * n + 2].rearrange("q h j c -> q h (j c)"),
                                               PS[0:WT, b:b + 2, 0:4 * WT], ACT.Exp, scale=HD ** -0.5)\
                                   .then_inc(s["exp"], 1)
                        for p in range(2):
                            act.wait_ge(s["ot_ps"], k * 2 + p + 1)
                            act.activation(ot[p][:, :, :].rearrange("p j c -> p (j c)"),
                                           PS[:, X[p], 0:4 * WT], ACT.Copy).then_inc(s["ot"], 1)

                @block.vector
                def _(dve):
                    dve.tensor_copy(mask[:, :], maskf[:, :])
                    for j in range(4):
                        i = dve.tensor_copy(four[:, j, :], t.ident[0:WT, 0:WT])
                    i.then_inc(s["mask"], 1)
                    dve.nop().then_inc(s["stored"], 2)
                    with dve.Fori(0, NB // 2) as k:
                        for p in range(2):
                            for h in range(2):
                                i = k * 4 + p * 2 + h
                                u = dve.tensor_scalar(us[p][:, h, :], t.U[:, i, :], t.MEAN[:, bass.ds(i, 1)],
                                                      t.RSTD[:, bass.ds(i, 1)], ALU.subtract, ALU.mult)
                            u.then_inc(s["u"], 1)
                        for p in range(2):
                            dve.wait_ge(s["v_ps"], k * 2 + p + 1)
                            bv = w.bvo[0:WT, 0, :].rearrange("q (h d) -> q h d", h=NH)
                            for j in range(4):
                                i = dve.tensor_tensor(v[p][:, j, :, 0:HD],
                                                      PS[0:WT, X[p] + 1, j * D:(j + 1) * D].rearrange(
                                                          "q (h d) -> q h d", h=NH), bv, ALU.add)
                            i.then_inc(s["v"], 1)

                        def maxima(p, n):
                            dve.wait_ge(s["st_ps"], k * 8 + p * 4 + n + 1)
                            b, g, i0 = 2 * (n % 2), n // 2, 2 * n % 4
                            dve.tensor_reduce(nm[p][:, :, g, i0:i0 + 2, HD].rearrange("q j i -> q i j"),
                                              PS[0:WT, b:b + 2, 0:4 * WT].rearrange("q i (j c) -> q i j c", j=4),
                                              AX.X, ALU.max, negate=True).then_inc(s["mx"], 1)

                        def shifted_queries(p):
                            dve.wait_ge(s["nt_ps"], k * 2 + p + 1)
                            for g in range(2):
                                for odd in range(2):
                                    i = dve.tensor_tensor(
                                        q2[p][:, g, 2 * odd:2 * odd + 2, :],
                                        PS[:, X[p] + g, 2 * odd * WT:(2 * odd + 2) * WT].rearrange(
                                            "p (j c) -> p j c", j=2),
                                        qt[p][:, g, HOP * odd:HOP * odd + 2 * WT].rearrange(
                                            "p (j c) -> p j c", j=2), ALU.add)
                            i.then_inc(s["q2"], 1)

                        for n in range(4):
                            maxima(0, n)
                        for n in range(2):
                            maxima(1, n)
                        shifted_queries(0)
                        for n in range(2, 4):
                            maxima(1, n)
                        shifted_queries(1)
                        for p in range(2):
                            dve.wait_ge(s["av_ps"], k * 2 + p + 1)
                            for y in range(2):
                                av = PS[0:WT, X[p] + y, 0:2 * NH * HV].rearrange("q (j h e) -> q j h e", j=2, h=NH)
                                dve.reciprocal(rc[p][:, 2 * y:2 * y + 2, :], av[:, :, :, HD])
                            dve.drain()
                            for j in range(4):
                                o = (j % 2) * NH * HV
                                av = PS[0:WT, X[p] + j // 2, o:o + NH * HV].rearrange("q (h e) -> q h e", h=NH)
                                i = dve.tensor_tensor(oc[p][:, j], av[:, :, 0:HD],
                                                      rc[p][:, j, :].unsqueeze(2).broadcast_to([WT, NH, HD]),
                                                      ALU.mult)
                            i.then_inc(s["norm"], 1)
                        for p in range(2):
                            dve.wait_ge(s["out_ps"], k * 2 + p + 1)
                            dve.wait_ge(s[f"sent{p}"], k * 64 + 64)
                            dve.tensor_tensor(sg[p][:, :, :], PS[0:WT, X[p] + 1, :].rearrange(
                                "q (j c) -> q j c", j=4),
                                w.bvo[0:WT, 1, :].unsqueeze(1).broadcast_to([WT, 4, D]), ALU.add)\
                               .then_inc(s["stored"], 1)

                @block.sync
                def _(sp):
                    for p in range(2):
                        sp.nop().then_inc(s[f"sent{p}"], 64)
                    with sp.Fori(0, NB // 2) as k:
                        for p in range(2):
                            sp.wait_ge(s["stored"], k * 2 + p + 3)
                            for j in range(4):
                                base = (k * 2 + p) * NW * WIN + (j % 2) * 2 * WT
                                rows = SEG[bass.ds(base, 2 * WT), :].rearrange(
                                    "(i o w) c -> o i w c", o=2, w=WIN)[j // 2]
                                sp.dma_start(rows, sg[p][:, j, :]).then_inc(s[f"sent{p}"], 16)
                    for p in range(2):
                        sp.wait_ge(s[f"sent{p}"], 64 + 64 * NB // 2)

        merge_windows(nc, t, a, sub, SEG)


def merge_windows(nc, t, a, ctx, SEG):
    first = ctx.enter_context(nc.sbuf_tensor("win_first", [P, NB, 2, D], F32))
    second = ctx.enter_context(nc.sbuf_tensor("win_second", [P, NB, 2, D], F32))
    share = ctx.enter_context(nc.sbuf_tensor("win_share", [P, 2], F32))
    s = Sems(nc, ctx, "merge", "cleared loaded")
    seg = SEG.rearrange("(s b w) c -> s w b c", b=NB, w=WIN)
    H4 = t.H[:, :, :].rearrange("p (b h) c -> p b h c", h=2)
    U4 = t.U[:, :, :].rearrange("p (b h) c -> p b h c", h=2)
    pieces = [(first, 0, 0, 0, 12, 0, 10), (first, 0, 120, 12, 13, 0, 8),
              (first, 1, 0, 12, 13, 8, 10), (first, 1, 2, 13, 24, 0, 10),
              (second, 0, 10, 0, 11, 10, 20), (second, 0, 120, 11, 12, 10, 18),
              (second, 1, 0, 11, 12, 18, 20), (second, 1, 2, 12, 24, 10, 20)]
    with nc.Block() as block:

        @block.gpsimd
        def _(pool):
            pool.memset(first[:, :, :, :], 0.0).then_inc(s["cleared"], 1)
            pool.memset(second[:, :, :, :], 0.0).then_inc(s["cleared"], 1)

        @block.sync
        def _(sp):
            sp.dma_start(share[:, :], a["c_share"]).then_inc(s["loaded"], 16)
            sp.wait_ge(s["cleared"], 2)
            n = 16
            for buf, h, p0, s0, s1, w0, w1 in pieces:
                rows = (s1 - s0) * (w1 - w0)
                for q in range(s0, s1):
                    r = p0 + (q - s0) * (w1 - w0)
                    sp.dma_start(buf[r:r + w1 - w0, :, h, :], seg[q, w0:w1]).then_inc(s["loaded"], 16)
                    n += 16
            sp.wait_ge(s["loaded"], n)

        @block.vector
        def _(dve):
            dve.tensor_tensor(t.H[:, :, :], t.H[:, :, :], t.U[:, :, :], ALU.add)
            dve.wait_ge(s["loaded"], 16 + 16 * sum(q[4] - q[3] for q in pieces))
            dve.tensor_tensor(first[:, :, :, :], first[:, :, :, :], second[:, :, :, :], ALU.add)
            dve.drain()
            for h in range(2):
                dve.scalar_tensor_tensor(H4[:, :, h, :], first[:, :, h, :], share[:, h:h + 1], H4[:, :, h, :],
                                         ALU.mult, ALU.add)
            dve.drain()
            with dve.Fori(0, NT) as i:
                dve.bn_stats(t.BN[:, i, :], t.H[:, i, :])


EXPERT_SEMS = ("weights w1 w2 b2 staged tr tt logits exp1 exp2 counts_in counts made "
               "xs0 xs1 picked xtr xt hid_ps pre hid out_ps res sent0 sent1")


def full_attention(nc, t, a, name):
    keep = name == "l0mha"
    ln_scales(nc, t, f"{name}_ln")
    with ExitStack() as ctx:
        def sb(n, shape, dt=F32):
            return ctx.enter_context(nc.sbuf_tensor(f"{name}_{n}", shape, dt))

        s = t.mha_sems
        if not keep:
            s.restart(nc)
        w = attention_weights(nc, ctx, a, name)
        two = range(2)
        us, ut = [sb(f"us{i}", [P, 2, D]) for i in two], [sb(f"ut{i}", [P, L]) for i in two]
        qt, kt = [sb(f"qt{i}", [P, 2, L]) for i in two], [sb(f"kt{i}", [P, 2, L]) for i in two]
        q2 = [sb(f"q2{i}", [P, 2, L]) for i in two]
        v = [sb(f"v{i}", [P, 2, NH, HV]) for i in two]
        nm = [sb(f"nm{i}", [P, 2, 2, 4, 32]) for i in two]
        pt = [sb(f"pt{i}", [P, NH, 2, L]) for i in two]
        rc = [sb(f"rc{i}", [P, 2, NH]) for i in two]
        oc = [sb(f"oc{i}", [P, 2, NH, HD]) for i in two]
        ot = [sb(f"ot{i}", [P, L]) for i in two]
        attention_prelude(nc, t, s, w, nm, v, w.loads)
        PS = t.PS
        X = [4, 6]

        with nc.Block() as block:

            @block.tensor
            def _(pe):
                with pe.Fori(0, NB // 2) as k:

                    def project(p):
                        c = k * 2 + p + 1
                        pe.wait_ge(s["u"], c)
                        for h in range(2):
                            mm = pe.transpose(PS[:, X[p], h * P:(h + 1) * P], us[p][:, h, :], t.ident[:, :])
                        mm.then_inc(s["tr"], 1)
                        pe.wait_ge(s["ut"], c)
                        for g in range(2):
                            mm = pe.matmul(PS[:, X[p] + 1, g * L:(g + 1) * L], w.wq[:, g, :], ut[p][:, :],
                                           start=True, stop=True)
                        mm.then_inc(s["q_ps"], 1)
                        for g in range(2):
                            mm = pe.matmul(PS[:, X[p], g * L:(g + 1) * L], w.wk[:, g, :], ut[p][:, :],
                                           start=True, stop=True)
                        mm.then_inc(s["k_ps"], 1)
                        pe.wait_ge(s["q"], c)
                        for h in range(2):
                            mm = pe.matmul(PS[:, X[p] + 1, h * D:(h + 1) * D], ut[p][:, h * P:(h + 1) * P],
                                           w.wvo[:, 0, :], start=True, stop=True)
                        mm.then_inc(s["v_ps"], 1)

                    def scores(n, stationary, moving, ready):
                        for tile in range(2):
                            for h in range(2):
                                g, r = n // 2, 32 * (2 * n % 4 + h)
                                mm = pe.matmul(PS[:, 2 * (n % 2) + h, tile * L:(tile + 1) * L],
                                               stationary[r:r + 32, g, tile * P:(tile + 1) * P],
                                               moving[r:r + 32, g, :], start=True, stop=True)
                        mm.then_inc(ready, 1)

                    def row_scores(p, n):
                        if p == 0 and n < 2:
                            pe.wait_ge(s["exp"], k * 8 + 7 + n)
                        else:
                            pe.wait_ge(s["mx"], k * 8 + p * 4 + n - 1)
                        scores(n, qt[p], kt[p], s["st_ps"])

                    def column_scores(p, n):
                        if p == 0 and n < 2:
                            pe.wait_ge(s["mx"], k * 8 + 7 + n)
                        else:
                            pe.wait_ge(s["exp"], 8 + k * 8 + p * 4 + n - 1)
                        scores(n, kt[p], q2[p], s["stt_ps"])

                    def transpose_maxima(p):
                        pe.wait_ge(s["mx"], k * 8 + p * 4 + 4)
                        for g in range(2):
                            for h in range(2):
                                o = g * L + h * P
                                mm = pe.transpose(PS[:, X[p], o:o + P],
                                                  nm[p][:, h, g].rearrange("q i r -> q (i r)"), t.ident[:, :])
                        mm.then_inc(s["nt_ps"], 1)

                    for p in range(2):
                        project(p)
                    pe.wait_ge(s["k"], k * 2 + 1)
                    for n in range(4):
                        row_scores(0, n)
                    pe.wait_ge(s["k"], k * 2 + 2)
                    for n in range(2):
                        row_scores(1, n)
                    transpose_maxima(0)
                    for n in range(2, 4):
                        row_scores(1, n)
                    pe.wait_ge(s["q2"], k * 2 + 1)
                    for n in range(2):
                        column_scores(0, n)
                    transpose_maxima(1)
                    for n in range(2, 4):
                        column_scores(0, n)
                    pe.wait_ge(s["q2"], k * 2 + 2)
                    for n in range(4):
                        column_scores(1, n)
                    for p in range(2):
                        pe.wait_ge(s["exp"], 8 + k * 8 + p * 4 + 4)
                        pe.wait_ge(s["v"], k * 2 + p + 1)
                        for q in range(2):
                            for h in range(NH):
                                o = q * NH * HV + h * HV
                                for tile in range(2):
                                    mm = pe.matmul(PS[:, X[p] + 1, o:o + HV],
                                                   pt[p][:, h, tile, q * P:(q + 1) * P], v[p][:, tile, h, :],
                                                   start=(tile == 0), stop=(tile == 1))
                        mm.then_inc(s["av_ps"], 1)
                    for p in range(2):
                        pe.wait_ge(s["norm"], k * 2 + p + 1)
                        for q in range(2):
                            mm = pe.transpose(PS[:, X[p], q * P:(q + 1) * P],
                                              oc[p][:, q].rearrange("q h d -> q (h d)"), t.ident[:, :])
                        mm.then_inc(s["ot_ps"], 1)
                    for p in range(2):
                        pe.wait_ge(s["ot"], k * 2 + p + 1)
                        for q in range(2):
                            mm = pe.matmul(PS[:, X[p] + 1, q * D:(q + 1) * D], ot[p][:, q * P:(q + 1) * P],
                                           w.wvo[:, 1, :], start=True, stop=True)
                        mm.then_inc(s["out_ps"], 1)

            @block.scalar
            def _(act):
                act.nop().then_inc(s["exp"], 8)
                with act.Fori(0, NB // 2) as k:
                    for p in range(2):
                        c = k * 2 + p + 1
                        act.wait_ge(s["tr"], c)
                        act.activation(ut[p][:, :], PS[:, X[p], 0:L], ACT.Copy).then_inc(s["ut"], 1)
                        act.wait_ge(s["q_ps"], c)
                        for g in range(2):
                            i = act.activation(qt[p][:, g, :], PS[:, X[p] + 1, g * L:(g + 1) * L],
                                               ACT.Identity, bias=w.bqk[:, 0, g:g + 1])
                        i.then_inc(s["q"], 1)
                        act.wait_ge(s["k_ps"], c)
                        for g in range(2):
                            i = act.activation(kt[p][:, g, :], PS[:, X[p], g * L:(g + 1) * L],
                                               ACT.Identity, bias=w.bqk[:, 1, g:g + 1])
                        i.then_inc(s["k"], 1)
                    for p in range(2):
                        for n in range(4):
                            act.wait_ge(s["stt_ps"], k * 8 + p * 4 + n + 1)
                            b = 2 * (n % 2)
                            act.activation(pt[p][:, 2 * n:2 * n + 2].rearrange("q h j c -> q h (j c)"),
                                           PS[:, b:b + 2, :], ACT.Exp, scale=HD ** -0.5).then_inc(s["exp"], 1)
                    for p in range(2):
                        act.wait_ge(s["ot_ps"], k * 2 + p + 1)
                        act.activation(ot[p][:, :], PS[:, X[p], 0:L], ACT.Copy).then_inc(s["ot"], 1)

            @block.vector
            def _(dve):
                with dve.Fori(0, NB // 2) as k:
                    for p in range(2):
                        for h in range(2):
                            i = k * 4 + p * 2 + h
                            u = dve.tensor_scalar(us[p][:, h, :], t.H[:, i, :], t.MEAN[:, bass.ds(i, 1)],
                                                  t.RSTD[:, bass.ds(i, 1)], ALU.subtract, ALU.mult)
                        u.then_inc(s["u"], 1)
                    for p in range(2):
                        dve.wait_ge(s["v_ps"], k * 2 + p + 1)
                        for h in range(2):
                            i = dve.tensor_tensor(
                                v[p][:, h, :, 0:HD],
                                PS[:, X[p] + 1, h * D:(h + 1) * D].rearrange("q (h d) -> q h d", h=NH),
                                w.bvo[:, 0, :].rearrange("q (h d) -> q h d", h=NH), ALU.add)
                        i.then_inc(s["v"], 1)

                    def maxima(p, n):
                        dve.wait_ge(s["st_ps"], k * 8 + p * 4 + n + 1)
                        b, g, i0 = 2 * (n % 2), n // 2, 2 * n % 4
                        dve.tensor_reduce(nm[p][:, :, g, i0:i0 + 2, HD].rearrange("q j i -> q i j"),
                                          PS[:, b:b + 2, :].rearrange("q i (j c) -> q i j c", j=2),
                                          AX.X, ALU.max, negate=True).then_inc(s["mx"], 1)

                    def shifted_queries(p):
                        dve.wait_ge(s["nt_ps"], k * 2 + p + 1)
                        dve.tensor_tensor(q2[p][:, :, :], PS[:, X[p], :].rearrange("p (g c) -> p g c", g=2),
                                          qt[p][:, :, :], ALU.add).then_inc(s["q2"], 1)

                    for n in range(4):
                        maxima(0, n)
                    for n in range(2):
                        maxima(1, n)
                    shifted_queries(0)
                    for n in range(2, 4):
                        maxima(1, n)
                    shifted_queries(1)
                    for p in range(2):
                        dve.wait_ge(s["av_ps"], k * 2 + p + 1)
                        av = PS[:, X[p] + 1, 0:2 * NH * HV].rearrange("q (j h e) -> q j h e", j=2, h=NH)
                        dve.reciprocal(rc[p][:, :, :], av[:, :, :, HD])
                        dve.drain()
                        for q in range(2):
                            i = dve.tensor_tensor(oc[p][:, q], av[:, q, :, 0:HD],
                                                  rc[p][:, q, :].unsqueeze(2).broadcast_to([P, NH, HD]), ALU.mult)
                        i.then_inc(s["norm"], 1)
                    for p in range(2):
                        dve.wait_ge(s["out_ps"], k * 2 + p + 1)
                        i0 = k * 4 + p * 2
                        out = PS[:, X[p] + 1, 0:2 * D].rearrange("q (j c) -> q j c", j=2)
                        bo = w.bvo[:, 1, :].unsqueeze(1).broadcast_to([P, 2, D])
                        if keep:
                            dve.tensor_tensor(us[p][:, :, :], us[p][:, :, :], bo, ALU.add)
                            dve.drain()
                            dve.tensor_tensor(t.R[:, bass.ds(i0, 2), :], out, us[p][:, :, :], ALU.add)
                            dve.drain()
                            for q in range(2):
                                dve.bn_stats(t.BN[:, i0 + q, :], t.R[:, i0 + q, :])
                        else:
                            dve.tensor_tensor(t.H[:, bass.ds(i0, 2), :], t.H[:, bass.ds(i0, 2), :], bo, ALU.add)
                            dve.drain()
                            dve.tensor_tensor(t.H[:, bass.ds(i0, 2), :], out, t.H[:, bass.ds(i0, 2), :], ALU.add)
                            dve.drain()
                            for q in range(2):
                                dve.bn_stats(t.BN[:, i0 + q, :], t.H[:, i0 + q, :])


def experts_layer(nc, t, a, name):
    first_layer = name == "l0moe"
    ntop = 1 if first_layer else 2
    tiles = TILES1 if first_layer else TILES2
    XS = t.XS1 if first_layer else t.XS2
    gelu = ACT.Gelu_apprx_tanh if first_layer else ACT.Gelu
    YS = nc.dram_tensor(f"{name}_out", [tiles * P, D], F32).ap()
    ln_scales(nc, t, f"{name}_ln")
    with ExitStack() as ctx:
        def sb(n, shape, dt=F32):
            return ctx.enter_context(nc.sbuf_tensor(f"{name}_{n}", shape, dt))

        s = t.moe_sems
        rows_moved = Sems(nc, ctx, name, "scattered gathered")
        if not first_layer:
            s.restart(nc)
        gb, gw, gbias = sb("gb", [P, 2, D]), sb("gate_w", [P, NE]), sb("gate_b", [P, NE])
        before, order, chain = sb("before", [P, P]), sb("order", [P, NE, NT]), sb("chain", [P, NE, NT])
        ones, trow = sb("ones", [P, P]), sb("trow", [1, NE, tiles])
        w1, w2, b2 = sb("w1", [P, NE, FF + KF]), sb("w2", [P, NE, KF, D]), sb("b2", [P, NE, D])
        pos = [sb(f"pos{i}", [P, NT], U32) for i in range(ntop)]
        gate = [sb(f"gate{i}", [P, NT]) for i in range(ntop)]
        te = sb("te", [1, tiles], I32)
        small = [(gb, a[name + "_gb"]), (gw, a[name + "_gate_w"]), (gbias, a[name + "_gate_b"]),
                 (before, a["c_before"]), (order, a["c_order"]), (chain, a["c_chain"])]
        PS = t.PS
        if not first_layer:
            t.U = sb("u", [P, NT, D])
            second_norm(nc, t)
            ln_scales(nc, t, f"{name}_ln2")
        src = t.R if first_layer else t.U

        with ExitStack() as sub:
            def tb(n, shape, dt=F32):
                return sub.enter_context(nc.sbuf_tensor(f"{name}_{n}", shape, dt))

            T = tb("t", [P, NT, D])
            stage, tt = [tb(f"st{i}", [P, D]) for i in range(2)], [tb(f"tt{i}", [P, P]) for i in range(2)]
            LG, E1, M = tb("lg", [P, NE, NT]), tb("e1", [P, NE, NT]), tb("m", [P, NE, NT])
            OH = [tb(f"oh{i}", [P, NE, NT]) for i in range(ntop)]
            CN, RK = tb("cn", [P, NE, NT]), tb("rk", [P, NE, NT])
            best, sm = tb("best", [P, NT]), tb("sm", [P, NT])
            nt_, en = tb("ntiles", [P, NE]), tb("ends", [P, NE])
            cmp_ = tb("cmp", [1, NE, tiles])

            with nc.Block() as block:
                load_all(block, small, s["weights"])

                @block.scalar
                def _(act):
                    act.dma_start(w1[:, :, :], a[name + "_w1"]).then_inc(s["w1"], 16)
                    act.dma_start(w2[:, :, :, :], a[name + "_w2"]).then_inc(s["w2"], 16)
                    act.dma_start(b2[:, :, :], a[name + "_b2"]).then_inc(s["b2"], 16)
                    with act.Fori(0, NT // 2) as k:
                        for p in range(2):
                            act.wait_ge(s["tr"], k * 2 + p + 1)
                            act.activation(tt[p][:, :], PS[:, p, 0:P], ACT.Copy).then_inc(s["tt"], 1)
                    act.wait_ge(s["exp1"], 1)
                    act.activation(E1[:, :, :], LG[:, :, :], ACT.Exp).then_inc(s["exp2"], 1)

                @block.gpsimd
                def _(pool):
                    pool.memset(ones[:, :], 1.0).then_inc(s["made"], 1)
                    pool.iota(trow[:, :, :], [[0, NE], [1, tiles]], base=0, channel_multiplier=0,
                              allow_small_or_imprecise_dtypes=True).then_inc(s["made"], 1)

                @block.tensor
                def _(pe):
                    pe.wait_ge(s["weights"], 16 * len(small))
                    with pe.Fori(0, NT // 2) as k:
                        for p in range(2):
                            pe.wait_ge(s["staged"], k * 2 + p + 1)
                            pe.transpose(PS[:, p, 0:P], stage[p][:, :], t.ident[:, :]).then_inc(s["tr"], 1)
                        for p in range(2):
                            pe.wait_ge(s["tt"], k * 2 + p + 1)
                            pe.matmul(PS[:, 2 + p, 0:NE], tt[p][:, :], gw[:, :], start=True, stop=True)\
                              .then_inc(s["logits"], 1)
                    pe.wait_ge(s["made"], 2)
                    pe.wait_ge(s["counts_in"], 1)
                    oh = CN[:, :, :].rearrange("p e i -> p (e i)")
                    pe.matmul(PS[:, 4, 0:NE * NT], ones[:, :], oh, start=True, stop=True)
                    pe.matmul(PS[:, 5, 0:NE * NT], before[:, :], oh, start=True, stop=True)\
                      .then_inc(s["counts"], 1)

                @block.vector
                def _(dve):
                    dve.wait_ge(s["weights"], 16 * len(small))
                    with dve.Fori(0, NT // 2) as k:
                        for p in range(2):
                            i = k * 2 + p
                            dve.tensor_scalar(T[:, i, :], src[:, i, :], t.MEAN[:, bass.ds(i, 1)],
                                              t.RSTD[:, bass.ds(i, 1)], ALU.subtract, ALU.mult)
                        dve.drain()
                        i0 = k * 2
                        dve.tensor_tensor(T[:, bass.ds(i0, 2), :], T[:, bass.ds(i0, 2), :],
                                          gb[:, 0, :].unsqueeze(1).broadcast_to([P, 2, D]), ALU.mult)
                        dve.drain()
                        dve.tensor_tensor(T[:, bass.ds(i0, 2), :], T[:, bass.ds(i0, 2), :],
                                          gb[:, 1, :].unsqueeze(1).broadcast_to([P, 2, D]), ALU.add)
                        dve.drain()
                        for p in range(2):
                            dve.tensor_copy(stage[p][:, :], T[:, k * 2 + p, :]).then_inc(s["staged"], 1)
                        for p in range(2):
                            dve.wait_ge(s["logits"], k * 2 + p + 1)
                            dve.tensor_tensor(LG[:, :, bass.ds(k * 2 + p, 1)].rearrange("p e i -> p (e i)"),
                                              PS[:, 2 + p, 0:NE], gbias[:, :], ALU.add)
                    dve.drain()

                    def over_experts(x):
                        return x.rearrange("p e i -> p i e")

                    def on_experts(x):
                        return x.unsqueeze(1).broadcast_to([P, NE, NT])

                    dve.tensor_reduce(best[:, :], over_experts(LG[:, :, :]), AX.X, ALU.max)
                    dve.drain()
                    dve.tensor_tensor(LG[:, :, :], LG[:, :, :], on_experts(best[:, :]), ALU.subtract)
                    dve.drain()

                    def first_at_least(onehot, floor):
                        dve.tensor_tensor(M[:, :, :], LG[:, :, :], floor, ALU.is_ge)
                        dve.drain()
                        dve.tensor_tensor(M[:, :, :], M[:, :, :], order[:, :, :], ALU.mult)
                        dve.drain()
                        dve.tensor_reduce(sm[:, :], over_experts(M[:, :, :]), AX.X, ALU.max)
                        dve.drain()
                        dve.tensor_tensor(onehot[:, :, :], order[:, :, :], on_experts(sm[:, :]), ALU.is_equal)
                        dve.drain()

                    dve.memset(best[:, :], 0.0)
                    dve.drain()
                    first_at_least(OH[0], on_experts(best[:, :]))
                    if first_layer:
                        dve.nop().then_inc(s["exp1"], 1)
                        dve.wait_ge(s["exp2"], 1)
                        dve.tensor_reduce(sm[:, :], over_experts(E1[:, :, :]), AX.X, ALU.add)
                        dve.drain()
                        dve.reciprocal(gate[0][:, :], sm[:, :])
                        dve.tensor_copy(CN[:, :, :], OH[0][:, :, :]).then_inc(s["counts_in"], 1)
                    else:
                        dve.scalar_tensor_tensor(LG[:, :, :], OH[0][:, :, :], NEG, LG[:, :, :], ALU.mult, ALU.add)
                        dve.drain()
                        dve.tensor_reduce(best[:, :], over_experts(LG[:, :, :]), AX.X, ALU.max)
                        dve.drain()
                        first_at_least(OH[1], on_experts(best[:, :]))
                        dve.tensor_tensor(CN[:, :, :], OH[0][:, :, :], OH[1][:, :, :], ALU.add)\
                           .then_inc(s["counts_in"], 1)
                        dve.tensor_tensor(LG[:, :, :], LG[:, :, :], OH[1][:, :, :], ALU.mult)
                        dve.drain()
                        dve.tensor_copy(LG[:, 0, :], best[:, :]).then_inc(s["exp1"], 1)
                        dve.wait_ge(s["exp2"], 1)
                        dve.tensor_scalar(sm[:, :], E1[:, 0, :], 1.0, None, ALU.add)
                        dve.drain()
                        dve.reciprocal(gate[0][:, :], sm[:, :])
                        dve.drain()
                        dve.tensor_tensor(gate[1][:, :], gate[0][:, :], E1[:, 0, :], ALU.mult)
                    dve.wait_ge(s["counts"], 1)
                    flat = "p e i -> p (e i)"
                    dve.tensor_tensor_scan(RK[:, :, :].rearrange(flat), chain[:, :, :].rearrange(flat),
                                           PS[:, 4, 0:NE * NT], 0.0, ALU.mult, ALU.add)
                    dve.drain()
                    dve.wait_ge(s["made"], 2)
                    dve.tensor_scalar(nt_[:, :], RK[:, :, NT - 1], 127.0, 1.0 / P, ALU.add, ALU.mult)
                    dve.drain()
                    dve.tensor_scalar(nt_[:, :], nt_[:, :], -127.0 / 256, MAGIC, ALU.add, ALU.add)
                    dve.drain()
                    dve.tensor_scalar(nt_[:, :], nt_[:, :], -MAGIC, None, ALU.add)
                    dve.drain()
                    dve.tensor_tensor_scan(en[:, :], ones[:, 0:NE], nt_[:, :], 0.0, ALU.mult, ALU.add)
                    dve.tensor_tensor(RK[:, :, :], RK[:, :, :],
                                      PS[:, 4, 0:NE * NT].rearrange("p (e i) -> p e i", e=NE), ALU.subtract)
                    dve.drain()
                    dve.tensor_tensor(RK[:, :, :], RK[:, :, :],
                                      PS[:, 5, 0:NE * NT].rearrange("p (e i) -> p e i", e=NE), ALU.add)
                    dve.tensor_tensor(nt_[:, :], en[:, :], nt_[:, :], ALU.subtract)
                    dve.drain()
                    dve.tensor_scalar(nt_[:, :], nt_[:, :], float(P), None, ALU.mult)
                    dve.drain()
                    dve.tensor_tensor(RK[:, :, :], RK[:, :, :],
                                      nt_[:, :].unsqueeze(2).broadcast_to([P, NE, NT]), ALU.add)
                    dve.drain()
                    for j in range(ntop):
                        dve.tensor_tensor(M[:, :, :], RK[:, :, :], OH[j][:, :, :], ALU.mult)
                        dve.drain()
                        dve.tensor_reduce(sm[:, :], over_experts(M[:, :, :]), AX.X, ALU.add)
                        dve.drain()
                        dve.tensor_copy(pos[j][:, :], sm[:, :])
                        dve.drain()
                    dve.tensor_tensor(cmp_[:, :, :], trow[:, :, :],
                                      en[0:1, :].unsqueeze(2).broadcast_to([1, NE, tiles]), ALU.is_ge)
                    dve.drain()
                    dve.tensor_reduce(trow[:, 0, :], cmp_[:, 0:NE - 1, :].rearrange("p e r -> p r e"), AX.X, ALU.add)
                    dve.drain()
                    dve.tensor_copy(te[:, :], trow[:, 0, :])

            with nc.Block() as block:

                @block.gpsimd
                def _(pool):
                    for j in range(ntop):
                        for i in range(NT):
                            pool.indirect_dma_start(
                                out=XS, out_offset=bass.IndirectOffsetOnAxis(ap=pos[j][:, i:i + 1], axis=0),
                                in_=T[:, i, :], in_offset=None).then_inc(rows_moved["scattered"], 16)
                    pool.wait_ge(rows_moved["scattered"], 16 * ntop * NT)

        with ExitStack() as sub:
            def tb(n, shape, dt=F32):
                return sub.enter_context(nc.sbuf_tensor(f"{name}_{n}", shape, dt))

            two = range(2)
            xs, xt = [tb(f"xs{i}", [P, D]) for i in two], [tb(f"xt{i}", [P, P]) for i in two]
            ws = [tb(f"ws{i}", [P, FF + KF]) for i in two]
            hp, hid = [tb(f"hp{i}", [P, KF, P]) for i in two], [tb(f"hid{i}", [P, KF, P]) for i in two]
            res = [tb(f"res{i}", [P, D]) for i in two]

            with nc.Block() as block:

                @block.sync
                def _(sp):
                    with sp.Fori(0, tiles // 2) as k:
                        for p in two:
                            sp.wait_ge(s["xtr"], k * 2 + p + 1)
                            sp.dma_start(xs[p][:, :], XS[bass.ds((k * 2 + p) * P, P), :])\
                              .then_inc(s[f"xs{p}"], 16)

                @block.gpsimd
                def _(pool):
                    pool.wait_ge(s["w1"], 16)
                    with pool.Fori(0, tiles // 2) as k:
                        for p in two:
                            e = pool.value_load(te[0:1, bass.ds(k * 2 + p, 1)], min_val=0, max_val=NE - 1)
                            pool.wait_ge(s["pre"], k * 2 + p + 1)
                            pool.tensor_copy(ws[p][:, :], w1[:, e, :]).then_inc(s["picked"], 1)

                @block.tensor
                def _(pe):
                    pe.nop().then_inc(s["xtr"], 2)
                    pe.wait_ge(s["w2"], 16)
                    with pe.Fori(0, tiles // 2) as k:
                        es = [pe.value_load(te[0:1, bass.ds(k * 2 + p, 1)], min_val=0, max_val=NE - 1)
                              for p in two]
                        for p in two:
                            pe.wait_ge(s[f"xs{p}"], k * 16 + 16)
                            pe.transpose(PS[:, p, 0:P], xs[p][:, :], t.ident[:, :]).then_inc(s["xtr"], 1)
                        for p in two:
                            pe.wait_ge(s["xt"], k * 2 + p + 1)
                            pe.wait_ge(s["picked"], k * 2 + p + 1)
                            for j in range(KF):
                                mm = pe.matmul(PS[:, 2 + p, j * P:(j + 1) * P], ws[p][:, j * P:(j + 1) * P],
                                               xt[p][:, :], start=True, stop=True)
                            mm.then_inc(s["hid_ps"], 1)
                        for p in two:
                            pe.wait_ge(s["hid"], k * 2 + p + 1)
                            for j in range(KF):
                                mm = pe.matmul(PS[:, 4 + p, 0:D], hid[p][:, j, :], w2[:, es[p], j, :],
                                               start=(j == 0), stop=(j == KF - 1))
                            mm.then_inc(s["out_ps"], 1)

                @block.scalar
                def _(act):
                    with act.Fori(0, tiles // 2) as k:
                        for p in two:
                            act.wait_ge(s["xtr"], k * 2 + p + 3)
                            act.activation(xt[p][:, :], PS[:, p, 0:P], ACT.Copy).then_inc(s["xt"], 1)
                        for p in two:
                            act.wait_ge(s["pre"], k * 2 + p + 3)
                            act.activation(hid[p][:, :, :], hp[p][:, :, :], gelu).then_inc(s["hid"], 1)
                        for p in two:
                            act.wait_ge(s["res"], k * 2 + p + 1)
                            act.dma_start(YS[bass.ds((k * 2 + p) * P, P), :], res[p][:, :])\
                               .then_inc(s[f"sent{p}"], 16)
                    for p in two:
                        act.wait_ge(s[f"sent{p}"], 16 + 16 * (tiles // 2))

                @block.vector
                def _(dve):
                    dve.wait_ge(s["b2"], 16)
                    dve.nop().then_inc(s["pre"], 2)
                    for p in two:
                        dve.nop().then_inc(s[f"sent{p}"], 16)
                    with dve.Fori(0, tiles // 2) as k:
                        es = [dve.value_load(te[0:1, bass.ds(k * 2 + p, 1)], min_val=0, max_val=NE - 1)
                              for p in two]
                        for p in two:
                            dve.wait_ge(s["hid_ps"], k * 2 + p + 1)
                            dve.tensor_tensor(hp[p][:, :, :], PS[:, 2 + p, :].rearrange("f (j r) -> f j r", j=KF),
                                              ws[p][:, FF:FF + KF].unsqueeze(2).broadcast_to([P, KF, P]), ALU.add)\
                               .then_inc(s["pre"], 1)
                        for p in two:
                            dve.wait_ge(s["out_ps"], k * 2 + p + 1)
                            dve.wait_ge(s[f"sent{p}"], k * 16 + 16)
                            dve.tensor_tensor(res[p][:, :], PS[:, 4 + p, 0:D], b2[:, es[p], :], ALU.add)\
                               .then_inc(s["res"], 1)

        with ExitStack() as sub:
            got = [sub.enter_context(nc.sbuf_tensor(f"{name}_got{j}", [P, NT, D], F32)) for j in range(ntop)]
            with nc.Block() as block:

                @block.gpsimd
                def _(pool):
                    for j in range(ntop):
                        for i in range(NT):
                            pool.indirect_dma_start(
                                out=got[j][:, i, :], out_offset=None, in_=YS,
                                in_offset=bass.IndirectOffsetOnAxis(ap=pos[j][:, i:i + 1], axis=0))\
                                .then_inc(rows_moved["gathered"], 16)
                    pool.wait_ge(rows_moved["gathered"], 16 * ntop * NT)

            with nc.Block() as block:

                @block.vector
                def _(dve):
                    for j in range(ntop):
                        dve.tensor_tensor(got[j][:, :, :], got[j][:, :, :],
                                          gate[j][:, :].unsqueeze(2).broadcast_to([P, NT, D]), ALU.mult)
                    dve.drain()
                    for j in range(ntop):
                        dve.tensor_tensor(t.H[:, :, :], t.H[:, :, :], got[j][:, :, :], ALU.add)
                        dve.drain()
                    if not first_layer:
                        dve.tensor_tensor(t.H[:, :, :], t.H[:, :, :], t.U[:, :, :], ALU.add)
                        dve.drain()
                    with dve.Fori(0, NT) as i:
                        dve.bn_stats(t.BN[:, i, :], t.H[:, i, :])


def bitlinear_ffn(nc, t, a):
    ln_scales(nc, t, "bit_ln")
    with ExitStack() as ctx:
        def sb(n, shape, dt=F32):
            return ctx.enter_context(nc.sbuf_tensor(f"bit_{n}", shape, dt))

        s = Sems(nc, ctx, "bit", "weights ones sums sum_ps ident xq tr xt up_ps h hq htr ht out_ps")
        up, down = sb("up", [P, FF]), sb("down", [P, KF, D])
        upq, downq = sb("upq", [P, FF], BF16), sb("downq", [P, KF, D], BF16)
        identb = sb("ident", [P, P], BF16)
        ones, sums, ws, wi = sb("ones", [P, P]), sb("sums", [P, 2]), sb("ws", [P, 2]), sb("wi", [P, 2])
        two = range(2)
        us = [sb(f"us{i}", [P, D]) for i in two]
        am, xsc, osc = ([sb(f"{n}{i}", [P, 2]) for i in two] for n in ("am", "xsc", "osc"))
        xq, xt = [sb(f"xq{i}", [P, D], BF16) for i in two], [sb(f"xt{i}", [P, P], BF16) for i in two]
        h = [sb(f"h{i}", [P, FF]) for i in two]
        hq, ht = [sb(f"hq{i}", [P, FF], BF16) for i in two], [sb(f"ht{i}", [P, FF], BF16) for i in two]
        PS = t.PS
        PB = PS[:, :, :].bitcast(BF16)

        with nc.Block() as block:
            load_all(block, [(up, a["bit_up"]), (down, a["bit_down"])], s["weights"])

            @block.tensor
            def _(pe):
                pe.wait_ge(s["sums"], 1)
                pe.matmul(PS[:, 0, 0:2], ones[:, :], sums[:, :], start=True, stop=True).then_inc(s["sum_ps"], 1)

            @block.vector
            def _(dve):
                dve.memset(ones[:, :], 1.0)
                dve.tensor_copy(identb[:, :], t.ident[:, :])
                dve.wait_ge(s["weights"], 32)
                dve.tensor_reduce(sums[:, 0:1], up[:, :], AX.X, ALU.add, apply_absolute_value=True)
                dve.tensor_reduce(sums[:, 1:2], down[:, :, :], AX.XY, ALU.add, apply_absolute_value=True)
                dve.drain()
                dve.nop().then_inc(s["sums"], 1)
                dve.wait_ge(s["sum_ps"], 1)
                dve.tensor_scalar(ws[:, :], PS[:, 0, 0:2], 1.0 / (D * FF), EPS, ALU.mult, ALU.max)
                dve.drain()
                dve.reciprocal(wi[:, :], ws[:, :])
                dve.drain()
                for n, (w, q) in enumerate(((up[:, :], upq[:, :]), (down[:, :, :], downq[:, :, :]))):
                    dve.tensor_scalar(w, w, wi[:, n:n + 1], MAGIC, ALU.mult, ALU.add)
                    dve.drain()
                    dve.tensor_scalar(w, w, -MAGIC, 1.0, ALU.add, ALU.min)
                    dve.drain()
                    dve.tensor_scalar(q, w, -1.0, None, ALU.max)

        with nc.Block() as block:

            @block.tensor
            def _(pe):
                with pe.Fori(0, NT // 2) as k:
                    for p in two:
                        pe.wait_ge(s["xq"], k * 2 + p + 1)
                        pe.transpose(PB[:, p, 0:P], xq[p][:, :], identb[:, :]).then_inc(s["tr"], 1)
                    for p in two:
                        pe.wait_ge(s["xt"], k * 2 + p + 1)
                        pe.matmul(PS[:, 2 + p, :], xt[p][:, :], upq[:, :], start=True, stop=True)\
                          .then_inc(s["up_ps"], 1)
                    for p in two:
                        pe.wait_ge(s["hq"], k * 2 + p + 1)
                        for j in range(KF):
                            mm = pe.transpose(PB[:, 4 + p, j * P:(j + 1) * P], hq[p][:, j * P:(j + 1) * P],
                                              identb[:, :])
                        mm.then_inc(s["htr"], 1)
                    for p in two:
                        pe.wait_ge(s["ht"], k * 2 + p + 1)
                        for j in range(KF):
                            mm = pe.matmul(PS[:, 6 + p, 0:D], ht[p][:, j * P:(j + 1) * P], downq[:, j, :],
                                           start=(j == 0), stop=(j == KF - 1))
                        mm.then_inc(s["out_ps"], 1)

            @block.scalar
            def _(act):
                with act.Fori(0, NT // 2) as k:
                    for p in two:
                        act.wait_ge(s["tr"], k * 2 + p + 1)
                        act.activation(xt[p][:, :], PB[:, p, 0:P], ACT.Copy).then_inc(s["xt"], 1)
                    for p in two:
                        act.wait_ge(s["up_ps"], k * 2 + p + 1)
                        act.activation(h[p][:, :], PS[:, 2 + p, :], ACT.Relu, scale=osc[p][:, 0:1])\
                           .then_inc(s["h"], 1)
                    for p in two:
                        act.wait_ge(s["htr"], k * 2 + p + 1)
                        act.activation(ht[p][:, :], PB[:, 4 + p, 0:FF], ACT.Copy).then_inc(s["ht"], 1)

            @block.vector
            def _(dve):
                def scales(p, n):
                    dve.drain()
                    dve.reciprocal(xsc[p][:, n:n + 1], am[p][:, n:n + 1])
                    dve.tensor_scalar(osc[p][:, n:n + 1], am[p][:, n:n + 1], 1.0 / 127, ws[:, n:n + 1],
                                      ALU.mult, ALU.mult)
                    dve.drain()
                    dve.tensor_scalar(xsc[p][:, n:n + 1], xsc[p][:, n:n + 1], 127.0, None, ALU.mult)
                    dve.drain()

                with dve.Fori(0, NT // 2) as k:
                    for p in two:
                        i = k * 2 + p
                        dve.tensor_scalar(us[p][:, :], t.H[:, i, :], t.MEAN[:, bass.ds(i, 1)],
                                          t.RSTD[:, bass.ds(i, 1)], ALU.subtract, ALU.mult)
                        dve.drain()
                        dve.tensor_reduce(am[p][:, 0:1], us[p][:, :], AX.X, ALU.max, apply_absolute_value=True)
                        dve.drain()
                        dve.tensor_scalar(am[p][:, 0:1], am[p][:, 0:1], EPS, None, ALU.max)
                        scales(p, 0)
                        dve.tensor_scalar(us[p][:, :], us[p][:, :], xsc[p][:, 0:1], MAGIC, ALU.mult, ALU.add)
                        dve.drain()
                        dve.tensor_scalar(xq[p][:, :], us[p][:, :], -MAGIC, None, ALU.add).then_inc(s["xq"], 1)
                    for p in two:
                        dve.wait_ge(s["h"], k * 2 + p + 1)
                        dve.tensor_scalar(h[p][:, :], h[p][:, :], MAGIC, -MAGIC, ALU.add, ALU.add)
                        dve.drain()
                        dve.tensor_reduce(am[p][:, 1:2], h[p][:, :], AX.X, ALU.max)
                        dve.drain()
                        dve.tensor_scalar(am[p][:, 1:2], am[p][:, 1:2], 127.0, EPS, ALU.min, ALU.max)
                        scales(p, 1)
                        dve.tensor_scalar(h[p][:, :], h[p][:, :], 127.0, xsc[p][:, 1:2], ALU.min, ALU.mult)
                        dve.drain()
                        dve.tensor_scalar(hq[p][:, :], h[p][:, :], MAGIC, -MAGIC, ALU.add, ALU.add)\
                           .then_inc(s["hq"], 1)
                    for p in two:
                        i = k * 2 + p
                        dve.wait_ge(s["out_ps"], k * 2 + p + 1)
                        dve.scalar_tensor_tensor(t.H[:, i, :], PS[:, 6 + p, 0:D], osc[p][:, 1:2], t.H[:, i, :],
                                                 ALU.mult, ALU.add)
                        dve.drain()
                        dve.bn_stats(t.BN[:, i, :], t.H[:, i, :])


def state_space(nc, t, a):
    N = NSTATE
    ln_scales(nc, t, "ssm_ln")
    with ExitStack() as ctx:
        def sb(n, shape, dt=F32):
            return ctx.enter_context(nc.sbuf_tensor(f"ssm_{n}", shape, dt))

        s = Sems(nc, ctx, "ssm", "loaded dt pe dve kernel zeros hankel u conv")
        A, E, G = sb("a", [N, 2, N]), sb("e", [N, 2, N]), sb("g", [N, 2, N])
        inv_t, bc, ldt, dt = sb("inv_t", [N, N]), sb("bc", [N, 2]), sb("ldt", [N, 1]), sb("dt", [N, 1])
        skip, flip = sb("skip", [P, 1]), sb("flip", [P, P])
        V, C, eb = sb("v", [N, 16]), sb("c", [N, 16]), sb("eb", [N, 1])
        K, zeros = sb("k", [16, 16]), sb("zeros", [1, L])
        hankel, toep = sb("hankel", [P, 2, P]), sb("toep", [P, 2, P])
        U = sb("u", [P, NT, D])
        KZ = nc.dram_tensor("ssm_kernel", [2 * L], F32).ap()
        loads = [(A, a["c_hippo"]), (inv_t, a["c_hippo_inv_t"]), (bc, a["ssm_bc"]), (ldt, a["ssm_log_dt"]),
                 (skip, a["ssm_d"]), (flip, a["c_flip"])]
        PS = t.PS
        U4 = U[:, :, :].rearrange("p (b h) c -> p b h c", h=2)
        doublings = [(V, m) for m in (1, 2, 4, 8)] + [(C, m) for m in (1, 2, 4, 8)]
        TERMS = 8

        with nc.Block() as block:

            @block.sync
            def _(sp):
                for dst, src in loads:
                    sp.dma_start(dst[tuple(slice(None) for _ in dst.shape)], src).then_inc(s["loaded"], 16)
                sp.wait_ge(s["zeros"], 1)
                sp.dma_start(KZ[L:2 * L].unsqueeze(0), zeros[:, :]).then_inc(s["kernel"], 16)
                sp.wait_ge(s["dve"], TERMS + SQUARINGS + 3 + 2 * len(doublings))
                sp.dma_start(KZ[0:L].rearrange("(i j) -> i j", i=16), K[:, :]).then_inc(s["kernel"], 16)
                sp.wait_ge(s["kernel"], 32)
                for n in range(2):
                    sp.dma_start(hankel[:, n, :], bass.AP(KZ.tensor, P * (1 - n), [[1, P], [1, P]]))\
                      .then_inc(s["hankel"], 16)

            @block.scalar
            def _(act):
                act.wait_ge(s["loaded"], 16 * len(loads))
                act.activation(dt[:, :], ldt[:, :], ACT.Exp).then_inc(s["dt"], 1)

            @block.tensor
            def _(pe):
                done = [0]

                def after_dve():
                    done[0] += 1
                    pe.wait_ge(s["dve"], done[0])

                def pair(x, y):
                    after_dve()
                    pe.matmul(PS[0:N, 0, 0:N], x[:, 1, :], y[:, 0, :], start=True, stop=True)
                    pe.matmul(PS[0:N, 0, N:2 * N], x[:, 0, :], y[:, 1, :], start=True, stop=True)\
                      .then_inc(s["pe"], 1)

                for _ in range(TERMS - 1):
                    pair(A, G)
                pair(A, G)
                for _ in range(SQUARINGS):
                    pair(E, E)
                after_dve()
                pe.matmul(PS[0:N, 0, 0:1], E[:, 1, :], bc[:, 0:1], start=True, stop=True).then_inc(s["pe"], 1)
                after_dve()
                pe.matmul(PS[0:N, 0, 0:1], inv_t[:, :], eb[:, :], start=True, stop=True).then_inc(s["pe"], 1)
                for n, (x, m) in enumerate(doublings):
                    after_dve()
                    side = E[:, 1, :] if x is V else E[:, 0, :]
                    pe.matmul(PS[0:N, 0, 0:m], side, x[:, 0:m], start=True, stop=True).then_inc(s["pe"], 1)
                    if n < len(doublings) - 1:
                        pair(E, E)
                after_dve()
                pe.matmul(PS[0:16, 0, 0:16], C[:, :], V[:, :], start=True, stop=True).then_inc(s["pe"], 1)
                pe.wait_ge(s["hankel"], 32)
                for n in range(2):
                    mm = pe.matmul(PS[:, 1, n * P:(n + 1) * P], hankel[:, n, :], flip[:, :], start=True, stop=True)
                mm.then_inc(s["pe"], 1)

            @block.vector
            def _(dve):
                done = [0]

                def after_pe():
                    done[0] += 1
                    dve.wait_ge(s["pe"], done[0])

                dve.memset(zeros[:, :], 0.0).then_inc(s["zeros"], 1)
                dve.wait_ge(s["dt"], 1)
                dve.tensor_scalar(A[:, :, :], A[:, :, :], dt[:, :], 2.0 ** -SQUARINGS, ALU.mult, ALU.mult)
                dve.tensor_copy(G[:, 0, :], t.ident[0:N, 0:N])
                dve.tensor_copy(G[:, 1, :], t.ident[0:N, 0:N])
                dve.drain()
                dve.nop().then_inc(s["dve"], 1)
                product = PS[0:N, 0, 0:2 * N].rearrange("p (h c) -> p h c", h=2)
                eye = t.ident[0:N, 0:N].unsqueeze(1).broadcast_to([N, 2, N])
                for n in range(TERMS, 1, -1):
                    after_pe()
                    dve.scalar_tensor_tensor(G[:, :, :], product, 1.0 / n, eye, ALU.mult, ALU.add)\
                       .then_inc(s["dve"], 1)
                after_pe()
                dve.tensor_copy(E[:, :, :], product).then_inc(s["dve"], 1)

                def double():
                    after_pe()
                    dve.scalar_tensor_tensor(E[:, :, :], E[:, :, :], 2.0, product, ALU.mult, ALU.add)\
                       .then_inc(s["dve"], 1)

                for _ in range(SQUARINGS):
                    double()
                after_pe()
                dve.tensor_copy(eb[:, :], PS[0:N, 0, 0:1]).then_inc(s["dve"], 1)
                after_pe()
                dve.tensor_copy(V[:, 0:1], PS[0:N, 0, 0:1])
                dve.tensor_copy(C[:, 0:1], bc[:, 1:2])
                dve.drain()
                dve.nop().then_inc(s["dve"], 1)
                for n, (x, m) in enumerate(doublings):
                    after_pe()
                    dve.tensor_tensor(x[:, m:2 * m], x[:, 0:m], PS[0:N, 0, 0:m], ALU.add).then_inc(s["dve"], 1)
                    if n < len(doublings) - 1:
                        double()
                after_pe()
                dve.tensor_copy(K[:, :], PS[0:16, 0, 0:16]).then_inc(s["dve"], 1)
                after_pe()
                dve.tensor_copy(toep[:, :, :], PS[:, 1, 0:2 * P].rearrange("p (n c) -> p n c", n=2))
                with dve.Fori(0, NT) as i:
                    dve.tensor_scalar(U[:, i, :], t.H[:, i, :], t.MEAN[:, bass.ds(i, 1)],
                                      t.RSTD[:, bass.ds(i, 1)], ALU.subtract, ALU.mult)

        with nc.Block() as block:

            @block.tensor
            def _(pe):
                for g in range(4):
                    rhs = [U4[:, 4 * g:4 * g + 4, h, :] for h in range(2)]
                    pe.matmul(PS[:, 2 * g, :], toep[:, 0, :], rhs[0], start=True, stop=True)
                    pe.matmul(PS[:, 2 * g + 1, :], toep[:, 1, :], rhs[0], start=True, stop=False)
                    pe.matmul(PS[:, 2 * g + 1, :], toep[:, 0, :], rhs[1], start=False, stop=True)\
                      .then_inc(s["conv"], 1)

            @block.vector
            def _(dve):
                H4 = t.H[:, :, :].rearrange("p (b h) c -> p b h c", h=2)
                dve.scalar_tensor_tensor(t.H[:, :, :], U[:, :, :], skip[:, 0:1], t.H[:, :, :], ALU.mult, ALU.add)
                dve.drain()
                for g in range(4):
                    dve.wait_ge(s["conv"], g + 1)
                    for h in range(2):
                        dve.tensor_tensor(H4[:, 4 * g:4 * g + 4, h, :], H4[:, 4 * g:4 * g + 4, h, :],
                                          PS[:, 2 * g + h, :].rearrange("p (b c) -> p b c", b=4), ALU.add)
                dve.drain()
                with dve.Fori(0, NT) as i:
                    dve.bn_stats(t.BN[:, i, :], t.H[:, i, :])


def bilinear_attention(nc, t, a):
    ln_scales(nc, t, "bil_ln")
    with ExitStack() as ctx:
        def sb(n, shape, dt=F32):
            return ctx.enter_context(nc.sbuf_tensor(f"bil_{n}", shape, dt))

        s = Sems(nc, ctx, "bil", "weights u tr ut v_ps v tq_ps tq st_ps mx exp pr_ps pr av_ps")
        wq, wv = sb("wq", [P, NH, D]), sb("wv", [P, D])
        two = range(2)
        us, ut = [sb(f"us{i}", [P, 2, D]) for i in two], [sb(f"ut{i}", [P, L]) for i in two]
        v = [sb(f"v{i}", [P, 2, NH, HV]) for i in two]
        tq = [sb(f"tq{i}", [P, NH, L]) for i in two]
        nm = [sb(f"nm{i}", [P, NH, 2]) for i in two]
        pr = [sb(f"pr{i}", [P, 2, 2, L]) for i in two]
        pt = [sb(f"pt{i}", [P, NH, 2, L]) for i in two]
        rc, oc = [sb(f"rc{i}", [P, 2, NH]) for i in two], [sb(f"oc{i}", [P, 2, NH, HD]) for i in two]
        attention_prelude(nc, t, s, None, None, v, [(wq, a["bil_q"]), (wv, a["bil_v"])])
        PS = t.PS

        with nc.Block() as block:

            @block.tensor
            def _(pe):
                with pe.Fori(0, NB // 2) as k:
                    for p in two:
                        c = k * 2 + p + 1
                        pe.wait_ge(s["u"], c)
                        for h in range(2):
                            mm = pe.transpose(PS[:, 4 + 2 * p, h * P:(h + 1) * P], us[p][:, h, :], t.ident[:, :])
                        mm.then_inc(s["tr"], 1)
                    for p in two:
                        pe.wait_ge(s["ut"], k * 2 + p + 1)
                        for n in range(4):
                            if p == 1:
                                pe.wait_ge(s["tq"], k * 8 + n + 1)
                            for h in range(2):
                                mm = pe.matmul(PS[:, n, h * L:(h + 1) * L], wq[:, 2 * n + h, :], ut[p][:, :],
                                               start=True, stop=True)
                            mm.then_inc(s["tq_ps"], 1)
                        for h in range(2):
                            mm = pe.matmul(PS[:, 5 + 2 * p, h * D:(h + 1) * D], ut[p][:, h * P:(h + 1) * P],
                                           wv[:, :], start=True, stop=True)
                        mm.then_inc(s["v_ps"], 1)

                    def scores(m):
                        p, n = m // 4, m % 4
                        if m < 2:
                            pe.wait_ge(s["tq"], k * 8 + 8)
                        else:
                            pe.wait_ge(s["exp"], k * 8 + m - 1)
                        for h in range(2):
                            for q in range(2):
                                mm = pe.matmul(PS[:, 2 * (m % 2) + h, q * L:(q + 1) * L],
                                               tq[p][:, 2 * n + h, q * P:(q + 1) * P], ut[p][:, :],
                                               start=True, stop=True)
                        mm.then_inc(s["st_ps"], 1)

                    def turn(m):
                        if m < 2:
                            pe.wait_ge(s["v"], k * 2 + m + 1)
                        else:
                            pe.wait_ge(s["pr"], k * 8 + m - 1)
                        pe.wait_ge(s["exp"], k * 8 + m + 1)
                        for h in range(2):
                            for q in range(2):
                                for tile in range(2):
                                    o = tile * L + q * P
                                    mm = pe.transpose(PS[:, 4 + 2 * (m % 2) + h, o:o + P],
                                                      pr[m % 2][:, h, q, tile * P:(tile + 1) * P], t.ident[:, :])
                        mm.then_inc(s["pr_ps"], 1)

                    scores(0)
                    for m in range(1, 8):
                        scores(m)
                        turn(m - 1)
                    turn(7)
                    pe.wait_ge(s["pr"], k * 8 + 8)
                    for p in two:
                        for q in range(2):
                            for h in range(NH):
                                o = q * NH * HV + h * HV
                                for tile in range(2):
                                    mm = pe.matmul(PS[:, 5 + 2 * p, o:o + HV],
                                                   pt[p][:, h, tile, q * P:(q + 1) * P], v[p][:, tile, h, :],
                                                   start=(tile == 0), stop=(tile == 1))
                        mm.then_inc(s["av_ps"], 1)

            @block.scalar
            def _(act):
                with act.Fori(0, NB // 2) as k:
                    for p in two:
                        act.wait_ge(s["tr"], k * 2 + p + 1)
                        act.activation(ut[p][:, :], PS[:, 4 + 2 * p, 0:L], ACT.Copy).then_inc(s["ut"], 1)
                    for p in two:
                        for n in range(4):
                            act.wait_ge(s["tq_ps"], k * 8 + p * 4 + n + 1)
                            act.activation(tq[p][:, 2 * n:2 * n + 2, :].rearrange("p h c -> p (h c)"), PS[:, n, :],
                                           ACT.Copy).then_inc(s["tq"], 1)
                    for m in range(8):
                        p, n = m // 4, m % 4
                        act.wait_ge(s["mx"], k * 8 + m + 1)
                        for h in range(2):
                            for q in range(2):
                                i = act.activation(pr[m % 2][:, h, q, :],
                                                   PS[:, 2 * (m % 2) + h, q * L:(q + 1) * L], ACT.Exp,
                                                   bias=nm[p][:, 2 * n + h, q:q + 1])
                        i.then_inc(s["exp"], 1)

            @block.vector
            def _(dve):
                with dve.Fori(0, NB // 2) as k:
                    for p in two:
                        for h in range(2):
                            i = k * 4 + p * 2 + h
                            u = dve.tensor_scalar(us[p][:, h, :], t.H[:, i, :], t.MEAN[:, bass.ds(i, 1)],
                                                  t.RSTD[:, bass.ds(i, 1)], ALU.subtract, ALU.mult)
                        u.then_inc(s["u"], 1)
                    for p in two:
                        dve.wait_ge(s["v_ps"], k * 2 + p + 1)
                        for h in range(2):
                            i = dve.tensor_copy(v[p][:, h, :, 0:HD], PS[:, 5 + 2 * p, h * D:(h + 1) * D].rearrange(
                                "q (h d) -> q h d", h=NH))
                        i.then_inc(s["v"], 1)

                    def maxima(m):
                        p, n = m // 4, m % 4
                        dve.wait_ge(s["st_ps"], k * 8 + m + 1)
                        b = 2 * (m % 2)
                        dve.tensor_reduce(nm[p][:, 2 * n:2 * n + 2, :],
                                          PS[:, b:b + 2, :].rearrange("q i (j c) -> q i j c", j=2),
                                          AX.X, ALU.max, negate=True).then_inc(s["mx"], 1)

                    def evict(m):
                        p, n = m // 4, m % 4
                        dve.wait_ge(s["pr_ps"], k * 8 + m + 1)
                        b = 4 + 2 * (m % 2)
                        dve.tensor_copy(pt[p][:, 2 * n:2 * n + 2].rearrange("q h j c -> q h (j c)"),
                                        PS[:, b:b + 2, :]).then_inc(s["pr"], 1)

                    maxima(0)
                    for m in range(1, 8):
                        maxima(m)
                        evict(m - 1)
                    evict(7)
                    for p in two:
                        dve.wait_ge(s["av_ps"], k * 2 + p + 1)
                        av = PS[:, 5 + 2 * p, 0:2 * NH * HV].rearrange("q (j h e) -> q j h e", j=2, h=NH)
                        dve.reciprocal(rc[p][:, :, :], av[:, :, :, HD])
                        dve.drain()
                        for q in range(2):
                            dve.tensor_tensor(oc[p][:, q], av[:, q, :, 0:HD],
                                              rc[p][:, q, :].unsqueeze(2).broadcast_to([P, NH, HD]), ALU.mult)
                        dve.drain()
                        i0 = k * 4 + p * 2
                        dve.tensor_tensor(t.H[:, bass.ds(i0, 2), :], t.H[:, bass.ds(i0, 2), :],
                                          oc[p][:, :].rearrange("q j h d -> q j (h d)"), ALU.add)
                        dve.drain()
                        for q in range(2):
                            dve.bn_stats(t.BN[:, i0 + q, :], t.H[:, i0 + q, :])


def expert_choice(nc, t, a, out):
    ln_scales(nc, t, "ec_ln")
    rows = out.rearrange("b l c -> (b l) c")
    NG = EC // ECG
    with ExitStack() as ctx:
        def sb(n, shape, dt=F32):
            return ctx.enter_context(nc.sbuf_tensor(f"ec_{n}", shape, dt))

        s = Sems(nc, ctx, "ec", "weights staged tr tt logits exp_in exp probs turned in_rows picked picked_t idx "
                                "u_sent h_sent gathered xg xg_staged xtr xt up_ps hid out_ps y scattered freed "
                                "up0 up1 down0 down1 late")
        s.restart(nc)
        UD = nc.dram_tensor("ec_tokens", [NT * P, D], F32).ap()
        wr, br = sb("wr", [P, EC]), sb("br", [P, EC])
        bup, bdown = sb("bup", [P, NG, 3]), sb("bdown", [P, EC, D])
        vals_t, idx_t, idx_u = sb("vals_t", [P, EC]), sb("idx_t", [P, EC]), sb("idx_u", [P, EC], U32)
        PS = t.PS
        two = range(2)

        with ExitStack() as sub:
            def tb(n, shape, dt=F32):
                return sub.enter_context(nc.sbuf_tensor(f"ec_{n}", shape, dt))

            U = tb("u", [P, NT, D])
            stage, tt = [tb(f"st{i}", [P, D]) for i in two], [tb(f"tt{i}", [P, P]) for i in two]
            LG, sm, row = tb("lg", [P, NT, EC]), tb("sm", [P, NT]), tb("row", [EC, NT * P])
            vals, idx, idxf = tb("vals", [EC, ECK]), tb("idx", [EC, ECK], U32), tb("idxf", [EC, ECK])

            with nc.Block() as block:

                @block.sync
                def _(sp):
                    sp.dma_start(wr[:, :], a["ec_wr"]).then_inc(s["weights"], 16)
                    sp.dma_start(br[:, :], a["ec_br"]).then_inc(s["weights"], 16)
                    sp.dma_start(bup[:, :, :], a["ec_bup"]).then_inc(s["late"], 16)
                    sp.dma_start(bdown[:, :, :], a["ec_bdown"]).then_inc(s["late"], 16)
                    sp.dma_start(rows.rearrange("(i p) c -> p i c", p=P), t.H[:, :, :]).then_inc(s["h_sent"], 16)
                    sp.wait_ge(s["staged"], NT)
                    sp.dma_start(UD.rearrange("(i p) c -> p i c", p=P), U[:, :, :]).then_inc(s["u_sent"], 16)
                    sp.wait_ge(s["u_sent"], 16)
                    sp.wait_ge(s["h_sent"], 16)
                    sp.wait_ge(s["late"], 32)

                @block.tensor
                def _(pe):
                    pe.wait_ge(s["weights"], 32)
                    with pe.Fori(0, NT // 2) as k:
                        for p in two:
                            pe.wait_ge(s["staged"], k * 2 + p + 1)
                            pe.transpose(PS[:, p, 0:P], stage[p][:, :], t.ident[:, :]).then_inc(s["tr"], 1)
                        for p in two:
                            pe.wait_ge(s["tt"], k * 2 + p + 1)
                            pe.matmul(PS[:, 2 + p, 0:EC], tt[p][:, :], wr[:, :], start=True, stop=True)\
                              .then_inc(s["logits"], 1)
                    pe.wait_ge(s["probs"], 1)
                    for i in range(NT):
                        mm = pe.transpose(PS[0:EC, i // 4, (i % 4) * P:(i % 4 + 1) * P], LG[:, i, :], t.ident[:, :])
                        if i % 4 == 3:
                            mm.then_inc(s["turned"], 1)
                    pe.wait_ge(s["picked"], 1)
                    pe.transpose(PS[:, 0, 0:EC], vals[:, :], t.ident[0:EC, 0:EC])
                    pe.transpose(PS[:, 0, EC:2 * EC], idxf[:, :], t.ident[0:EC, 0:EC]).then_inc(s["picked_t"], 1)

                @block.scalar
                def _(act):
                    with act.Fori(0, NT // 2) as k:
                        for p in two:
                            act.wait_ge(s["tr"], k * 2 + p + 1)
                            act.activation(tt[p][:, :], PS[:, p, 0:P], ACT.Copy).then_inc(s["tt"], 1)
                    act.wait_ge(s["exp_in"], 1)
                    act.activation(LG[:, :, :], LG[:, :, :], ACT.Exp).then_inc(s["exp"], 1)

                @block.vector
                def _(dve):
                    dve.wait_ge(s["weights"], 32)
                    with dve.Fori(0, NT // 2) as k:
                        for p in two:
                            i = k * 2 + p
                            dve.tensor_scalar(U[:, i, :], t.H[:, i, :], t.MEAN[:, bass.ds(i, 1)],
                                              t.RSTD[:, bass.ds(i, 1)], ALU.subtract, ALU.mult)
                        dve.drain()
                        for p in two:
                            dve.tensor_copy(stage[p][:, :], U[:, k * 2 + p, :]).then_inc(s["staged"], 1)
                        for p in two:
                            dve.wait_ge(s["logits"], k * 2 + p + 1)
                            dve.tensor_tensor(LG[:, k * 2 + p, :], PS[:, 2 + p, 0:EC], br[:, :], ALU.add)
                    dve.drain()
                    dve.tensor_reduce(sm[:, :], LG[:, :, :], AX.X, ALU.max)
                    dve.drain()
                    over = sm[:, :].unsqueeze(2).broadcast_to([P, NT, EC])
                    dve.tensor_tensor(LG[:, :, :], LG[:, :, :], over, ALU.subtract).then_inc(s["exp_in"], 1)
                    dve.wait_ge(s["exp"], 1)
                    dve.tensor_reduce(sm[:, :], LG[:, :, :], AX.X, ALU.add)
                    dve.drain()
                    dve.reciprocal(sm[:, :], sm[:, :])
                    dve.drain()
                    dve.tensor_tensor(LG[:, :, :], LG[:, :, :], over, ALU.mult).then_inc(s["probs"], 1)
                    for b in range(8):
                        dve.wait_ge(s["turned"], b + 1)
                        dve.tensor_copy(row[:, b * 512:(b + 1) * 512], PS[0:EC, b, :])
                    dve.drain()
                    for r in range(ECK // 8):
                        v8 = vals[:, 8 * r:8 * r + 8]
                        dve.max(v8, row[:, :])
                        dve.drain()
                        dve.max_index(idx[:, 8 * r:8 * r + 8], v8, row[:, :])
                        dve.drain()
                        dve.match_replace(row[:, :], v8, row[:, :], -1.0)
                        dve.drain()
                    dve.tensor_copy(idxf[:, :], idx[:, :]).then_inc(s["picked"], 1)
                    dve.wait_ge(s["picked_t"], 1)
                    dve.tensor_copy(vals_t[:, :], PS[:, 0, 0:EC])
                    dve.tensor_copy(idx_u[:, :], PS[:, 0, EC:2 * EC])

        XG = sb("xg", [P, EC, D])
        wu = [sb(f"wu{i}", [P, ECF]) for i in two]
        wd = [sb(f"wd{i}", [P, ECG, 3, D]) for i in two]
        xg, xt = [sb(f"xgs{i}", [P, ECG, D]) for i in two], [sb(f"xt{i}", [P, ECG * P]) for i in two]
        hid = [sb(f"hid{i}", [P, 3, ECG * P]) for i in two]
        y = [sb(f"y{i}", [P, ECG, D]) for i in two]
        with nc.Block() as block:

            @block.sync
            def _(sp):
                with sp.Fori(0, NG // 2) as k:
                    for p in two:
                        g = k * 2 + p
                        sp.wait_ge(s["hid"], g * 3 + 3)
                        sp.dma_start(wu[p][:, :], a["ec_up"][bass.ds(g, 1)].rearrange("g h f -> h (g f)"))\
                          .then_inc(s[f"up{p}"], 16)
                        sp.wait_ge(s["out_ps"], g + 1)
                        down = a["ec_down"][bass.ds(g * ECG, ECG)]
                        for j, (f, n) in enumerate(ECT):
                            sp.dma_start(wd[p][0:n, :, j, :], down[:, f:f + n, :].rearrange("j f c -> f j c"))\
                              .then_inc(s[f"down{p}"], 16)

            @block.gpsimd
            def _(pool):
                for e in range(EC):
                    pool.indirect_dma_start(out=XG[:, e, :], out_offset=None, in_=UD,
                                            in_offset=bass.IndirectOffsetOnAxis(ap=idx_u[:, e:e + 1], axis=0))\
                        .then_inc(s["gathered"], 16)
                    if e % ECG == ECG - 1:
                        pool.wait_ge(s["gathered"], 16 * (e + 1))
                        pool.nop().then_inc(s["xg"], 1)
                pool.nop().then_inc(s["freed"], 2)
                for e in range(EC):
                    if e:
                        pool.wait_ge(s["scattered"], 16 * e)
                        if e % ECG == 0:
                            pool.nop().then_inc(s["freed"], 1)
                    pool.wait_ge(s["y"], 2 + e // ECG + 1)
                    pool.indirect_dma_start(out=rows, out_offset=bass.IndirectOffsetOnAxis(ap=idx_u[:, e:e + 1], axis=0),
                                            in_=y[e // ECG % 2][:, e % ECG, :], in_offset=None,
                                            compute_op=ALU.add).then_inc(s["scattered"], 16)
                pool.wait_ge(s["scattered"], 16 * EC)

            @block.tensor
            def _(pe):
                pe.nop().then_inc(s["out_ps"], 2)
                with pe.Fori(0, NG // 2) as k:
                    for p in two:
                        g = k * 2 + p
                        pe.wait_ge(s["xg_staged"], g + 1)
                        for j in range(ECG):
                            mm = pe.transpose(PS[:, p, j * P:(j + 1) * P], xg[p][:, j, :], t.ident[:, :])
                        mm.then_inc(s["xtr"], 1)
                        pe.wait_ge(s["xt"], g + 1)
                        pe.wait_ge(s[f"up{p}"], k * 16 + 16)
                        for j, (f, n) in enumerate(ECT):
                            pe.wait_ge(s["hid"], g * 3 + j + 4)
                            pe.matmul(PS[0:n, 2 + j, :], wu[p][:, f:f + n], xt[p][:, :], start=True, stop=True)\
                              .then_inc(s["up_ps"], 1)
                        pe.wait_ge(s["hid"], g * 3 + 9)
                        pe.wait_ge(s[f"down{p}"], k * 48 + 48)
                        pe.wait_ge(s["y"], g + 1)
                        for e in range(ECG):
                            for j, (f, n) in enumerate(ECT):
                                mm = pe.matmul(PS[:, 5 + p, e * D:(e + 1) * D], hid[p][0:n, j, e * P:(e + 1) * P],
                                               wd[p][0:n, e, j, :], start=(j == 0), stop=(j == 2))
                        mm.then_inc(s["out_ps"], 1)

            @block.scalar
            def _(act):
                act.nop().then_inc(s["hid"], 6)
                with act.Fori(0, NG // 2) as k:
                    for p in two:
                        g = k * 2 + p
                        act.wait_ge(s["xtr"], g + 1)
                        act.activation(xt[p][:, :], PS[:, p, :], ACT.Copy).then_inc(s["xt"], 1)
                        for j, (f, n) in enumerate(ECT):
                            act.wait_ge(s["up_ps"], g * 3 + j + 1)
                            act.activation(hid[p][0:n, j, :], PS[0:n, 2 + j, :], ACT.Silu,
                                           bias=bup[0:n, bass.ds(g, 1), j]).then_inc(s["hid"], 1)

            @block.vector
            def _(dve):
                dve.nop().then_inc(s["y"], 2)
                with dve.Fori(0, NG // 2) as k:
                    for p in two:
                        g = k * 2 + p
                        dve.wait_ge(s["xg"], g + 1)
                        dve.tensor_copy(xg[p][:, :, :], XG[:, bass.ds(g * ECG, ECG), :])\
                           .then_inc(s["xg_staged"], 1)
                        dve.wait_ge(s["out_ps"], g + 3)
                        dve.wait_ge(s["freed"], g + 1)
                        dve.tensor_tensor(y[p][:, :, :], PS[:, 5 + p, :].rearrange("r (e c) -> r e c", e=ECG),
                                          bdown[:, bass.ds(g * ECG, ECG), :], ALU.add)
                        dve.drain()
                        dve.tensor_tensor(y[p][:, :, :], y[p][:, :, :],
                                          vals_t[:, bass.ds(g * ECG, ECG)].unsqueeze(2).broadcast_to([P, ECG, D]),
                                          ALU.mult).then_inc(s["y"], 1)


def alloc_shared(nc, t, ctx):
    def sb(name, shape, dt=F32):
        return ctx.enter_context(nc.sbuf_tensor(name, shape, dt))

    t.H = sb("hidden", [P, NT, D])
    t.BN = sb("bn", [P, NT, 6])
    t.MEAN = sb("mean", [P, NT])
    t.RSTD = sb("rstd", [P, NT])
    t.ident = sb("ident", [P, P])
    t.ln_sems, t.ln_uses = Sems(nc, ctx, "ln", "var_ready root_ready"), 0
    t.mha_sems = Sems(nc, ctx, "mha", ATTENTION_SEMS)
    t.moe_sems = Sems(nc, ctx, "moe", EXPERT_SEMS)
    t.PS = ctx.enter_context(nc.psum_tensor("psum", [P, 8, 512], F32))
    t.XS1 = nc.dram_tensor("expert_in1", [TILES1 * P, D], F32).ap()
    t.XS2 = nc.dram_tensor("expert_in2", [TILES2 * P, D], F32).ap()


def build(nc, a, out, upto=99):
    t = NS()
    with ExitStack() as ctx:
        alloc_shared(nc, t, ctx)
        with ExitStack() as tok:
            t.w1 = tok.enter_context(nc.sbuf_tensor("w1", [NF, 2, NHID * NF], F32))
            t.b1 = tok.enter_context(nc.sbuf_tensor("b1", [NF, NHID], F32))
            t.w2 = tok.enter_context(nc.sbuf_tensor("w2", [NF, NHID, D], F32))
            t.b2 = tok.enter_context(nc.sbuf_tensor("b2", [P, D], F32))
            t.dft = tok.enter_context(nc.sbuf_tensor("dft", [HP, 2, 2, NF], F32))
            setup(nc, t, a, tok)
            tokenizer(nc, t, a)
        def attention_and_experts():
            with ExitStack() as sub:
                t.R = sub.enter_context(nc.sbuf_tensor("attended", [P, NT, D], F32))
                full_attention(nc, t, a, "l0mha")
                experts_layer(nc, t, a, "l0moe")

        steps = [lambda: windowed_attention(nc, t, a, ctx),
                 attention_and_experts,
                 lambda: full_attention(nc, t, a, "l1mha"),
                 lambda: bitlinear_ffn(nc, t, a),
                 lambda: state_space(nc, t, a),
                 lambda: experts_layer(nc, t, a, "l2moe"),
                 lambda: bilinear_attention(nc, t, a),
                 lambda: expert_choice(nc, t, a, out)]
        for step in steps[:upto]:
            step()
        if upto < len(steps):
            with nc.semaphore("dump") as dump, nc.Block() as block:
                @block.sync
                def _(sp):
                    sp.dma_start(out.rearrange("b (h p) c -> p (b h) c", p=P), t.H[:, :, :]).then_inc(dump, 16)
                    sp.wait_ge(dump, 16)


def head_columns(w):
    o = np.zeros((w.shape[0], 2, 4, 32), w.dtype)
    o[:, :, :, :HD] = w.reshape(w.shape[0], 2, 4, HD)
    return o.reshape(w.shape[0], 2, P)


def head_bias(b, one):
    o = np.zeros((2, 4, 32), b.dtype)
    o[:, :, :HD] = b.reshape(2, 4, HD)
    if one:
        o[:, :, HD] = 1
    return np.ascontiguousarray(o.reshape(2, P).T)


def on_all(row):
    return np.ascontiguousarray(np.broadcast_to(row, (P,) + row.shape))


def constants():
    n = np.arange(PATCH)
    f = np.arange(NF)
    w = 2 * np.pi * ((n[:, None] * f[None, :]) % PATCH) / PATCH
    sin = np.where((f[None, :] * 2) % PATCH == 0, 0.0, np.sin(w))
    dft = np.stack([np.cos(w), -sin], 1).reshape(2, HP, 2, NF).transpose(1, 0, 2, 3)
    c = {"c_ident": np.eye(P), "c_dft": dft}
    win = np.arange(WT) // WIN
    c["c_mask"] = np.where(win[:, None] == win[None, :], 0.0, NEG)
    cnt = np.zeros(L)
    for w_ in range(NW):
        cnt[w_ * HOP:w_ * HOP + WIN] += 1
    c["c_share"] = (1.0 / np.maximum(cnt, 1)).reshape(2, P).T
    c["c_before"] = np.triu(np.ones((P, P)), 1)
    c["c_order"] = np.broadcast_to((NE - np.arange(NE))[None, :, None], (P, NE, NT))
    c["c_chain"] = np.broadcast_to((np.arange(NT) > 0)[None, None, :], (P, NE, NT))
    q = np.sqrt(1 + 2 * np.arange(NSTATE))
    hippo = -(np.tril(q[:, None] * q[None, :]) - np.diag(np.arange(NSTATE)))
    c["c_hippo"] = np.stack([hippo, hippo.T], 1)
    c["c_hippo_inv_t"] = np.linalg.inv(hippo).T
    c["c_flip"] = np.eye(P)[::-1]
    return {k: np.ascontiguousarray(v, dtype=np.float32) for k, v in c.items()}


def arrays(i):
    a = dict(constants())
    a["x"] = i["x"]
    a["tok_w1"] = i["L0_tok_w1"].reshape(2, NF, NHID * NF).transpose(1, 0, 2)
    a["tok_b1"] = i["L0_tok_b1"].reshape(NHID, NF).T
    a["tok_w2"] = i["L0_tok_w2"].reshape(NHID, NF, D).transpose(1, 0, 2)
    a["tok_b2"] = on_all(i["L0_tok_b2"])
    w_in, b_in = i["L0_attn_w_in"], i["L0_attn_b_in"]
    a["win_gb"] = np.stack([i["L0_attn_ln_g"], i["L0_attn_ln_b"]], 1)

    def attention(name, wq, wk, wv, wo, bq, bk, bv, bo):
        a[name + "_wq"], a[name + "_wk"] = head_columns(wq), head_columns(wk)
        a[name + "_wvo"] = np.stack([wv, wo], 1)
        a[name + "_bqk"] = np.stack([head_bias(bq, False), head_bias(bk, True)], 1)
        a[name + "_bvo"] = on_all(np.stack([bv, bo]))

    attention("win", w_in[:D].T, w_in[D:2 * D].T, w_in[2 * D:].T, i["L0_attn_w_out"].T,
              b_in[:D], b_in[D:2 * D], b_in[2 * D:], i["L0_attn_b_out"])
    attention("l0mha", *(i["L0_ffn_" + n] for n in ("Wq", "Wk", "Wv", "Wo", "bq", "bk", "bv", "bo")))
    flat = [i["L1_attn_" + n].transpose(1, 0, 2).reshape(D, D) for n in ("Wq", "Wk", "Wv")]
    attention("l1mha", *flat, i["L1_attn_Wo"], *(i["L1_attn_" + n].reshape(D) for n in ("bq", "bk", "bv")),
              i["L1_attn_bo"])

    def moe(name, g, b, gate_w, gate_b, w1, b1, w2, b2):
        a[name + "_gb"] = np.stack([g, b], 1)
        a[name + "_gate_w"] = gate_w
        a[name + "_gate_b"] = on_all(gate_b)
        a[name + "_w1"] = np.concatenate(
            [w1.transpose(1, 0, 2), b1.reshape(NE, KF, P).transpose(2, 0, 1)], 2)
        a[name + "_w2"] = w2.reshape(NE, KF, P, D).transpose(2, 0, 1, 3)
        a[name + "_b2"] = on_all(b2)

    moe("l0moe", i["L0_ffn_ln1_g"], i["L0_ffn_ln1_b"], i["L0_ffn_gate_W"], i["L0_ffn_gate_b"],
        i["L0_ffn_W1"], i["L0_ffn_b1"], i["L0_ffn_W2"], i["L0_ffn_b2"])
    moe("l2moe", i["L2_ffn_ln_g"], i["L2_ffn_ln_b"], i["L2_ffn_w_r"].T, i["L2_ffn_b_r"],
        i["L2_ffn_W1"], i["L2_ffn_b1"], i["L2_ffn_W2"], i["L2_ffn_b2"])
    a["l0moe_gb"] = on_all(np.stack([i["L0_ffn_ln1_g"], i["L0_ffn_ln1_b"]]))
    a["l2moe_gb"] = on_all(np.stack([i["L2_ffn_ln_g"], i["L2_ffn_ln_b"]]))
    a["bit_up"] = i["L1_ffn_w_up"].T
    a["bit_down"] = i["L1_ffn_w_down"].T.reshape(KF, P, D).transpose(1, 0, 2)
    a["ssm_bc"] = np.stack([i["L2_attn_B_ssm"][:, 0], i["L2_attn_C_ssm"][0]], 1)
    a["ssm_d"] = on_all(i["L2_attn_D_skip"])
    a["ssm_log_dt"] = on_all(i["L2_attn_log_dt"])[:NSTATE]
    a["bil_q"] = i["L3_attn_Q"].transpose(1, 0, 2)
    a["bil_v"] = i["L3_attn_V"].transpose(1, 0, 2).reshape(D, D)
    a["ec_wr"] = i["L3_ffn_W_router"]
    a["ec_br"] = on_all(i["L3_ffn_b_router"])
    a["ec_up"] = i["L3_ffn_W_up"]
    pad = np.zeros((EC // ECG, 3 * P), np.float32)
    pad[:, :ECF] = i["L3_ffn_b_up"]
    a["ec_bup"] = pad.reshape(EC // ECG, 3, P).transpose(2, 0, 1)
    a["ec_down"] = i["L3_ffn_W_down"]
    a["ec_bdown"] = on_all(i["L3_ffn_b_down"])
    return {k: np.ascontiguousarray(v) for k, v in a.items()}


TILES1 = 40
TILES2 = 72


def kernel(**inputs):
    import concourse.bacc as bacc
    from concourse.bass_utils import run_bass_kernel_spmd

    given = arrays({k: np.asarray(v) for k, v in inputs.items()})
    nc = bacc.Bacc("TRN2", target_bir_lowering=False, num_devices=1)
    aps = {k: nc.dram_tensor(f"in_{k}", v.shape, mybir.dt.from_np(v.dtype), kind="ExternalInput").ap()
           for k, v in given.items()}
    out = nc.dram_tensor("out_0", (NB, L, D), F32, kind="ExternalOutput").ap()
    build(nc, aps, out)
    r = run_bass_kernel_spmd(nc, [{f"in_{k}": v for k, v in given.items()}], core_ids=[0])
    return r.results[0]["out_0"]
```

```python
from contextlib import ExitStack

import numpy as np
import concourse.bass as bass
from concourse import mybir
from concourse.alu_op_type import AluOpType as ALU

F32 = mybir.dt.float32
BF16 = mybir.dt.bfloat16
U32 = mybir.dt.uint32
I32 = mybir.dt.int32
ACT = mybir.ActivationFunctionType
AX = mybir.AxisListType

P = 128
NB = 16
L = 256
D = 128
NT = NB * L // P
NH, HD = 8, 16
HV = HD + 1
PATCH, NPATCH, HP = 200, 4, 100
NF = PATCH // 2 + 1
NHID = 8
WIN, HOP = 20, 10
NW = (L - WIN) // HOP + 1
WT = 120
EPS = 1e-5
NE, FF = 8, 512
KF = FF // P
EC, ECF = 32, 341
ECK = NB * L // EC
ECG = 4
ECT = [(0, 128), (128, 128), (256, 85)]
NSTATE = 64
SQUARINGS = 12
MAGIC = 1.5 * 2.0 ** 23
NEG = -1e30
TINY = 1e-37


class NS:
    pass


def window_offset(w):
    return HOP * (w // 2) + WT * (w % 2)


class Sems:

    def __init__(self, nc, ctx, phase, names):
        self.s = {n: ctx.enter_context(nc.semaphore(f"{phase}_{n}")) for n in names.split()}

    def __getitem__(self, name):
        return self.s[name]

    def restart(self, nc):
        with nc.Block() as block:

            @block.gpsimd
            def _(pool):
                for sem in self.s.values():
                    pool.sem_clear(sem)


def ln_scales(nc, t, phase):
    with ExitStack() as ctx:
        s, n = t.ln_sems, t.ln_uses + 1
        t.ln_uses = n
        tmp = ctx.enter_context(nc.sbuf_tensor(f"{phase}_tmp", [P, 4, NT], F32))
        with nc.Block() as block:

            @block.vector
            def _(dve):
                me, mo = t.BN[:, :, 1], t.BN[:, :, 4]
                ve, vo = t.BN[:, :, 2], t.BN[:, :, 5]
                dve.tensor_tensor(tmp[:, 0], me, mo, ALU.subtract)
                dve.tensor_tensor(tmp[:, 1], ve, vo, ALU.add)
                dve.tensor_tensor(t.MEAN[:, :], me, mo, ALU.add)
                dve.drain()
                dve.tensor_tensor(tmp[:, 0], tmp[:, 0], tmp[:, 0], ALU.mult)
                dve.tensor_scalar(tmp[:, 1], tmp[:, 1], 1.0 / D, EPS, ALU.mult, ALU.add)
                dve.tensor_scalar(t.MEAN[:, :], t.MEAN[:, :], 0.5, None, ALU.mult)
                dve.drain()
                dve.scalar_tensor_tensor(tmp[:, 2], tmp[:, 0], 0.25, tmp[:, 1], ALU.mult, ALU.add)\
                   .then_inc(s["var_ready"], 1)
                dve.wait_ge(s["root_ready"], n)
                dve.reciprocal(t.RSTD[:, :], tmp[:, 3])
                dve.drain()
                dve.tensor_tensor(tmp[:, 0], t.RSTD[:, :], t.RSTD[:, :], ALU.mult)
                dve.drain()
                dve.tensor_tensor(tmp[:, 0], tmp[:, 0], tmp[:, 2], ALU.mult)
                dve.drain()
                dve.tensor_scalar(tmp[:, 0], tmp[:, 0], -0.5, 1.5, ALU.mult, ALU.add)
                dve.drain()
                dve.tensor_tensor(t.RSTD[:, :], t.RSTD[:, :], tmp[:, 0], ALU.mult)

            @block.scalar
            def _(act):
                act.wait_ge(s["var_ready"], n)
                act.activation(tmp[:, 3], tmp[:, 2], ACT.Sqrt).then_inc(s["root_ready"], 1)


def setup(nc, t, a, ctx):
    s = Sems(nc, ctx, "setup", "loaded zeroed scratch_zeroed")
    zero = ctx.enter_context(nc.sbuf_tensor("zero_tile", [P, 2048], F32))
    loads = [(t.ident, a["c_ident"]), (t.w1, a["tok_w1"]), (t.b1, a["tok_b1"]), (t.w2, a["tok_w2"]),
             (t.b2, a["tok_b2"]), (t.dft, a["c_dft"])]
    with nc.Block() as block:

        @block.sync
        def _(sp):
            for dst, src in loads:
                sp.dma_start(dst[tuple(slice(None) for _ in dst.shape)], src).then_inc(s["loaded"], 16)
            sp.wait_ge(s["loaded"], 16 * len(loads))

        @block.vector
        def _(dve):
            dve.memset(zero[:, :], 0.0).then_inc(s["zeroed"], 1)
            dve.wait_ge(s["loaded"], 16 * len(loads))
            dve.tensor_copy(t.ident16[:, :], t.ident[:, :])

        @block.scalar
        def _(act):
            act.wait_ge(s["zeroed"], 1)
            n = 0
            for buf in (t.XS1, t.XS2):
                rows = buf.rearrange("(p r) c -> p (r c)", p=P)
                for c in range(0, rows.shape[1], 2048):
                    m = min(2048, rows.shape[1] - c)
                    act.dma_start(rows[:, c:c + m], zero[:, 0:m]).then_inc(s["scratch_zeroed"], 16)
                    n += 16
            t.scratch_zeroed = s["scratch_zeroed"], n


def tokenizer(nc, t, a):
    N = 2 * L
    with ExitStack() as ctx:
        def sb(name, shape, dt=F32):
            return ctx.enter_context(nc.sbuf_tensor(f"tok_{name}", shape, dt))

        s = Sems(nc, ctx, "tok", "w1_doubled padded loaded0 loaded1 tr xt dft squares sum mag ratio atan feat "
                                 "hid_ps hid out_ps stored")
        rows = [sb(f"rows{i}", [P, 2 * NPATCH * HP]) for i in range(2)]
        xt = [sb(f"xt{i}", [HP, 2, P, NPATCH]) for i in range(2)]
        feat = [sb(f"feat{i}", [NF, 2, N]) for i in range(2)]
        sq = [sb(f"sq{i}", [NF, 2, N]) for i in range(2)]
        den = [sb(f"den{i}", [NF, N]) for i in range(2)]
        rat = [sb(f"rat{i}", [NF, N]) for i in range(2)]
        at = [sb(f"at{i}", [NF, N]) for i in range(2)]
        hid = [sb(f"hid{i}", [NF, NHID, N]) for i in range(2)]
        T = a["x"].shape[2]
        x_rows = a["x"].rearrange("b c t -> (b c) t")
        PS = t.PS

        STEPS = NB // 2

        def each_step(eng, first, body, last):
            first()
            for i in range(2):
                body(i, 0, i)
            with eng.Fori(1, STEPS // 2 - 1) as k:
                for p in range(2):
                    body(k * 2 + p, k, p)
            for i in range(STEPS - 2, STEPS):
                body(i, i // 2, i % 2)
            last()

        def there(i):
            return not isinstance(i, int) or 0 <= i < STEPS

        with nc.Block() as block:

            @block.sync
            def _(sp):
                def load(i, k, p):
                    if there(i - 2):
                        sp.wait_ge(s["tr"], i - 1)
                    sp.dma_start(rows[p][:, 0:T], x_rows[bass.ds(i * P, P), :]).then_inc(s[f"loaded{p}"], 16)

                each_step(sp, lambda: sp.wait_ge(s["padded"], 2), load, lambda: None)

            @block.tensor
            def _(pe):
                def turn(i, k, p):
                    pe.wait_ge(s[f"loaded{p}"], k * 16 + 16)
                    for j in range(2 * NPATCH):
                        mm = pe.transpose(PS[0:HP, j % 2, (j // 2) * P:(j // 2 + 1) * P],
                                          rows[p][:, j * HP:(j + 1) * HP], t.ident[:, :])
                    mm.then_inc(s["tr"], 1)

                def spectrum(i, p):
                    pe.wait_ge(s["xt"], i + 1)
                    if there(i - 1):
                        pe.wait_ge(s["feat"], i)
                    for part in range(2):
                        for half in range(2):
                            mm = pe.matmul(PS[0:NF, 2 + part, :], t.dft[:, half, part, :],
                                           xt[p][:, half].rearrange("h q s -> h (q s)"),
                                           start=(half == 0), stop=(half == 1))
                    mm.then_inc(s["dft"], 1)

                def up(i, p, m):
                    if m == 0:
                        pe.wait_ge(s["feat"], i + 1)
                    if m >= 2 or there(i - 1):
                        pe.wait_ge(s["hid"], i * NHID + m - 1)
                    for f in range(2):
                        mm = pe.matmul(PS[0:NF, 4 + m % 2, :], t.w1[:, f, m * NF:(m + 1) * NF],
                                       feat[p][:, f, :], start=(f == 0), stop=(f == 1))
                    mm.then_inc(s["hid_ps"], 1)

                def down(i, p):
                    pe.wait_ge(s["hid"], i * NHID + NHID)
                    if there(i - 2):
                        pe.wait_ge(s["stored"], i - 1)
                    for q in range(4):
                        for m in range(NHID):
                            mm = pe.matmul(PS[:, 6 + p, q * D:(q + 1) * D],
                                           hid[p][:, m, q * P:(q + 1) * P], t.w2[:, m, :],
                                           start=(m == 0), stop=(m == NHID - 1))
                    mm.then_inc(s["out_ps"], 1)

                def start():
                    pe.wait_ge(s["w1_doubled"], 1)
                    turn(0, 0, 0)
                    spectrum(0, 0)

                def body(i, k, p):
                    if there(i + 1):
                        turn(i + 1, k + p, 1 - p)
                    for m in range(NHID):
                        up(i, p, m)
                        if m == 1:
                            if there(i + 1):
                                spectrum(i + 1, 1 - p)
                            if there(i - 1):
                                down(i - 1, 1 - p)

                each_step(pe, start, body, lambda: down(STEPS - 1, 1))

            @block.scalar
            def _(act):
                def magnitude(i, p):
                    act.wait_ge(s["dft"], i + 1)
                    act.activation(den[p][:, :], PS[0:NF, 2, :], ACT.Abs)
                    act.activation(sq[p][:, 0], PS[0:NF, 2, :], ACT.Square)
                    act.activation(sq[p][:, 1], PS[0:NF, 3, :], ACT.Square).then_inc(s["squares"], 1)
                    act.wait_ge(s["sum"], i + 1)
                    act.activation(feat[p][:, 0], sq[p][:, 0], ACT.Sqrt).then_inc(s["mag"], 1)

                def angle(i, p):
                    act.wait_ge(s["ratio"], i + 1)
                    act.activation(at[p][:, :], rat[p][:, :], ACT.Arctan).then_inc(s["atan"], 1)

                def start():
                    magnitude(0, 0)
                    angle(0, 0)

                def body(i, k, p):
                    for m in range(NHID):
                        act.wait_ge(s["hid_ps"], i * NHID + m + 1)
                        act.activation(hid[p][:, m], PS[0:NF, 4 + m % 2, :], ACT.Gelu,
                                       bias=t.b1[:, m:m + 1]).then_inc(s["hid"], 1)
                        if m == 1 and there(i + 1):
                            magnitude(i + 1, 1 - p)
                        if m == 3 and there(i + 1):
                            angle(i + 1, 1 - p)

                each_step(act, start, body, lambda: act.wait_ge(*t.scratch_zeroed))

            @block.vector
            def _(dve):
                re, im = PS[0:NF, 2, :], PS[0:NF, 3, :]

                def ratio(i, p):
                    dve.wait_ge(s["tr"], i + 1)
                    for half in range(2):
                        c = dve.tensor_copy(xt[p][:, half].rearrange("h q s -> h s q"),
                                            PS[0:HP, half, :].rearrange("h (s q) -> h s q", s=NPATCH))
                    c.then_inc(s["xt"], 1)
                    dve.wait_ge(s["squares"], i + 1)
                    dve.tensor_tensor(sq[p][:, 0], sq[p][:, 0], sq[p][:, 1], ALU.add).then_inc(s["sum"], 1)
                    dve.wait_ge(s["mag"], i + 1)
                    dve.tensor_tensor(den[p][:, :], den[p][:, :], feat[p][:, 0], ALU.add)
                    dve.drain()
                    dve.tensor_scalar(den[p][:, :], den[p][:, :], TINY, None, ALU.max)
                    dve.drain()
                    dve.reciprocal(den[p][:, :], den[p][:, :])
                    dve.drain()
                    dve.tensor_tensor(rat[p][:, :], im, den[p][:, :], ALU.mult).then_inc(s["ratio"], 1)
                    dve.tensor_scalar(sq[p][:, 1], im, 0.0, -0.5, ALU.is_ge, ALU.add)
                    dve.drain()

                def angle(i, p):
                    dve.wait_ge(s["atan"], i + 1)
                    dve.scalar_tensor_tensor(sq[p][:, 0], at[p][:, :], -2.0 / np.pi, sq[p][:, 1],
                                             ALU.mult, ALU.add)
                    dve.drain()
                    dve.scalar_tensor_tensor(sq[p][:, 1], re, 0.0, sq[p][:, 0], ALU.is_lt, ALU.mult)
                    dve.drain()
                    dve.scalar_tensor_tensor(feat[p][:, 1], sq[p][:, 1], float(np.pi), at[p][:, :],
                                             ALU.mult, ALU.add).then_inc(s["feat"], 1)

                def store(i, p):
                    dve.wait_ge(s["out_ps"], i + 1)
                    dve.tensor_tensor(t.H[:, bass.ds(i * 4, 4), :],
                                      PS[:, 6 + p, :].rearrange("p (q c) -> p q c", q=4),
                                      t.b2[:, :].unsqueeze(1).broadcast_to([P, 4, D]), ALU.add)\
                       .then_inc(s["stored"], 1)
                    dve.drain()
                    for q in range(4):
                        dve.bn_stats(t.BN[:, i * 4 + q, :], t.H[:, i * 4 + q, :])

                def start():
                    for p in range(2):
                        dve.memset(rows[p][:, T:], 0.0).then_inc(s["padded"], 1)
                    dve.tensor_scalar(t.w1[:, 1, :], t.w1[:, 1, :], 2.0, None, ALU.mult)\
                       .then_inc(s["w1_doubled"], 1)
                    ratio(0, 0)
                    angle(0, 0)

                def body(i, k, p):
                    if there(i + 1):
                        ratio(i + 1, 1 - p)
                        angle(i + 1, 1 - p)
                    if there(i - 1):
                        store(i - 1, 1 - p)

                each_step(dve, start, body, lambda: store(STEPS - 1, 1))


def second_norm(nc, t):
    with nc.Block() as block:

        @block.vector
        def _(dve):
            with dve.Fori(0, NT // 2) as k:
                for p in range(2):
                    i = k * 2 + p
                    dve.tensor_scalar(t.U[:, i, :], t.H[:, i, :], t.MEAN[:, bass.ds(i, 1)],
                                      t.RSTD[:, bass.ds(i, 1)], ALU.subtract, ALU.mult)
                dve.drain()
                for p in range(2):
                    dve.bn_stats(t.BN[:, k * 2 + p, :], t.U[:, k * 2 + p, :])


def load_all(block, pairs, sem):
    @block.sync
    def _(sp):
        for dst, src in pairs:
            sp.dma_start(dst[tuple(slice(None) for _ in dst.shape)], src).then_inc(sem, 16)
        sp.wait_ge(sem, 16 * len(pairs))


def attention_weights(nc, ctx, a, name):
    w = NS()

    def sb(n, shape):
        return ctx.enter_context(nc.sbuf_tensor(f"{name}_{n}", shape, F32))

    w.wqk, w.wvo = sb("wqk", [P, 2, P]), sb("wvo", [P, 2, D])
    w.bqk, w.bvo = sb("bqk", [P, 2]), sb("bvo", [P, 2, D])
    w.loads = [(w.wqk, a[name + "_wqk"]), (w.wvo, a[name + "_wvo"]),
               (w.bqk, a[name + "_bqk"]), (w.bvo, a[name + "_bvo"])]
    return w


def attention_prelude(nc, t, s, nms, zero, values, loads):
    with nc.Block() as block:
        load_all(block, loads, s["weights"])

        @block.vector
        def _(dve):
            if nms is not None:
                dve.memset(nms[tuple(slice(None) for _ in nms.shape)], 0.0)
                dve.memset(zero[:, :], 0.0)
            for p in range(2):
                dve.memset(values[p][:, :, :, HD:HV], 1.0)


QUERY_PARTS = (0, 0, 1, 1, 0, 2)
KEY_PARTS = (0, 1, 0, 1, 2, 0)
STACK = 6 * HD
STACK_DMAS = 2 * 6 * 16


ATTENTION_SEMS = ("weights made u tr ut qk_ps qk parts base stacks0 stacks1 v_ps v st_ps mx nms nt_ps mt "
                  "stt_ps exp av_ps norm ot_ps ot out_ps")


def each_batch(eng, first, body, last):
    first()
    for b in range(2):
        body(b, 0, b)
    with eng.Fori(1, NB // 2 - 2) as k:
        for p in range(2):
            body(k * 2 + p, k, p)
    for b in range(NB - 4, NB):
        body(b, b // 2, b % 2)
    last()


def exists(b):
    return not isinstance(b, int) or 0 <= b < NB


def windowed_attention(nc, t, a, ctx):
    ln_scales(nc, t, "ln_a")
    with ExitStack() as sub:
        def sb(name, shape, dt=F32):
            return sub.enter_context(nc.sbuf_tensor(f"win_{name}", shape, dt))

        t.U = sb("u", [P, NT, D])
        second_norm(nc, t)
        ln_scales(nc, t, "ln_b")
        SEG = nc.dram_tensor("window_out", [NB * NW * WIN, D], F32).ap()
        with ExitStack() as loop:
            def lb(name, shape, dt=F32):
                return loop.enter_context(nc.sbuf_tensor(f"win_{name}", shape, dt))

            s = Sems(nc, loop, "win", ATTENTION_SEMS + " stored sent0 sent1")
            w = attention_weights(nc, loop, a, "win")
            two = range(2)
            gb, cover = lb("gb", [P, 2]), lb("cover", [P, 2])
            us, own = [lb(f"us{i}", [P, 2, D]) for i in two], [lb(f"own{i}", [P, L]) for i in two]
            ut, qk = [lb(f"ut{i}", [P, L]) for i in two], [lb(f"qk{i}", [P, 2, L]) for i in two]
            parts, rest = [lb(f"parts{i}", [P, 3, 2, L], BF16) for i in two], lb("rest", [P, 2, L])
            qs = [lb(f"qs{i}", [STACK, NH, L], BF16) for i in two]
            ks = [lb(f"ks{i}", [STACK, NH, L], BF16) for i in two]
            v = [lb(f"v{i}", [WT, 4, NH, HV]) for i in two]
            nm, nmrest, nms = lb("nm", [WT, 4, NH]), lb("nmrest", [WT, 4, NH]), lb("nms", [WT, 4, P], BF16)
            zero = lb("zero", [P, 1])
            mt, blocks, blocksf = lb("mt", [P, 4, WT], BF16), lb("blocks", [P, 4, WT], BF16), lb("blocksf", [P, WT])
            pt = lb("pt", [WT, NH, 4, WT])
            rc, oc, ot = lb("rc", [WT, 4, NH]), lb("oc", [WT, 4, NH, HD]), lb("ot", [P, 4, WT])
            sg = [lb(f"sg{i}", [WT, 4, D]) for i in two]
            self_, sel = lb("self", [P, NH + 1, WT]), lb("sel", [P, NH + 1, WT], BF16)
            attention_prelude(nc, t, s, nms, zero, v, w.loads + [(gb, a["win_gb"]),
                                                           (cover, a["c_cover"]), (self_, a["c_win_sel"]),
                                                           (blocksf, a["c_blocks"])])
            PS = t.PS

            with nc.Block() as block:

                @block.tensor
                def _(pe):
                    def transpose_tokens(b, p):
                        pe.wait_ge(s["u"], b + 1)
                        if exists(b - 2):
                            pe.wait_ge(s["v"], b - 1)
                        for h in range(2):
                            mm = pe.transpose(PS[:, 4 + p, h * P:(h + 1) * P], us[p][:, h, :], t.ident[:, :])
                        mm.then_inc(s["tr"], 1)

                    def project_queries_keys(b, p):
                        pe.wait_ge(s["ut"], b + 1)
                        for g in range(2):
                            mm = pe.matmul(PS[:, 4 + p, g * L:(g + 1) * L], w.wqk[:, g, :], ut[p][:, :],
                                           start=True, stop=True)
                        mm.then_inc(s["qk_ps"], 1)

                    def project_values(b, p):
                        pe.wait_ge(s["qk"], b + 1)
                        for j in range(4):
                            o = window_offset(j)
                            mm = pe.matmul(PS[0:WT, 4 + p, j * D:(j + 1) * D], ut[p][:, o:o + WT],
                                           w.wvo[:, 0, :], start=True, stop=True)
                        mm.then_inc(s["v_ps"], 1)

                    def scores(n, row, shift, stationary, moving):
                        for h in range(2):
                            bank = 2 * (n % 2) + h
                            pe.matmul(PS[0:WT, bank, 0:4 * WT], sel[:, row(2 * n + h), :],
                                      shift[:, :, :].rearrange("p j c -> p (j c)"), start=True, stop=False)
                            for j in range(4):
                                o = window_offset(j)
                                mm = pe.matmul(PS[0:WT, bank, j * WT:(j + 1) * WT],
                                               stationary[:, 2 * n + h, o:o + WT],
                                               moving[:, 2 * n + h, o:o + WT], start=False, stop=(j == 3))
                        return mm

                    def row_scores(b, p, n):
                        if n < 2:
                            pe.wait_ge(s["exp"], b * 4 + 3 + n)
                        else:
                            pe.wait_ge(s["mx"], b * 4 + n - 1)
                        scores(n, lambda h: NH, blocks, qs[p], ks[p]).then_inc(s["st_ps"], 1)

                    def column_scores(b, p, n):
                        if n < 2:
                            pe.wait_ge(s["mx"], b * 4 + 3 + n)
                        else:
                            pe.wait_ge(s["exp"], b * 4 + 3 + n)
                        scores(n, lambda h: h, mt, ks[p], qs[p]).then_inc(s["stt_ps"], 1)

                    def sum_values(b, p, half):
                        pe.wait_ge(s["exp"], b * 4 + 8)
                        pe.wait_ge(s["v"], b + 1)
                        if exists(b - 1):
                            pe.wait_ge(s["stored"], b)
                        for j in range(2 * half, 2 * half + 2):
                            for h in range(NH):
                                o = (j % 2) * NH * HV + h * HV
                                mm = pe.matmul(PS[0:WT, 6 + half, o:o + HV], pt[:, h, j, :], v[p][:, j, h, :],
                                               start=True, stop=True)
                        mm.then_inc(s["av_ps"], 1)

                    def transpose_sums(b):
                        pe.wait_ge(s["norm"], b + 1)
                        for j in range(4):
                            mm = pe.transpose(PS[:, 6, j * WT:(j + 1) * WT],
                                              oc[:, j].rearrange("q h d -> q (h d)"), t.ident[0:WT, 0:WT])
                        mm.then_inc(s["ot_ps"], 1)

                    def project_output(b, p):
                        pe.wait_ge(s["ot"], b + 1)
                        for j in range(4):
                            o = window_offset(j)
                            pe.matmul(PS[0:WT, 7, j * D:(j + 1) * D], ot[:, j, :], w.wvo[:, 1, :],
                                      start=True, stop=False)
                            mm = pe.matmul(PS[0:WT, 7, j * D:(j + 1) * D], own[p][:, o:o + WT], t.ident[:, :],
                                           start=False, stop=True)
                        mm.then_inc(s["out_ps"], 1)

                    def transpose_maxima(b, p):
                        pe.wait_ge(s["nms"], b + 1)
                        if exists(b + 1):
                            pe.wait_ge(s["qk"], b + 2)
                        for j in range(4):
                            mm = pe.transpose(PS[:, 5 - p, j * (WT // 2):(j + 1) * (WT // 2)].bitcast(BF16),
                                              nms[:, j, :], t.ident16[0:WT, 0:WT])
                        mm.then_inc(s["nt_ps"], 1)

                    def start():
                        pe.wait_ge(s["made"], 1)
                        for b in range(2):
                            transpose_tokens(b, b)
                            project_queries_keys(b, b)
                        project_values(0, 0)

                    def body(b, k, p):
                        pe.wait_ge(s[f"stacks{p}"], k * STACK_DMAS + STACK_DMAS)
                        for n in range(2):
                            row_scores(b, p, n)
                        if exists(b + 2):
                            transpose_tokens(b + 2, p)
                        if exists(b - 1):
                            sum_values(b - 1, 1 - p, 0)
                        for n in range(2, 4):
                            row_scores(b, p, n)
                        if exists(b - 1):
                            sum_values(b - 1, 1 - p, 1)
                        transpose_maxima(b, p)
                        if exists(b + 2):
                            project_queries_keys(b + 2, p)
                        if exists(b - 1):
                            transpose_sums(b - 1)
                        pe.wait_ge(s["mt"], b + 1)
                        if exists(b + 1):
                            project_values(b + 1, 1 - p)
                        if exists(b - 1):
                            project_output(b - 1, 1 - p)
                        for n in range(4):
                            column_scores(b, p, n)

                    def end():
                        for half in range(2):
                            sum_values(NB - 1, 1, half)
                        transpose_sums(NB - 1)
                        project_output(NB - 1, 1)

                    each_batch(pe, start, body, end)

                @block.scalar
                def _(act):
                    def tokens(b, p):
                        act.wait_ge(s["tr"], b + 1)
                        act.activation(ut[p][:, :], PS[:, 4 + p, 0:L], ACT.Identity, scale=gb[:, 0:1],
                                       bias=gb[:, 1:2]).then_inc(s["ut"], 1)

                    def queries_keys(b, p):
                        act.wait_ge(s["qk_ps"], b + 1)
                        for g in range(2):
                            i = act.activation(qk[p][:, g, :], PS[:, 4 + p, g * L:(g + 1) * L],
                                               ACT.Identity, bias=w.bqk[:, g:g + 1])
                        i.then_inc(s["qk"], 1)

                    def sums(b):
                        act.wait_ge(s["ot_ps"], b + 1)
                        act.activation(ot[:, :, :].rearrange("p j c -> p (j c)"),
                                       PS[:, 6, 0:4 * WT], ACT.Copy).then_inc(s["ot"], 1)

                    def rows_out(b, p, k):
                        act.wait_ge(s["out_ps"], b + 1)
                        if exists(b - 2):
                            act.wait_ge(s[f"sent{p}"], k * 64)
                        act.activation(sg[p][:, :, :].rearrange("q j c -> q (j c)"),
                                       PS[0:WT, 7, :], ACT.Copy).then_inc(s["stored"], 1)

                    def start():
                        act.nop().then_inc(s["exp"], 4)
                        act.wait_ge(s["made"], 1)
                        for b in range(2):
                            tokens(b, b)
                            queries_keys(b, b)

                    def body(b, k, p):
                        act.activation(own[p][:, :], ut[p][:, :], ACT.Copy)
                        act.drain()
                        if exists(b + 2):
                            tokens(b + 2, p)
                        act.wait_ge(s["nt_ps"], b + 1)
                        act.activation(mt[0:32, :, :].rearrange("p j c -> p (j c)"),
                                       PS[0:32, 5 - p, 0:2 * WT].bitcast(BF16), ACT.Copy).then_inc(s["mt"], 1)
                        if exists(b + 2):
                            queries_keys(b + 2, p)
                        if exists(b - 1):
                            sums(b - 1)
                        for n in range(4):
                            if n == 1 and exists(b - 1):
                                rows_out(b - 1, 1 - p, k - 1 if p == 0 else k)
                            act.wait_ge(s["stt_ps"], b * 4 + n + 1)
                            bank = 2 * (n % 2)
                            act.activation(pt[:, 2 * n:2 * n + 2].rearrange("q h j c -> q h (j c)"),
                                           PS[0:WT, bank:bank + 2, 0:4 * WT], ACT.Exp, scale=HD ** -0.5)\
                               .then_inc(s["exp"], 1)

                    def end():
                        sums(NB - 1)
                        rows_out(NB - 1, 1, NB // 2 - 1)

                    each_batch(act, start, body, end)

                @block.gpsimd
                def _(pool):
                    zeros = zero[:, :].unsqueeze(2).broadcast_to([P, 2, L])

                    def cut(b, p):
                        pool.wait_ge(s["qk"], b + 1)
                        pool.tensor_tensor(parts[p][:, 0], qk[p][:, :, :], zeros, ALU.add)
                        pool.drain()
                        pool.tensor_tensor(rest[:, :, :], qk[p][:, :, :], parts[p][:, 0], ALU.subtract)
                        pool.drain()
                        pool.tensor_tensor(parts[p][:, 1], rest[:, :, :], zeros, ALU.add)
                        pool.drain()
                        pool.tensor_tensor(parts[p][:, 2], rest[:, :, :], parts[p][:, 1], ALU.subtract)\
                            .then_inc(s["parts"], 1)

                    def start():
                        for b in range(2):
                            cut(b, b)

                    def body(b, k, p):
                        if exists(b + 2):
                            cut(b + 2, p)

                    each_batch(pool, start, body, lambda: None)

                @block.sync
                def _(sp):
                    def stack(b, p):
                        sp.wait_ge(s["parts"], b + 1)
                        if exists(b - 2):
                            sp.wait_ge(s["stt_ps"], b * 4 - 4)
                        for g in range(6):
                            rows = slice(g * HD, (g + 1) * HD)
                            sp.dma_start(qs[p][rows, :, :], parts[p][:, QUERY_PARTS[g], 0, :])\
                              .then_inc(s[f"stacks{p}"], 16)
                            sp.dma_start(ks[p][rows, :, :], parts[p][:, KEY_PARTS[g], 1, :])\
                              .then_inc(s[f"stacks{p}"], 16)

                    def store(b, p):
                        sp.wait_ge(s["stored"], b + 1)
                        for j in range(4):
                            base = b * (NW * WIN) + (j % 2) * 2 * WT
                            rows = SEG[bass.ds(base, 2 * WT), :].rearrange(
                                "(i o w) c -> o i w c", o=2, w=WIN)[j // 2]
                            sp.dma_start(rows, sg[p][:, j, :]).then_inc(s[f"sent{p}"], 16)

                    def body(b, k, p):
                        if exists(b + 1):
                            stack(b + 1, 1 - p)
                        if exists(b - 1):
                            store(b - 1, 1 - p)

                    def end():
                        store(NB - 1, 1)
                        for p in range(2):
                            sp.wait_ge(s[f"sent{p}"], 64 * NB // 2)

                    each_batch(sp, lambda: stack(0, 0), body, end)

                @block.vector
                def _(dve):
                    def normalize(b, p):
                        for h in range(2):
                            i = b * 2 + h
                            u = dve.tensor_scalar(us[p][:, h, :], t.U[:, i, :], t.MEAN[:, bass.ds(i, 1)],
                                                  t.RSTD[:, bass.ds(i, 1)], ALU.subtract, ALU.mult)
                        u.then_inc(s["u"], 1)
                        for h in range(2):
                            x = t.H[:, b * 2 + h, :]
                            dve.scalar_tensor_tensor(x, w.bvo[:, 1, :], cover[:, h:h + 1], x, ALU.mult, ALU.add)

                    def values(b, p):
                        dve.wait_ge(s["v_ps"], b + 1)
                        i = dve.tensor_tensor(
                            v[p][:, :, :, 0:HD],
                            PS[0:WT, 4 + p, :].rearrange("q (j h d) -> q j h d", j=4, h=NH),
                            w.bvo[0:WT, 0, :].rearrange("q (h d) -> q h d", h=NH).unsqueeze(1)
                             .broadcast_to([WT, 4, NH, HD]), ALU.add)
                        i.then_inc(s["v"], 1)

                    def maxima(b, n):
                        dve.wait_ge(s["st_ps"], b * 4 + n + 1)
                        bank = 2 * (n % 2)
                        dve.tensor_reduce(nm[:, :, 2 * n:2 * n + 2].rearrange("q j i -> q i j"),
                                          PS[0:WT, bank:bank + 2, 0:4 * WT].rearrange("q i (j c) -> q i j c", j=4),
                                          AX.X, ALU.max, negate=True).then_inc(s["mx"], 1)

                    def cut_maxima():
                        dve.drain()
                        dve.tensor_copy(nms[:, :, 0:NH], nm[:, :, :])
                        dve.drain()
                        dve.tensor_tensor(nmrest[:, :, :], nm[:, :, :], nms[:, :, 0:NH], ALU.subtract)
                        dve.drain()
                        dve.tensor_copy(nms[:, :, NH:2 * NH], nmrest[:, :, :])
                        dve.drain()
                        dve.tensor_tensor(nms[:, :, 2 * NH:3 * NH], nmrest[:, :, :], nms[:, :, NH:2 * NH],
                                          ALU.subtract).then_inc(s["nms"], 1)

                    def divide(b):
                        dve.wait_ge(s["av_ps"], b * 2 + 2)
                        for y in range(2):
                            av = PS[0:WT, 6 + y, 0:2 * NH * HV].rearrange("q (j h e) -> q j h e", j=2, h=NH)
                            dve.reciprocal(rc[:, 2 * y:2 * y + 2, :], av[:, :, :, HD])
                        dve.drain()
                        for y in range(2):
                            av = PS[0:WT, 6 + y, 0:2 * NH * HV].rearrange("q (j h e) -> q j h e", j=2, h=NH)
                            i = dve.tensor_tensor(oc[:, 2 * y:2 * y + 2], av[:, :, :, 0:HD],
                                                  rc[:, 2 * y:2 * y + 2, :].unsqueeze(3)
                                                  .broadcast_to([WT, 2, NH, HD]), ALU.mult)
                        i.then_inc(s["norm"], 1)

                    def start():
                        dve.tensor_copy(sel[:, :, :], self_[:, :, :])
                        for j in range(4):
                            dve.tensor_copy(blocks[:, j, :], blocksf[:, :])
                            dve.tensor_copy(mt[:, j, :], blocksf[:, :])
                        dve.drain()
                        dve.nop().then_inc(s["made"], 1)
                        for b in range(2):
                            normalize(b, b)
                        dve.wait_ge(s["tr"], 1)
                        normalize(2, 0)
                        values(0, 0)

                    def body(b, k, p):
                        for n in range(4):
                            maxima(b, n)
                        cut_maxima()
                        if exists(b - 1):
                            divide(b - 1)
                        if exists(b + 1):
                            values(b + 1, 1 - p)
                        if exists(b + 3):
                            normalize(b + 3, 1 - p)

                    each_batch(dve, start, body, lambda: divide(NB - 1))

        merge_windows(nc, t, a, sub, SEG)


def merge_windows(nc, t, a, ctx, SEG):
    first = ctx.enter_context(nc.sbuf_tensor("win_first", [P, NB, 2, D], F32))
    second = ctx.enter_context(nc.sbuf_tensor("win_second", [P, NB, 2, D], F32))
    share = ctx.enter_context(nc.sbuf_tensor("win_share", [P, 2], F32))
    s = Sems(nc, ctx, "merge", "cleared loaded")
    seg = SEG.rearrange("(s b w) c -> s w b c", b=NB, w=WIN)
    H4 = t.H[:, :, :].rearrange("p (b h) c -> p b h c", h=2)
    U4 = t.U[:, :, :].rearrange("p (b h) c -> p b h c", h=2)
    pieces = [(first, 0, 0, 0, 12, 0, 10), (first, 0, 120, 12, 13, 0, 8),
              (first, 1, 0, 12, 13, 8, 10), (first, 1, 2, 13, 24, 0, 10),
              (second, 0, 10, 0, 11, 10, 20), (second, 0, 120, 11, 12, 10, 18),
              (second, 1, 0, 11, 12, 18, 20), (second, 1, 2, 12, 24, 10, 20)]
    with nc.Block() as block:

        @block.gpsimd
        def _(pool):
            pool.memset(first[:, :, :, :], 0.0).then_inc(s["cleared"], 1)
            pool.memset(second[:, :, :, :], 0.0).then_inc(s["cleared"], 1)

        @block.sync
        def _(sp):
            sp.dma_start(share[:, :], a["c_share"]).then_inc(s["loaded"], 16)
            sp.wait_ge(s["cleared"], 2)
            n = 16
            for buf, h, p0, s0, s1, w0, w1 in pieces:
                rows = (s1 - s0) * (w1 - w0)
                for q in range(s0, s1):
                    r = p0 + (q - s0) * (w1 - w0)
                    sp.dma_start(buf[r:r + w1 - w0, :, h, :], seg[q, w0:w1]).then_inc(s["loaded"], 16)
                    n += 16
            sp.wait_ge(s["loaded"], n)

        @block.vector
        def _(dve):
            dve.tensor_tensor(t.H[:, :, :], t.H[:, :, :], t.U[:, :, :], ALU.add)
            dve.wait_ge(s["loaded"], 16 + 16 * sum(q[4] - q[3] for q in pieces))
            dve.tensor_tensor(first[:, :, :, :], first[:, :, :, :], second[:, :, :, :], ALU.add)
            dve.drain()
            for h in range(2):
                dve.scalar_tensor_tensor(H4[:, :, h, :], first[:, :, h, :], share[:, h:h + 1], H4[:, :, h, :],
                                         ALU.mult, ALU.add)
            dve.drain()
            with dve.Fori(0, NT) as i:
                dve.bn_stats(t.BN[:, i, :], t.H[:, i, :])


EXPERT_SEMS = ("weights w1 w2 b2 staged tr tt logits exp1 exp2 counts_in counts made "
               "xs0 xs1 picked xtr xt hid_ps pre hid out_ps res sent0 sent1")


def full_attention(nc, t, a, name):
    keep = name == "l0mha"
    ln_scales(nc, t, f"{name}_ln")
    with ExitStack() as ctx:
        def sb(n, shape, dt=F32):
            return ctx.enter_context(nc.sbuf_tensor(f"{name}_{n}", shape, dt))

        s = t.mha_sems
        if not keep:
            s.restart(nc)
        w = attention_weights(nc, ctx, a, name)
        two = range(2)
        us, ut = [sb(f"us{i}", [P, 2, D]) for i in two], [sb(f"ut{i}", [P, L]) for i in two]
        qk = [sb(f"qk{i}", [P, 2, L]) for i in two]
        parts = [sb(f"parts{i}", [P, 3, 2, L], BF16) for i in two]
        rest = sb("rest", [P, 2, L])
        qs = [sb(f"qs{i}", [STACK, NH, L], BF16) for i in two]
        ks = [sb(f"ks{i}", [STACK, NH, L], BF16) for i in two]
        v = [sb(f"v{i}", [P, 2, NH, HV]) for i in two]
        nm, nmrest, nms = sb("nm", [P, 2, NH]), sb("nmrest", [P, 2, NH]), sb("nms", [P, 2, P], BF16)
        mt, zero = sb("mt", [P, L], BF16), sb("zero", [P, 1])
        pt = sb("pt", [P, NH, 2, L])
        rc, oc, ot = sb("rc", [P, 2, NH]), sb("oc", [P, 2, NH, HD]), sb("ot", [P, L])
        self_, sel = sb("self", [P, NH, P]), sb("sel", [P, NH, P], BF16)
        attention_prelude(nc, t, s, nms, zero, v, w.loads + [(self_, a["c_sel"])])
        PS = t.PS

        with nc.Block() as block:

            @block.tensor
            def _(pe):
                def transpose_tokens(b, p):
                    pe.wait_ge(s["u"], b + 1)
                    if exists(b - 2):
                        pe.wait_ge(s["v"], b - 1)
                    for h in range(2):
                        mm = pe.transpose(PS[:, 4 + p, h * P:(h + 1) * P], us[p][:, h, :], t.ident[:, :])
                    mm.then_inc(s["tr"], 1)

                def project_queries_keys(b, p):
                    pe.wait_ge(s["ut"], b + 1)
                    for g in range(2):
                        mm = pe.matmul(PS[:, 4 + p, g * L:(g + 1) * L], w.wqk[:, g, :], ut[p][:, :],
                                       start=True, stop=True)
                    mm.then_inc(s["qk_ps"], 1)

                def project_values(b, p):
                    pe.wait_ge(s["qk"], b + 1)
                    for h in range(2):
                        mm = pe.matmul(PS[:, 4 + p, h * D:(h + 1) * D], ut[p][:, h * P:(h + 1) * P],
                                       w.wvo[:, 0, :], start=True, stop=True)
                    mm.then_inc(s["v_ps"], 1)

                def row_scores(b, p, n):
                    if n < 2:
                        pe.wait_ge(s["exp"], b * 4 + 3 + n)
                    else:
                        pe.wait_ge(s["mx"], b * 4 + n - 1)
                    for h in range(2):
                        for tile in range(2):
                            mm = pe.matmul(PS[:, 2 * (n % 2) + h, tile * L:(tile + 1) * L],
                                           qs[p][:, 2 * n + h, tile * P:(tile + 1) * P],
                                           ks[p][:, 2 * n + h, :], start=True, stop=True)
                    mm.then_inc(s["st_ps"], 1)

                def column_scores(b, p, n):
                    if n < 2:
                        pe.wait_ge(s["mx"], b * 4 + 3 + n)
                    else:
                        pe.wait_ge(s["exp"], b * 4 + 3 + n)
                    for h in range(2):
                        bank = 2 * (n % 2) + h
                        pe.matmul(PS[:, bank, :].rearrange("p (j c) -> p j c", j=2), sel[:, 2 * n + h, :],
                                  mt[:, :].unsqueeze(1).broadcast_to([P, 2, L]), start=True, stop=False)
                        for tile in range(2):
                            mm = pe.matmul(PS[:, bank, tile * L:(tile + 1) * L],
                                           ks[p][:, 2 * n + h, tile * P:(tile + 1) * P],
                                           qs[p][:, 2 * n + h, :], start=False, stop=(tile == 1))
                    mm.then_inc(s["stt_ps"], 1)

                def sum_values(b, p, q):
                    pe.wait_ge(s["exp"], b * 4 + 8)
                    pe.wait_ge(s["v"], b + 1)
                    for h in range(NH):
                        o = q * NH * HV + h * HV
                        for tile in range(2):
                            mm = pe.matmul(PS[:, 6 + p, o:o + HV], pt[:, h, tile, q * P:(q + 1) * P],
                                           v[p][:, tile, h, :], start=(tile == 0), stop=(tile == 1))
                    mm.then_inc(s["av_ps"], 1)

                def transpose_sums(b, p):
                    pe.wait_ge(s["norm"], b + 1)
                    for q in range(2):
                        mm = pe.transpose(PS[:, 6 + p, q * P:(q + 1) * P],
                                          oc[:, q].rearrange("q h d -> q (h d)"), t.ident[:, :])
                    mm.then_inc(s["ot_ps"], 1)

                def project_output(b, p):
                    pe.wait_ge(s["ot"], b + 1)
                    for q in range(2):
                        mm = pe.matmul(PS[:, 6 + p, L + q * D:L + (q + 1) * D], ot[:, q * P:(q + 1) * P],
                                       w.wvo[:, 1, :], start=True, stop=True)
                    mm.then_inc(s["out_ps"], 1)

                def transpose_maxima(b, p):
                    pe.wait_ge(s["nms"], b + 1)
                    for j in range(2):
                        mm = pe.transpose(PS[:, 6 + p, j * (P // 2):(j + 1) * (P // 2)].bitcast(BF16),
                                          nms[:, j, :], t.ident16[:, :])
                    mm.then_inc(s["nt_ps"], 1)

                def start():
                    pe.wait_ge(s["made"], 1)
                    for b in range(2):
                        transpose_tokens(b, b)
                        project_queries_keys(b, b)
                    project_values(0, 0)

                def body(b, k, p):
                    pe.wait_ge(s[f"stacks{p}"], k * STACK_DMAS + STACK_DMAS)
                    for n in range(2):
                        row_scores(b, p, n)
                    if exists(b + 2):
                        transpose_tokens(b + 2, p)
                    if exists(b - 1):
                        sum_values(b - 1, 1 - p, 0)
                    for n in range(2, 4):
                        row_scores(b, p, n)
                    if exists(b - 1):
                        sum_values(b - 1, 1 - p, 1)
                    transpose_maxima(b, p)
                    if exists(b + 2):
                        project_queries_keys(b + 2, p)
                    if exists(b - 1):
                        transpose_sums(b - 1, 1 - p)
                    if exists(b + 1):
                        project_values(b + 1, 1 - p)
                    if exists(b - 1):
                        project_output(b - 1, 1 - p)
                    pe.wait_ge(s["mt"], b + 1)
                    for n in range(4):
                        column_scores(b, p, n)

                def end():
                    for q in range(2):
                        sum_values(NB - 1, 1, q)
                    transpose_sums(NB - 1, 1)
                    project_output(NB - 1, 1)

                each_batch(pe, start, body, end)

            @block.scalar
            def _(act):
                def tokens(b, p):
                    act.wait_ge(s["tr"], b + 1)
                    act.activation(ut[p][:, :], PS[:, 4 + p, 0:L], ACT.Copy).then_inc(s["ut"], 1)

                def queries_keys(b, p):
                    act.wait_ge(s["qk_ps"], b + 1)
                    for g in range(2):
                        i = act.activation(qk[p][:, g, :], PS[:, 4 + p, g * L:(g + 1) * L],
                                           ACT.Identity, bias=w.bqk[:, g:g + 1])
                    i.then_inc(s["qk"], 1)

                def sums(b, p):
                    act.wait_ge(s["ot_ps"], b + 1)
                    act.activation(ot[:, :], PS[:, 6 + p, 0:L], ACT.Copy).then_inc(s["ot"], 1)

                def start():
                    act.nop().then_inc(s["exp"], 4)
                    for b in range(2):
                        tokens(b, b)
                        queries_keys(b, b)

                def body(b, k, p):
                    if exists(b + 2):
                        tokens(b + 2, p)
                    act.wait_ge(s["nt_ps"], b + 1)
                    act.activation(mt[:, :], PS[:, 6 + p, 0:P].bitcast(BF16), ACT.Copy).then_inc(s["mt"], 1)
                    if exists(b + 2):
                        queries_keys(b + 2, p)
                    if exists(b - 1):
                        sums(b - 1, 1 - p)
                    for n in range(4):
                        act.wait_ge(s["stt_ps"], b * 4 + n + 1)
                        bank = 2 * (n % 2)
                        act.activation(pt[:, 2 * n:2 * n + 2].rearrange("q h j c -> q h (j c)"),
                                       PS[:, bank:bank + 2, :], ACT.Exp, scale=HD ** -0.5).then_inc(s["exp"], 1)

                each_batch(act, start, body, lambda: sums(NB - 1, 1))

            @block.gpsimd
            def _(pool):
                zeros = zero[:, :].unsqueeze(2).broadcast_to([P, 2, L])

                def base_and_parts(b, p):
                    pool.wait_ge(s["u"], b + 1)
                    pool.wait_ge(s["qk"], b + 1)
                    bo = w.bvo[:, 1, :].unsqueeze(1).broadcast_to([P, 2, D])
                    if keep:
                        pool.tensor_tensor(t.R[:, bass.ds(b * 2, 2), :], us[p][:, :, :], bo, ALU.add)\
                            .then_inc(s["base"], 1)
                    else:
                        pool.tensor_tensor(t.H[:, bass.ds(b * 2, 2), :], t.H[:, bass.ds(b * 2, 2), :], bo, ALU.add)\
                            .then_inc(s["base"], 1)
                    pool.tensor_tensor(parts[p][:, 0], qk[p][:, :, :], zeros, ALU.add)
                    pool.drain()
                    pool.tensor_tensor(rest[:, :, :], qk[p][:, :, :], parts[p][:, 0], ALU.subtract)
                    pool.drain()
                    pool.tensor_tensor(parts[p][:, 1], rest[:, :, :], zeros, ALU.add)
                    pool.drain()
                    pool.tensor_tensor(parts[p][:, 2], rest[:, :, :], parts[p][:, 1], ALU.subtract)\
                        .then_inc(s["parts"], 1)

                def start():
                    for b in range(2):
                        base_and_parts(b, b)

                def body(b, k, p):
                    if exists(b + 2):
                        base_and_parts(b + 2, p)

                each_batch(pool, start, body, lambda: None)

            @block.sync
            def _(sp):
                def stack(b, p):
                    sp.wait_ge(s["parts"], b + 1)
                    if exists(b - 2):
                        sp.wait_ge(s["stt_ps"], b * 4 - 4)
                    for g in range(6):
                        rows = slice(g * HD, (g + 1) * HD)
                        sp.dma_start(qs[p][rows, :, :], parts[p][:, QUERY_PARTS[g], 0, :])\
                          .then_inc(s[f"stacks{p}"], 16)
                        sp.dma_start(ks[p][rows, :, :], parts[p][:, KEY_PARTS[g], 1, :])\
                          .then_inc(s[f"stacks{p}"], 16)

                def body(b, k, p):
                    if exists(b + 1):
                        stack(b + 1, 1 - p)

                each_batch(sp, lambda: stack(0, 0), body, lambda: None)

            @block.vector
            def _(dve):
                def normalize(b, p):
                    for h in range(2):
                        i = b * 2 + h
                        u = dve.tensor_scalar(us[p][:, h, :], t.H[:, i, :], t.MEAN[:, bass.ds(i, 1)],
                                              t.RSTD[:, bass.ds(i, 1)], ALU.subtract, ALU.mult)
                    u.then_inc(s["u"], 1)

                def values(b, p):
                    dve.wait_ge(s["v_ps"], b + 1)
                    for h in range(2):
                        i = dve.tensor_tensor(
                            v[p][:, h, :, 0:HD],
                            PS[:, 4 + p, h * D:(h + 1) * D].rearrange("q (h d) -> q h d", h=NH),
                            w.bvo[:, 0, :].rearrange("q (h d) -> q h d", h=NH), ALU.add)
                    i.then_inc(s["v"], 1)

                def maxima(b, n):
                    dve.wait_ge(s["st_ps"], b * 4 + n + 1)
                    bank = 2 * (n % 2)
                    dve.tensor_reduce(nm[:, :, 2 * n:2 * n + 2].rearrange("q j i -> q i j"),
                                      PS[:, bank:bank + 2, :].rearrange("q i (j c) -> q i j c", j=2),
                                      AX.X, ALU.max, negate=True).then_inc(s["mx"], 1)

                def cut_maxima():
                    dve.drain()
                    dve.tensor_copy(nms[:, :, 0:NH], nm[:, :, :])
                    dve.drain()
                    dve.tensor_tensor(nmrest[:, :, :], nm[:, :, :], nms[:, :, 0:NH], ALU.subtract)
                    dve.drain()
                    dve.tensor_copy(nms[:, :, NH:2 * NH], nmrest[:, :, :])
                    dve.drain()
                    dve.tensor_tensor(nms[:, :, 2 * NH:3 * NH], nmrest[:, :, :], nms[:, :, NH:2 * NH],
                                      ALU.subtract).then_inc(s["nms"], 1)

                def divide(b, p):
                    dve.wait_ge(s["av_ps"], b * 2 + 2)
                    av = PS[:, 6 + p, 0:2 * NH * HV].rearrange("q (j h e) -> q j h e", j=2, h=NH)
                    dve.reciprocal(rc[:, :, :], av[:, :, :, HD])
                    dve.drain()
                    for q in range(2):
                        i = dve.tensor_tensor(oc[:, q], av[:, q, :, 0:HD],
                                              rc[:, q, :].unsqueeze(2).broadcast_to([P, NH, HD]), ALU.mult)
                    i.then_inc(s["norm"], 1)

                def add_attention(b, p):
                    dve.wait_ge(s["out_ps"], b + 1)
                    dve.wait_ge(s["base"], b + 1)
                    out = PS[:, 6 + p, L:L + 2 * D].rearrange("q (j c) -> q j c", j=2)
                    x = t.R if keep else t.H
                    dve.tensor_tensor(x[:, bass.ds(b * 2, 2), :], out, x[:, bass.ds(b * 2, 2), :], ALU.add)
                    dve.drain()
                    for q in range(2):
                        dve.bn_stats(t.BN[:, b * 2 + q, :], x[:, b * 2 + q, :])

                def start():
                    dve.tensor_copy(sel[:, :, :], self_[:, :, :]).then_inc(s["made"], 1)
                    for b in range(2):
                        normalize(b, b)
                    dve.wait_ge(s["tr"], 1)
                    dve.wait_ge(s["base"], 1)
                    normalize(2, 0)
                    values(0, 0)

                def body(b, k, p):
                    for n in range(4):
                        maxima(b, n)
                    cut_maxima()
                    if exists(b - 1):
                        divide(b - 1, 1 - p)
                    if exists(b + 1):
                        values(b + 1, 1 - p)
                    if exists(b - 1):
                        add_attention(b - 1, 1 - p)
                    if exists(b + 3):
                        dve.wait_ge(s["base"], b + 2)
                        normalize(b + 3, 1 - p)

                def end():
                    divide(NB - 1, 1)
                    add_attention(NB - 1, 1)

                each_batch(dve, start, body, end)


def experts_layer(nc, t, a, name):
    first_layer = name == "l0moe"
    ntop = 1 if first_layer else 2
    tiles = TILES1 if first_layer else TILES2
    XS = t.XS1 if first_layer else t.XS2
    gelu = ACT.Gelu_apprx_tanh if first_layer else ACT.Gelu
    YS = nc.dram_tensor(f"{name}_out", [tiles * P, D], F32).ap()
    ln_scales(nc, t, f"{name}_ln")
    with ExitStack() as ctx:
        def sb(n, shape, dt=F32):
            return ctx.enter_context(nc.sbuf_tensor(f"{name}_{n}", shape, dt))

        s = t.moe_sems
        rows_moved = Sems(nc, ctx, name, "scattered gathered0 gathered1 gathered2 gathered3")
        if not first_layer:
            s.restart(nc)
        gb, gw, gbias = sb("gb", [P, 2, D]), sb("gate_w", [P, NE]), sb("gate_b", [P, NE])
        before, order, chain = sb("before", [P, P]), sb("order", [P, NE, NT]), sb("chain", [P, NE, NT])
        ones, trow = sb("ones", [P, P]), sb("trow", [1, NE, tiles])
        w1, w2, b2 = sb("w1", [P, NE, FF + KF]), sb("w2", [P, NE, KF, D]), sb("b2", [P, NE, D])
        pos = [sb(f"pos{i}", [P, NT], U32) for i in range(ntop)]
        gate = [sb(f"gate{i}", [P, NT]) for i in range(ntop)]
        te = sb("te", [1, tiles], I32)
        small = [(gb, a[name + "_gb"]), (gw, a[name + "_gate_w"]), (gbias, a[name + "_gate_b"]),
                 (before, a["c_before"]), (order, a["c_order"]), (chain, a["c_chain"])]
        PS = t.PS
        if not first_layer:
            t.U = sb("u", [P, NT, D])
            second_norm(nc, t)
            ln_scales(nc, t, f"{name}_ln2")
        src = t.R if first_layer else t.U

        with ExitStack() as sub:
            def tb(n, shape, dt=F32):
                return sub.enter_context(nc.sbuf_tensor(f"{name}_{n}", shape, dt))

            T = tb("t", [P, NT, D])
            stage, tt = [tb(f"st{i}", [P, D]) for i in range(2)], [tb(f"tt{i}", [P, P]) for i in range(2)]
            LG, E1, M = tb("lg", [P, NE, NT]), tb("e1", [P, NE, NT]), tb("m", [P, NE, NT])
            OH = [tb(f"oh{i}", [P, NE, NT]) for i in range(ntop)]
            CN, RK = tb("cn", [P, NE, NT]), tb("rk", [P, NE, NT])
            best, sm = tb("best", [P, NT]), tb("sm", [P, NT])
            nt_, en = tb("ntiles", [P, NE]), tb("ends", [P, NE])
            cmp_ = tb("cmp", [1, NE, tiles])

            with nc.Block() as block:
                load_all(block, small, s["weights"])

                @block.scalar
                def _(act):
                    act.dma_start(w1[:, :, :], a[name + "_w1"]).then_inc(s["w1"], 16)
                    act.dma_start(w2[:, :, :, :], a[name + "_w2"]).then_inc(s["w2"], 16)
                    act.dma_start(b2[:, :, :], a[name + "_b2"]).then_inc(s["b2"], 16)
                    with act.Fori(0, NT // 2) as k:
                        for p in range(2):
                            act.wait_ge(s["tr"], k * 2 + p + 3)
                            act.activation(tt[p][:, :], PS[:, p, 0:P], ACT.Copy).then_inc(s["tt"], 1)
                    act.wait_ge(s["exp1"], 1)
                    act.activation(E1[:, :, :], LG[:, :, :], ACT.Exp).then_inc(s["exp2"], 1)

                @block.gpsimd
                def _(pool):
                    pool.memset(ones[:, :], 1.0).then_inc(s["made"], 1)
                    pool.iota(trow[:, :, :], [[0, NE], [1, tiles]], base=0, channel_multiplier=0,
                              allow_small_or_imprecise_dtypes=True).then_inc(s["made"], 1)

                @block.tensor
                def _(pe):
                    pe.wait_ge(s["weights"], 16 * len(small))
                    pe.nop().then_inc(s["tr"], 2)
                    with pe.Fori(0, NT // 2) as k:
                        for p in range(2):
                            pe.wait_ge(s["staged"], k * 2 + p + 1)
                            pe.transpose(PS[:, p, 0:P], stage[p][:, :], t.ident[:, :]).then_inc(s["tr"], 1)
                        for p in range(2):
                            pe.wait_ge(s["tt"], k * 2 + p + 1)
                            pe.matmul(PS[:, 2, bass.ds((k * 2 + p) * NE, NE)], tt[p][:, :], gw[:, :],
                                      start=True, stop=True).then_inc(s["logits"], 1)
                    pe.wait_ge(s["made"], 2)
                    pe.wait_ge(s["counts_in"], 1)
                    oh = CN[:, :, :].rearrange("p e i -> p (e i)")
                    pe.matmul(PS[:, 4, 0:NE * NT], ones[:, :], oh, start=True, stop=True)
                    pe.matmul(PS[:, 5, 0:NE * NT], before[:, :], oh, start=True, stop=True)\
                      .then_inc(s["counts"], 1)

                @block.vector
                def _(dve):
                    dve.wait_ge(s["weights"], 16 * len(small))
                    with dve.Fori(0, NT // 2) as k:
                        for p in range(2):
                            i = k * 2 + p
                            dve.tensor_scalar(T[:, i, :], src[:, i, :], t.MEAN[:, bass.ds(i, 1)],
                                              t.RSTD[:, bass.ds(i, 1)], ALU.subtract, ALU.mult)
                        dve.drain()
                        i0 = k * 2
                        dve.tensor_tensor(T[:, bass.ds(i0, 2), :], T[:, bass.ds(i0, 2), :],
                                          gb[:, 0, :].unsqueeze(1).broadcast_to([P, 2, D]), ALU.mult)
                        dve.drain()
                        dve.wait_ge(s["tr"], k * 2 + 2)
                        dve.tensor_tensor(T[:, bass.ds(i0, 2), :], T[:, bass.ds(i0, 2), :],
                                          gb[:, 1, :].unsqueeze(1).broadcast_to([P, 2, D]), ALU.add)
                        dve.drain()
                        for p in range(2):
                            dve.tensor_copy(stage[p][:, :], T[:, k * 2 + p, :]).then_inc(s["staged"], 1)
                    dve.wait_ge(s["logits"], NT)
                    dve.tensor_tensor(LG[:, :, :].rearrange("p e i -> p i e"),
                                      PS[:, 2, 0:NT * NE].rearrange("p (i e) -> p i e", e=NE),
                                      gbias[:, :].unsqueeze(1).broadcast_to([P, NT, NE]), ALU.add)
                    dve.drain()

                    def over_experts(x):
                        return x.rearrange("p e i -> p i e")

                    def on_experts(x):
                        return x.unsqueeze(1).broadcast_to([P, NE, NT])

                    dve.tensor_reduce(best[:, :], over_experts(LG[:, :, :]), AX.X, ALU.max)
                    dve.drain()
                    dve.tensor_tensor(LG[:, :, :], LG[:, :, :], on_experts(best[:, :]), ALU.subtract)
                    dve.drain()

                    def first_at_least(onehot, floor):
                        dve.tensor_tensor(M[:, :, :], LG[:, :, :], floor, ALU.is_ge)
                        dve.drain()
                        dve.tensor_tensor(M[:, :, :], M[:, :, :], order[:, :, :], ALU.mult)
                        dve.drain()
                        dve.tensor_reduce(sm[:, :], over_experts(M[:, :, :]), AX.X, ALU.max)
                        dve.drain()
                        dve.tensor_tensor(onehot[:, :, :], order[:, :, :], on_experts(sm[:, :]), ALU.is_equal)
                        dve.drain()

                    dve.memset(best[:, :], 0.0)
                    dve.drain()
                    first_at_least(OH[0], on_experts(best[:, :]))
                    if first_layer:
                        dve.nop().then_inc(s["exp1"], 1)
                        dve.wait_ge(s["exp2"], 1)
                        dve.tensor_reduce(sm[:, :], over_experts(E1[:, :, :]), AX.X, ALU.add)
                        dve.drain()
                        dve.reciprocal(gate[0][:, :], sm[:, :])
                        dve.tensor_copy(CN[:, :, :], OH[0][:, :, :]).then_inc(s["counts_in"], 1)
                    else:
                        dve.scalar_tensor_tensor(LG[:, :, :], OH[0][:, :, :], NEG, LG[:, :, :], ALU.mult, ALU.add)
                        dve.drain()
                        dve.tensor_reduce(best[:, :], over_experts(LG[:, :, :]), AX.X, ALU.max)
                        dve.drain()
                        first_at_least(OH[1], on_experts(best[:, :]))
                        dve.tensor_tensor(CN[:, :, :], OH[0][:, :, :], OH[1][:, :, :], ALU.add)\
                           .then_inc(s["counts_in"], 1)
                        dve.tensor_tensor(LG[:, :, :], LG[:, :, :], OH[1][:, :, :], ALU.mult)
                        dve.drain()
                        dve.tensor_copy(LG[:, 0, :], best[:, :]).then_inc(s["exp1"], 1)
                        dve.wait_ge(s["exp2"], 1)
                        dve.tensor_scalar(sm[:, :], E1[:, 0, :], 1.0, None, ALU.add)
                        dve.drain()
                        dve.reciprocal(gate[0][:, :], sm[:, :])
                        dve.drain()
                        dve.tensor_tensor(gate[1][:, :], gate[0][:, :], E1[:, 0, :], ALU.mult)
                    dve.wait_ge(s["counts"], 1)
                    flat = "p e i -> p (e i)"
                    dve.tensor_tensor_scan(RK[:, :, :].rearrange(flat), chain[:, :, :].rearrange(flat),
                                           PS[:, 4, 0:NE * NT], 0.0, ALU.mult, ALU.add)
                    dve.drain()
                    dve.wait_ge(s["made"], 2)
                    dve.tensor_scalar(nt_[:, :], RK[:, :, NT - 1], 127.0, 1.0 / P, ALU.add, ALU.mult)
                    dve.drain()
                    dve.tensor_scalar(nt_[:, :], nt_[:, :], -127.0 / 256, MAGIC, ALU.add, ALU.add)
                    dve.drain()
                    dve.tensor_scalar(nt_[:, :], nt_[:, :], -MAGIC, None, ALU.add)
                    dve.drain()
                    dve.tensor_tensor_scan(en[:, :], ones[:, 0:NE], nt_[:, :], 0.0, ALU.mult, ALU.add)
                    dve.tensor_tensor(RK[:, :, :], RK[:, :, :],
                                      PS[:, 4, 0:NE * NT].rearrange("p (e i) -> p e i", e=NE), ALU.subtract)
                    dve.drain()
                    dve.tensor_tensor(RK[:, :, :], RK[:, :, :],
                                      PS[:, 5, 0:NE * NT].rearrange("p (e i) -> p e i", e=NE), ALU.add)
                    dve.tensor_tensor(nt_[:, :], en[:, :], nt_[:, :], ALU.subtract)
                    dve.drain()
                    dve.tensor_scalar(nt_[:, :], nt_[:, :], float(P), None, ALU.mult)
                    dve.drain()
                    dve.tensor_tensor(RK[:, :, :], RK[:, :, :],
                                      nt_[:, :].unsqueeze(2).broadcast_to([P, NE, NT]), ALU.add)
                    dve.drain()
                    for j in range(ntop):
                        dve.tensor_tensor(M[:, :, :], RK[:, :, :], OH[j][:, :, :], ALU.mult)
                        dve.drain()
                        dve.tensor_reduce(sm[:, :], over_experts(M[:, :, :]), AX.X, ALU.add)
                        dve.drain()
                        dve.tensor_copy(pos[j][:, :], sm[:, :])
                        dve.drain()
                    dve.tensor_tensor(cmp_[:, :, :], trow[:, :, :],
                                      en[0:1, :].unsqueeze(2).broadcast_to([1, NE, tiles]), ALU.is_ge)
                    dve.drain()
                    dve.tensor_reduce(trow[:, 0, :], cmp_[:, 0:NE - 1, :].rearrange("p e r -> p r e"), AX.X, ALU.add)
                    dve.drain()
                    dve.tensor_copy(te[:, :], trow[:, 0, :])

            with nc.Block() as block:
                if first_layer:
                    convolution_kernel(nc, t, a, sub, block)

                @block.gpsimd
                def _(pool):
                    for j in range(ntop):
                        for i in range(NT):
                            pool.indirect_dma_start(
                                out=XS, out_offset=bass.IndirectOffsetOnAxis(ap=pos[j][:, i:i + 1], axis=0),
                                in_=T[:, i, :], in_offset=None).then_inc(rows_moved["scattered"], 16)
                    pool.wait_ge(rows_moved["scattered"], 16 * ntop * NT)

        with ExitStack() as sub:
            def tb(n, shape, dt=F32):
                return sub.enter_context(nc.sbuf_tensor(f"{name}_{n}", shape, dt))

            two = range(2)
            xs, xt = [tb(f"xs{i}", [P, D]) for i in two], [tb(f"xt{i}", [P, P]) for i in two]
            ws = [tb(f"ws{i}", [P, FF + KF]) for i in two]
            hp, hid = [tb(f"hp{i}", [P, KF, P]) for i in two], [tb(f"hid{i}", [P, KF, P]) for i in two]
            res = [tb(f"res{i}", [P, D]) for i in two]

            def each_tile(eng, first, body, last):
                first()
                for i in range(2):
                    body(i, 0, i)
                with eng.Fori(1, tiles // 2 - 1) as k:
                    for p in range(2):
                        body(k * 2 + p, k, p)
                for i in range(tiles - 2, tiles):
                    body(i, i // 2, i % 2)
                last()

            def there(i):
                return not isinstance(i, int) or 0 <= i < tiles

            def expert_of(eng, i):
                return eng.value_load(te[0:1, bass.ds(i, 1)], min_val=0, max_val=NE - 1)

            with nc.Block() as block:

                @block.sync
                def _(sp):
                    def body(i, k, p):
                        if there(i - 2):
                            sp.wait_ge(s["xtr"], i - 1)
                        sp.dma_start(xs[p][:, :], XS[bass.ds(i * P, P), :]).then_inc(s[f"xs{p}"], 16)

                    each_tile(sp, lambda: None, body, lambda: None)

                @block.tensor
                def _(pe):
                    def turn(i, k, p):
                        pe.wait_ge(s[f"xs{p}"], k * 16 + 16)
                        pe.transpose(PS[:, p, 0:P], xs[p][:, :], t.ident[:, :]).then_inc(s["xtr"], 1)

                    def up(i, p):
                        pe.wait_ge(s["picked"], i + 1)
                        for j in range(KF):
                            mm = pe.matmul(PS[:, 2 + p, j * P:(j + 1) * P], ws[p][:, j * P:(j + 1) * P],
                                           xt[p][:, :], start=True, stop=True)
                        mm.then_inc(s["hid_ps"], 1)

                    def down(i, p):
                        e = expert_of(pe, i)
                        pe.wait_ge(s["hid"], i + 1)
                        if there(i - 2):
                            pe.wait_ge(s["res"], i - 1)
                        for j in range(KF):
                            mm = pe.matmul(PS[:, 4 + p, 0:D], hid[p][:, j, :], w2[:, e, j, :],
                                           start=(j == 0), stop=(j == KF - 1))
                        mm.then_inc(s["out_ps"], 1)

                    def start():
                        pe.wait_ge(s["w2"], 16)
                        turn(0, 0, 0)

                    def body(i, k, p):
                        if there(i + 1):
                            turn(i + 1, k + p, 1 - p)
                        up(i, p)
                        if there(i - 1):
                            down(i - 1, 1 - p)

                    each_tile(pe, start, body, lambda: down(tiles - 1, 1))

                @block.scalar
                def _(act):
                    def store(i, p):
                        act.wait_ge(s["res"], i + 1)
                        act.dma_start(YS[bass.ds(i * P, P), :], res[p][:, :]).then_inc(s[f"sent{p}"], 16)

                    def body(i, k, p):
                        act.wait_ge(s["pre"], i + 1)
                        act.activation(hid[p][:, :, :], hp[p][:, :, :], gelu).then_inc(s["hid"], 1)
                        if there(i - 1):
                            store(i - 1, 1 - p)

                    def end():
                        store(tiles - 1, 1)
                        for p in range(2):
                            act.wait_ge(s[f"sent{p}"], 16 * (tiles // 2))

                    each_tile(act, lambda: None, body, end)

                @block.vector
                def _(dve):
                    def pick(i, p):
                        e = expert_of(dve, i)
                        dve.drain()
                        dve.wait_ge(s["xtr"], i + 1)
                        dve.tensor_copy(xt[p][:, :], PS[:, p, 0:P])
                        dve.tensor_copy(ws[p][:, :], w1[:, e, :]).then_inc(s["picked"], 1)

                    def add_bias(i, p):
                        dve.wait_ge(s["hid_ps"], i + 1)
                        dve.tensor_tensor(hp[p][:, :, :], PS[:, 2 + p, :].rearrange("f (j r) -> f j r", j=KF),
                                          ws[p][:, FF:FF + KF].unsqueeze(2).broadcast_to([P, KF, P]), ALU.add)\
                           .then_inc(s["pre"], 1)

                    def finish(i, k, p):
                        e = expert_of(dve, i)
                        dve.wait_ge(s["out_ps"], i + 1)
                        if there(i - 2):
                            dve.wait_ge(s[f"sent{p}"], k * 16)
                        dve.tensor_tensor(res[p][:, :], PS[:, 4 + p, 0:D], b2[:, e, :], ALU.add)\
                           .then_inc(s["res"], 1)

                    def start():
                        dve.wait_ge(s["b2"], 16)
                        dve.wait_ge(s["w1"], 16)
                        pick(0, 0)

                    def body(i, k, p):
                        if there(i + 1):
                            pick(i + 1, 1 - p)
                        add_bias(i, p)
                        if there(i - 1):
                            finish(i - 1, k - 1 + p, 1 - p)

                    each_tile(dve, start, body, lambda: finish(tiles - 1, tiles // 2 - 1, 1))

        CH = 4
        n = NT // CH
        with ExitStack() as sub:
            got = [sub.enter_context(nc.sbuf_tensor(f"{name}_got{j}", [P, NT, D], F32)) for j in range(ntop)]
            with nc.Block() as block:

                @block.gpsimd
                def _(pool):
                    for c in range(CH):
                        for i in range(c * n, (c + 1) * n):
                            for j in range(ntop):
                                pool.indirect_dma_start(
                                    out=got[j][:, i, :], out_offset=None, in_=YS,
                                    in_offset=bass.IndirectOffsetOnAxis(ap=pos[j][:, i:i + 1], axis=0))\
                                    .then_inc(rows_moved[f"gathered{c}"], 16)
                    for c in range(CH):
                        pool.wait_ge(rows_moved[f"gathered{c}"], 16 * ntop * n)

                @block.vector
                def _(dve):
                    if not first_layer:
                        dve.tensor_tensor(t.H[:, :, :], t.H[:, :, :], t.U[:, :, :], ALU.add)
                        dve.drain()
                    for c in range(CH):
                        tiles_ = slice(c * n, (c + 1) * n)
                        dve.wait_ge(rows_moved[f"gathered{c}"], 16 * ntop * n)
                        for j in range(ntop):
                            dve.tensor_tensor(got[j][:, tiles_, :], got[j][:, tiles_, :],
                                              gate[j][:, tiles_].unsqueeze(2).broadcast_to([P, n, D]), ALU.mult)
                        dve.drain()
                        for j in range(ntop):
                            dve.tensor_tensor(t.H[:, tiles_, :], t.H[:, tiles_, :], got[j][:, tiles_, :], ALU.add)
                            dve.drain()
                        with dve.Fori(0, n) as i:
                            dve.bn_stats(t.BN[:, i + c * n, :], t.H[:, i + c * n, :])


def bitlinear_ffn(nc, t, a):
    ln_scales(nc, t, "bit_ln")
    with ExitStack() as ctx:
        def sb(n, shape, dt=F32):
            return ctx.enter_context(nc.sbuf_tensor(f"bit_{n}", shape, dt))

        s = Sems(nc, ctx, "bit", "weights ones sums sum_ps ident xq tr xt up_ps h hr hq htr ht out_ps added")
        up, down = sb("up", [P, FF]), sb("down", [P, KF, D])
        upq, downq = sb("upq", [P, FF], BF16), sb("downq", [P, KF, D], BF16)
        identb = sb("ident", [P, P], BF16)
        ones, sums, ws, wi = sb("ones", [P, P]), sb("sums", [P, 2]), sb("ws", [P, 2]), sb("wi", [P, 2])
        two = range(2)
        U, XQ, XT = sb("u", [P, NT, D]), sb("xq", [P, NT, D], BF16), sb("xt", [P, NT, P], BF16)
        am0, xsc0, osc0 = sb("token_am", [P, NT]), sb("token_xsc", [P, NT]), sb("token_osc", [P, NT])
        am, xsc, osc = [sb(f"am{i}", [P, 2]) for i in two], sb("xsc", [P, 2]), [sb(f"osc{i}", [P, 2]) for i in two]
        h, hr = [sb(f"h{i}", [P, 2, FF]) for i in two], [sb(f"hr{i}", [P, 2, FF]) for i in two]
        hq, ht = [sb(f"hq{i}", [P, 2, FF], BF16) for i in two], [sb(f"ht{i}", [P, 2, FF], BF16) for i in two]
        xts = [sb(f"xts{i}", [P, 2, P], BF16) for i in two]
        PS = t.PS
        PB = PS[:, :, :].bitcast(BF16)

        with nc.Block() as block:
            load_all(block, [(up, a["bit_up"]), (down, a["bit_down"])], s["weights"])

            @block.tensor
            def _(pe):
                pe.wait_ge(s["sums"], 1)
                pe.matmul(PS[:, 0, 0:2], ones[:, :], sums[:, :], start=True, stop=True).then_inc(s["sum_ps"], 1)
                for g in range(4):
                    pe.wait_ge(s["xq"], g + 1)
                    for i in range(8):
                        mm = pe.transpose(PB[:, 4 + g, i * P:(i + 1) * P], XQ[:, 8 * g + i, :], identb[:, :])
                    mm.then_inc(s["tr"], 1)

            @block.scalar
            def _(act):
                for g in range(4):
                    act.wait_ge(s["tr"], g + 1)
                    act.activation(XT[:, 8 * g:8 * g + 8, :].rearrange("p i c -> p (i c)"), PB[:, 4 + g, :],
                                   ACT.Copy)

            @block.vector
            def _(dve):
                dve.memset(ones[:, :], 1.0)
                dve.tensor_copy(identb[:, :], t.ident[:, :])
                dve.wait_ge(s["weights"], 32)
                dve.tensor_reduce(sums[:, 0:1], up[:, :], AX.X, ALU.add, apply_absolute_value=True)
                dve.tensor_reduce(sums[:, 1:2], down[:, :, :], AX.XY, ALU.add, apply_absolute_value=True)
                dve.drain()
                dve.nop().then_inc(s["sums"], 1)
                dve.wait_ge(s["sum_ps"], 1)
                dve.tensor_scalar(ws[:, :], PS[:, 0, 0:2], 1.0 / (D * FF), EPS, ALU.mult, ALU.max)
                dve.drain()
                dve.reciprocal(wi[:, :], ws[:, :])
                dve.drain()
                for n, (w, q) in enumerate(((up[:, :], upq[:, :]), (down[:, :, :], downq[:, :, :]))):
                    dve.tensor_scalar(w, w, wi[:, n:n + 1], MAGIC, ALU.mult, ALU.add)
                    dve.drain()
                    dve.tensor_scalar(w, w, -MAGIC, 1.0, ALU.add, ALU.min)
                    dve.drain()
                    dve.tensor_scalar(q, w, -1.0, None, ALU.max)
                with dve.Fori(0, NT) as i:
                    dve.tensor_scalar(U[:, i, :], t.H[:, i, :], t.MEAN[:, bass.ds(i, 1)],
                                      t.RSTD[:, bass.ds(i, 1)], ALU.subtract, ALU.mult)
                dve.drain()
                dve.tensor_reduce(am0[:, :], U[:, :, :], AX.X, ALU.max, apply_absolute_value=True)
                dve.drain()
                dve.tensor_scalar(am0[:, :], am0[:, :], EPS, None, ALU.max)
                dve.drain()
                dve.reciprocal(xsc0[:, :], am0[:, :])
                dve.tensor_scalar(osc0[:, :], am0[:, :], 1.0 / 127, ws[:, 0:1], ALU.mult, ALU.mult)
                dve.drain()
                dve.tensor_scalar(xsc0[:, :], xsc0[:, :], 127.0, None, ALU.mult)
                dve.drain()
                for g in range(4):
                    n = slice(8 * g, 8 * g + 8)
                    dve.tensor_tensor(U[:, n, :], U[:, n, :], xsc0[:, n].unsqueeze(2).broadcast_to([P, 8, D]),
                                      ALU.mult)
                    dve.drain()
                    dve.tensor_scalar(XQ[:, n, :], U[:, n, :], MAGIC, -MAGIC, ALU.add, ALU.add)\
                       .then_inc(s["xq"], 1)

        with nc.Block() as block:

            @block.tensor
            def _(pe):
                def up(b, p):
                    pe.wait_ge(s["xt"], b + 1)
                    if exists(b - 2):
                        pe.wait_ge(s["h"], b - 1)
                    for j in range(2):
                        mm = pe.matmul(PS[:, 2 * p + j, :], xts[p][:, j, :], upq[:, :], start=True, stop=True)
                    mm.then_inc(s["up_ps"], 1)

                def turn(b, p):
                    pe.wait_ge(s["hq"], b + 1)
                    for j in range(2):
                        for f in range(KF):
                            o = (j * KF + f) * P
                            mm = pe.transpose(PB[:, 4 + p, o:o + P], hq[p][:, j, f * P:(f + 1) * P], identb[:, :])
                    mm.then_inc(s["htr"], 1)

                def down(b, p):
                    pe.wait_ge(s["ht"], b + 1)
                    if exists(b - 2):
                        pe.wait_ge(s["added"], b - 1)
                    for j in range(2):
                        for f in range(KF):
                            mm = pe.matmul(PS[:, 6 + p, j * D:(j + 1) * D], ht[p][:, j, f * P:(f + 1) * P],
                                           downq[:, f, :], start=(f == 0), stop=(f == KF - 1))
                    mm.then_inc(s["out_ps"], 1)

                def body(b, k, p):
                    if exists(b + 1):
                        up(b + 1, 1 - p)
                    turn(b, p)
                    down(b, p)

                each_batch(pe, lambda: up(0, 0), body, lambda: None)

            @block.scalar
            def _(act):
                def relu(b, p):
                    act.wait_ge(s["up_ps"], b + 1)
                    for j in range(2):
                        i = act.activation(h[p][:, j, :], PS[:, 2 * p + j, :], ACT.Relu,
                                           scale=osc0[:, bass.ds(b * 2 + j, 1)])
                    i.then_inc(s["h"], 1)

                def body(b, k, p):
                    if exists(b + 1):
                        relu(b + 1, 1 - p)
                    act.wait_ge(s["htr"], b + 1)
                    act.activation(ht[p][:, :, :].rearrange("p j f -> p (j f)"), PB[:, 4 + p, :], ACT.Copy)\
                       .then_inc(s["ht"], 1)

                each_batch(act, lambda: relu(0, 0), body, lambda: None)

            @block.gpsimd
            def _(pool):
                def stage(b, p):
                    pool.tensor_copy(xts[p][:, :, :], XT[:, bass.ds(b * 2, 2), :]).then_inc(s["xt"], 1)

                def body(b, k, p):
                    pool.wait_ge(s["h"], b + 1)
                    if exists(b + 2):
                        stage(b + 2, p)
                    pool.tensor_scalar(hr[p][:, 0, :], h[p][:, 0, :], MAGIC, -MAGIC, ALU.add, ALU.add)\
                        .then_inc(s["hr"], 1)

                def start():
                    for b in range(2):
                        stage(b, b)

                each_batch(pool, start, body, lambda: None)

            @block.vector
            def _(dve):
                def quantize(b, p):
                    dve.wait_ge(s["h"], b + 1)
                    dve.tensor_scalar(hr[p][:, 1, :], h[p][:, 1, :], MAGIC, -MAGIC, ALU.add, ALU.add)
                    dve.tensor_reduce(am[p][:, :], h[p][:, :, :], AX.X, ALU.max)
                    dve.drain()
                    dve.tensor_scalar(am[p][:, :], am[p][:, :], MAGIC, -MAGIC, ALU.add, ALU.add)
                    dve.drain()
                    dve.tensor_scalar(am[p][:, :], am[p][:, :], 127.0, EPS, ALU.min, ALU.max)
                    dve.drain()
                    dve.reciprocal(xsc[:, :], am[p][:, :])
                    dve.tensor_scalar(osc[p][:, :], am[p][:, :], 1.0 / 127, ws[:, 1:2], ALU.mult, ALU.mult)
                    dve.drain()
                    dve.tensor_scalar(xsc[:, :], xsc[:, :], 127.0, None, ALU.mult)
                    dve.drain()
                    for j in (1, 0):
                        if j == 0:
                            dve.wait_ge(s["hr"], b + 1)
                        dve.tensor_scalar(hr[p][:, j, :], hr[p][:, j, :], 127.0, xsc[:, j:j + 1],
                                          ALU.min, ALU.mult)
                    dve.drain()
                    dve.tensor_scalar(hq[p][:, :, :], hr[p][:, :, :], MAGIC, -MAGIC, ALU.add, ALU.add)\
                       .then_inc(s["hq"], 1)

                def add(b, p):
                    dve.wait_ge(s["out_ps"], b + 1)
                    for j in range(2):
                        i = b * 2 + j
                        x = dve.scalar_tensor_tensor(t.H[:, i, :], PS[:, 6 + p, j * D:(j + 1) * D],
                                                     osc[p][:, j:j + 1], t.H[:, i, :], ALU.mult, ALU.add)
                    x.then_inc(s["added"], 1)
                    dve.drain()
                    for j in range(2):
                        dve.bn_stats(t.BN[:, b * 2 + j, :], t.H[:, b * 2 + j, :])

                def body(b, k, p):
                    quantize(b, p)
                    if exists(b - 1):
                        add(b - 1, 1 - p)

                each_batch(dve, lambda: None, body, lambda: add(NB - 1, 1))


def convolution_kernel(nc, t, a, ctx, block):
    N = NSTATE

    def sb(n, shape, dt=F32):
        return ctx.enter_context(nc.sbuf_tensor(f"ssm_{n}", shape, dt))

    s = Sems(nc, ctx, "ssm", "loaded dt pe dve kernel zeros hankel")
    A, E, G = sb("a", [N, 2, N]), sb("e", [N, 2, N]), sb("g", [N, 2, N])
    inv_t, bc, ldt, dt = sb("inv_t", [N, N]), sb("bc", [N, 2]), sb("ldt", [N, 1]), sb("dt", [N, 1])
    flip = sb("flip", [P, P])
    V, C, eb = sb("v", [N, 16]), sb("c", [N, 16]), sb("eb", [N, 1])
    K, zeros = sb("k", [16, 16]), sb("zeros", [1, L])
    hankel = sb("hankel", [P, 2, P])
    KZ = nc.dram_tensor("ssm_kernel", [2 * L], F32).ap()
    loads = [(A, a["c_hippo"]), (inv_t, a["c_hippo_inv_t"]), (bc, a["ssm_bc"]), (ldt, a["ssm_log_dt"]),
             (flip, a["c_flip"])]
    PS = t.PS
    doublings = [(V, m) for m in (1, 2, 4, 8)] + [(C, m) for m in (1, 2, 4, 8)]
    TERMS = 8

    @block.sync
    def _(sp):
        for dst, src in loads:
            sp.dma_start(dst[tuple(slice(None) for _ in dst.shape)], src).then_inc(s["loaded"], 16)
        sp.wait_ge(s["zeros"], 1)
        sp.dma_start(KZ[L:2 * L].unsqueeze(0), zeros[:, :]).then_inc(s["kernel"], 16)
        sp.wait_ge(s["dve"], TERMS + SQUARINGS + 3 + 2 * len(doublings))
        sp.dma_start(KZ[0:L].rearrange("(i j) -> i j", i=16), K[:, :]).then_inc(s["kernel"], 16)
        sp.wait_ge(s["kernel"], 32)
        for n in range(2):
            sp.dma_start(hankel[:, n, :], bass.AP(KZ.tensor, P * (1 - n), [[1, P], [1, P]]))\
              .then_inc(s["hankel"], 16)

    @block.scalar
    def _(act):
        act.wait_ge(s["loaded"], 16 * len(loads))
        act.activation(dt[:, :], ldt[:, :], ACT.Exp).then_inc(s["dt"], 1)

    @block.tensor
    def _(pe):
        done = [0]

        def after_dve():
            done[0] += 1
            pe.wait_ge(s["dve"], done[0])

        def pair(x, y):
            after_dve()
            pe.matmul(PS[0:N, 0, 0:N], x[:, 1, :], y[:, 0, :], start=True, stop=True)
            pe.matmul(PS[0:N, 0, N:2 * N], x[:, 0, :], y[:, 1, :], start=True, stop=True)\
              .then_inc(s["pe"], 1)

        for _ in range(TERMS - 1):
            pair(A, G)
        pair(A, G)
        for _ in range(SQUARINGS):
            pair(E, E)
        after_dve()
        pe.matmul(PS[0:N, 0, 0:1], E[:, 1, :], bc[:, 0:1], start=True, stop=True).then_inc(s["pe"], 1)
        after_dve()
        pe.matmul(PS[0:N, 0, 0:1], inv_t[:, :], eb[:, :], start=True, stop=True).then_inc(s["pe"], 1)
        for n, (x, m) in enumerate(doublings):
            after_dve()
            side = E[:, 1, :] if x is V else E[:, 0, :]
            pe.matmul(PS[0:N, 0, 0:m], side, x[:, 0:m], start=True, stop=True).then_inc(s["pe"], 1)
            if n < len(doublings) - 1:
                pair(E, E)
        after_dve()
        pe.matmul(PS[0:16, 0, 0:16], C[:, :], V[:, :], start=True, stop=True).then_inc(s["pe"], 1)
        pe.wait_ge(s["hankel"], 32)
        for n in range(2):
            mm = pe.matmul(PS[:, 1, n * P:(n + 1) * P], hankel[:, n, :], flip[:, :], start=True, stop=True)
        mm.then_inc(s["pe"], 1)

    @block.vector
    def _(dve):
        done = [0]

        def after_pe():
            done[0] += 1
            dve.wait_ge(s["pe"], done[0])

        dve.memset(zeros[:, :], 0.0).then_inc(s["zeros"], 1)
        dve.wait_ge(s["dt"], 1)
        dve.tensor_scalar(A[:, :, :], A[:, :, :], dt[:, :], 2.0 ** -SQUARINGS, ALU.mult, ALU.mult)
        dve.tensor_copy(G[:, 0, :], t.ident[0:N, 0:N])
        dve.tensor_copy(G[:, 1, :], t.ident[0:N, 0:N])
        dve.drain()
        dve.nop().then_inc(s["dve"], 1)
        product = PS[0:N, 0, 0:2 * N].rearrange("p (h c) -> p h c", h=2)
        eye = t.ident[0:N, 0:N].unsqueeze(1).broadcast_to([N, 2, N])
        for n in range(TERMS, 1, -1):
            after_pe()
            dve.scalar_tensor_tensor(G[:, :, :], product, 1.0 / n, eye, ALU.mult, ALU.add)\
               .then_inc(s["dve"], 1)
        after_pe()
        dve.tensor_copy(E[:, :, :], product).then_inc(s["dve"], 1)

        def double():
            after_pe()
            dve.scalar_tensor_tensor(E[:, :, :], E[:, :, :], 2.0, product, ALU.mult, ALU.add)\
               .then_inc(s["dve"], 1)

        for _ in range(SQUARINGS):
            double()
        after_pe()
        dve.tensor_copy(eb[:, :], PS[0:N, 0, 0:1]).then_inc(s["dve"], 1)
        after_pe()
        dve.tensor_copy(V[:, 0:1], PS[0:N, 0, 0:1])
        dve.tensor_copy(C[:, 0:1], bc[:, 1:2])
        dve.drain()
        dve.nop().then_inc(s["dve"], 1)
        for n, (x, m) in enumerate(doublings):
            after_pe()
            dve.tensor_tensor(x[:, m:2 * m], x[:, 0:m], PS[0:N, 0, 0:m], ALU.add).then_inc(s["dve"], 1)
            if n < len(doublings) - 1:
                double()
        after_pe()
        dve.tensor_copy(K[:, :], PS[0:16, 0, 0:16]).then_inc(s["dve"], 1)
        after_pe()
        dve.tensor_copy(t.toep[:, :, :], PS[:, 1, 0:2 * P].rearrange("p (n c) -> p n c", n=2))


def state_space(nc, t, a):
    ln_scales(nc, t, "ssm_ln")
    with ExitStack() as ctx:
        s = Sems(nc, ctx, "conv", "skip u conv")
        skip = ctx.enter_context(nc.sbuf_tensor("ssm_skip", [P, 1], F32))
        U = ctx.enter_context(nc.sbuf_tensor("ssm_u", [P, NT, D], F32))
        PS = t.PS
        U4 = U[:, :, :].rearrange("p (b h) c -> p b h c", h=2)

        with nc.Block() as block:

            @block.sync
            def _(sp):
                sp.dma_start(skip[:, :], a["ssm_d"]).then_inc(s["skip"], 16)

            @block.tensor
            def _(pe):
                for g in range(4):
                    pe.wait_ge(s["u"], 8 * g + 8)
                    rhs = [U4[:, 4 * g:4 * g + 4, h, :] for h in range(2)]
                    pe.matmul(PS[:, 2 * g, :], t.toep[:, 0, :], rhs[0], start=True, stop=True)
                    pe.matmul(PS[:, 2 * g + 1, :], t.toep[:, 1, :], rhs[0], start=True, stop=False)
                    pe.matmul(PS[:, 2 * g + 1, :], t.toep[:, 0, :], rhs[1], start=False, stop=True)\
                      .then_inc(s["conv"], 1)

            @block.vector
            def _(dve):
                H4 = t.H[:, :, :].rearrange("p (b h) c -> p b h c", h=2)
                with dve.Fori(0, NT) as i:
                    dve.tensor_scalar(U[:, i, :], t.H[:, i, :], t.MEAN[:, bass.ds(i, 1)],
                                      t.RSTD[:, bass.ds(i, 1)], ALU.subtract, ALU.mult).then_inc(s["u"], 1)
                dve.drain()
                dve.wait_ge(s["skip"], 16)
                dve.scalar_tensor_tensor(t.H[:, :, :], U[:, :, :], skip[:, 0:1], t.H[:, :, :], ALU.mult, ALU.add)
                dve.drain()
                for g in range(4):
                    dve.wait_ge(s["conv"], g + 1)
                    for h in range(2):
                        dve.tensor_tensor(H4[:, 4 * g:4 * g + 4, h, :], H4[:, 4 * g:4 * g + 4, h, :],
                                          PS[:, 2 * g + h, :].rearrange("p (b c) -> p b c", b=4), ALU.add)
                dve.drain()
                with dve.Fori(0, NT) as i:
                    dve.bn_stats(t.BN[:, i, :], t.H[:, i, :])


def bilinear_attention(nc, t, a):
    ln_scales(nc, t, "bil_ln")
    with ExitStack() as ctx:
        def sb(n, shape, dt=F32):
            return ctx.enter_context(nc.sbuf_tensor(f"bil_{n}", shape, dt))

        s = Sems(nc, ctx, "bil", "weights u tr ut v_ps v tq_ps tq st_ps mx exp pr_ps pr av_ps norm")
        wq, wv = sb("wq", [P, NH, D]), sb("wv", [P, D])
        two = range(2)
        us, ut = [sb(f"us{i}", [P, 2, D]) for i in two], [sb(f"ut{i}", [P, L]) for i in two]
        v = [sb(f"v{i}", [P, 2, NH, HV]) for i in two]
        tq = [sb(f"tq{i}", [P, NH, L]) for i in two]
        nm = sb("nm", [P, NH, 2])
        pr = [sb(f"pr{i}", [P, 2, L]) for i in range(4)]
        pt = [sb(f"pt{i}", [P, NH, 2, L]) for i in two]
        rc, oc = sb("rc", [P, 2, NH]), sb("oc", [P, 2, NH, HD])
        attention_prelude(nc, t, s, None, None, v, [(wq, a["bil_q"]), (wv, a["bil_v"])])
        PS = t.PS
        LAG = 2
        A_BANK, SUMS = 6, 7

        def first(b, h, back):
            return isinstance(b, int) and b * NH + h < back

        with nc.Block() as block:

            @block.tensor
            def _(pe):
                def transpose_tokens(b, p):
                    pe.wait_ge(s["u"], b + 1)
                    if exists(b - 1):
                        pe.wait_ge(s["v"], b)
                    for h in range(2):
                        mm = pe.transpose(PS[:, A_BANK, h * P:(h + 1) * P], us[p][:, h, :], t.ident[:, :])
                    mm.then_inc(s["tr"], 1)

                def project_queries(b, p, n):
                    if n == 0:
                        pe.wait_ge(s["ut"], b + 1)
                    else:
                        pe.wait_ge(s["tq"], b * 4 + n)
                    for h in range(2):
                        mm = pe.matmul(PS[:, A_BANK, h * L:(h + 1) * L], wq[:, 2 * n + h, :], ut[p][:, :],
                                       start=True, stop=True)
                    mm.then_inc(s["tq_ps"], 1)

                def project_values(b, p):
                    pe.wait_ge(s["tq"], b * 4 + 4)
                    for h in range(2):
                        mm = pe.matmul(PS[:, A_BANK, h * D:(h + 1) * D], ut[p][:, h * P:(h + 1) * P],
                                       wv[:, :], start=True, stop=True)
                    mm.then_inc(s["v_ps"], 1)

                def scores(b, p, h):
                    if not first(b, h, 4):
                        pe.wait_ge(s["exp"], b * NH + h - 3)
                    if h == 0:
                        pe.wait_ge(s["tq"], b * 4 + 4)
                    for q in range(2):
                        mm = pe.matmul(PS[:, h % 4, q * L:(q + 1) * L], tq[p][:, h, q * P:(q + 1) * P],
                                       ut[p][:, :], start=True, stop=True)
                    mm.then_inc(s["st_ps"], 1)

                def turn(b, h):
                    pe.wait_ge(s["exp"], b * NH + h + 1)
                    if not first(b, h, 2):
                        pe.wait_ge(s["pr"], b * NH + h - 1)
                    for q in range(2):
                        for tile in range(2):
                            o = tile * L + q * P
                            mm = pe.transpose(PS[:, 4 + h % 2, o:o + P], pr[h % 4][:, q, tile * P:(tile + 1) * P],
                                              t.ident[:, :])
                    mm.then_inc(s["pr_ps"], 1)

                def sum_values(b, p, q):
                    if q == 0:
                        pe.wait_ge(s["pr"], b * NH + NH)
                        pe.wait_ge(s["v"], b + 1)
                        if exists(b - 1):
                            pe.wait_ge(s["norm"], b)
                    for h in range(NH):
                        o = q * NH * HV + h * HV
                        for tile in range(2):
                            mm = pe.matmul(PS[:, SUMS, o:o + HV], pt[p][:, h, tile, q * P:(q + 1) * P],
                                           v[p][:, tile, h, :], start=(tile == 0), stop=(tile == 1))
                    mm.then_inc(s["av_ps"], 1)

                def start():
                    transpose_tokens(0, 0)
                    for n in range(4):
                        project_queries(0, 0, n)
                    project_values(0, 0)

                def body(b, k, p):
                    for h in range(NH):
                        scores(b, p, h)
                        if h >= LAG:
                            turn(b, h - LAG)
                        if h == 0 and exists(b + 1):
                            transpose_tokens(b + 1, 1 - p)
                        if h in (2, 4) and exists(b - 1):
                            sum_values(b - 1, 1 - p, h // 2 - 1)
                        if h in (1, 3, 5, 6) and exists(b + 1):
                            project_queries(b + 1, 1 - p, (1, 3, 5, 6).index(h))
                    turn(b, NH - 2)
                    if exists(b + 1):
                        project_values(b + 1, 1 - p)
                    turn(b, NH - 1)

                def end():
                    for q in range(2):
                        sum_values(NB - 1, 1, q)

                each_batch(pe, start, body, end)

            @block.scalar
            def _(act):
                def tokens(b, p):
                    act.wait_ge(s["tr"], b + 1)
                    act.activation(ut[p][:, :], PS[:, A_BANK, 0:L], ACT.Copy).then_inc(s["ut"], 1)

                def queries(b, p, n):
                    act.wait_ge(s["tq_ps"], b * 4 + n + 1)
                    act.activation(tq[p][:, 2 * n:2 * n + 2, :].rearrange("p h c -> p (h c)"),
                                   PS[:, A_BANK, :], ACT.Copy).then_inc(s["tq"], 1)

                def start():
                    tokens(0, 0)
                    for n in range(4):
                        queries(0, 0, n)

                def body(b, k, p):
                    for h in range(NH):
                        act.wait_ge(s["mx"], b * NH + h + 1)
                        for q in range(2):
                            i = act.activation(pr[h % 4][:, q, :], PS[:, h % 4, q * L:(q + 1) * L], ACT.Exp,
                                               bias=nm[:, h, q:q + 1])
                        i.then_inc(s["exp"], 1)
                        if h == 0 and exists(b + 1):
                            tokens(b + 1, 1 - p)
                        if h in (1, 3, 5, 6) and exists(b + 1):
                            queries(b + 1, 1 - p, (1, 3, 5, 6).index(h))

                each_batch(act, start, body, lambda: None)

            @block.vector
            def _(dve):
                def normalize(b, p):
                    for h in range(2):
                        i = b * 2 + h
                        u = dve.tensor_scalar(us[p][:, h, :], t.H[:, i, :], t.MEAN[:, bass.ds(i, 1)],
                                              t.RSTD[:, bass.ds(i, 1)], ALU.subtract, ALU.mult)
                    u.then_inc(s["u"], 1)

                def values(b, p):
                    dve.wait_ge(s["v_ps"], b + 1)
                    dve.tensor_copy(v[p][:, :, :, 0:HD], PS[:, A_BANK, 0:2 * D].rearrange(
                        "q (j h d) -> q j h d", j=2, h=NH)).then_inc(s["v"], 1)

                def maxima(b, h):
                    dve.wait_ge(s["st_ps"], b * NH + h + 1)
                    dve.tensor_reduce(nm[:, h, :], PS[:, h % 4, :].rearrange("q (j c) -> q j c", j=2),
                                      AX.X, ALU.max, negate=True).then_inc(s["mx"], 1)

                def evict(b, p, h):
                    dve.wait_ge(s["pr_ps"], b * NH + h + 1)
                    dve.tensor_copy(pt[p][:, h].rearrange("q j c -> q (j c)"), PS[:, 4 + h % 2, :])\
                       .then_inc(s["pr"], 1)

                def add_attention(b):
                    dve.wait_ge(s["av_ps"], b * 2 + 2)
                    av = PS[:, SUMS, 0:2 * NH * HV].rearrange("q (j h e) -> q j h e", j=2, h=NH)
                    dve.reciprocal(rc[:, :, :], av[:, :, :, HD])
                    dve.drain()
                    dve.tensor_tensor(oc[:, :, :, :], av[:, :, :, 0:HD],
                                      rc[:, :, :].unsqueeze(3).broadcast_to([P, 2, NH, HD]), ALU.mult)\
                       .then_inc(s["norm"], 1)
                    dve.drain()
                    x = t.H[:, bass.ds(b * 2, 2), :]
                    dve.tensor_tensor(x, x, oc[:, :].rearrange("q j h d -> q j (h d)"), ALU.add)
                    dve.drain()
                    for q in range(2):
                        dve.bn_stats(t.BN[:, b * 2 + q, :], t.H[:, b * 2 + q, :])

                def start():
                    for b in range(2):
                        normalize(b, b)
                    values(0, 0)

                def body(b, k, p):
                    for h in range(NH):
                        maxima(b, h)
                        if h >= LAG:
                            evict(b, p, h - LAG)
                        if h == 6 and exists(b - 1):
                            add_attention(b - 1)
                    evict(b, p, NH - 2)
                    if exists(b + 1):
                        values(b + 1, 1 - p)
                    evict(b, p, NH - 1)
                    if exists(b + 2):
                        normalize(b + 2, p)

                each_batch(dve, start, body, lambda: add_attention(NB - 1))


def expert_choice(nc, t, a, out):
    ln_scales(nc, t, "ec_ln")
    rows = out.rearrange("b l c -> (b l) c")
    NG = EC // ECG
    with ExitStack() as ctx:
        def sb(n, shape, dt=F32):
            return ctx.enter_context(nc.sbuf_tensor(f"ec_{n}", shape, dt))

        s = Sems(nc, ctx, "ec", "weights staged tr tt logits exp_in exp probs turned in_rows picked picked_t idx "
                                "u_sent h_sent gathered0 gathered1 gathered2 gathered3 gathered4 gathered5 "
                                "gathered6 gathered7 xg_staged xtr xt up_ps hid out_ps y scattered freed "
                                "up0 up1 down0 down1 late")
        s.restart(nc)
        UD = nc.dram_tensor("ec_tokens", [NT * P, D], F32).ap()
        wr, br = sb("wr", [P, EC]), sb("br", [P, EC])
        bup, bdown = sb("bup", [P, NG, 3]), sb("bdown", [P, EC, D])
        vals_t, idx_t, idx_u = sb("vals_t", [P, EC]), sb("idx_t", [P, EC]), sb("idx_u", [P, EC], U32)
        PS = t.PS
        two = range(2)

        with ExitStack() as sub:
            def tb(n, shape, dt=F32):
                return sub.enter_context(nc.sbuf_tensor(f"ec_{n}", shape, dt))

            U = tb("u", [P, NT, D])
            stage, tt = [tb(f"st{i}", [P, D]) for i in two], [tb(f"tt{i}", [P, P]) for i in two]
            logits = PS[:, 2:4, :].rearrange("p a b -> p (a b)")
            LG, sm, row = tb("lg", [P, NT, EC]), tb("sm", [P, NT]), tb("row", [EC, NT * P])
            vals, idx, idxf = tb("vals", [EC, ECK]), tb("idx", [EC, ECK], U32), tb("idxf", [EC, ECK])

            with nc.Block() as block:

                @block.sync
                def _(sp):
                    sp.dma_start(wr[:, :], a["ec_wr"]).then_inc(s["weights"], 16)
                    sp.dma_start(br[:, :], a["ec_br"]).then_inc(s["weights"], 16)
                    sp.dma_start(bup[:, :, :], a["ec_bup"]).then_inc(s["late"], 16)
                    sp.dma_start(bdown[:, :, :], a["ec_bdown"]).then_inc(s["late"], 16)
                    sp.dma_start(rows.rearrange("(i p) c -> p i c", p=P), t.H[:, :, :]).then_inc(s["h_sent"], 16)
                    sp.wait_ge(s["staged"], NT)
                    sp.dma_start(UD.rearrange("(i p) c -> p i c", p=P), U[:, :, :]).then_inc(s["u_sent"], 16)
                    sp.wait_ge(s["u_sent"], 16)
                    sp.wait_ge(s["h_sent"], 16)
                    sp.wait_ge(s["late"], 32)

                @block.tensor
                def _(pe):
                    pe.wait_ge(s["weights"], 32)
                    pe.nop().then_inc(s["tr"], 2)
                    with pe.Fori(0, NT // 2) as k:
                        for p in two:
                            pe.wait_ge(s["staged"], k * 2 + p + 1)
                            pe.transpose(PS[:, p, 0:P], stage[p][:, :], t.ident[:, :]).then_inc(s["tr"], 1)
                        for p in two:
                            pe.wait_ge(s["tt"], k * 2 + p + 1)
                            pe.matmul(logits[:, bass.ds((k * 2 + p) * EC, EC)], tt[p][:, :], wr[:, :],
                                      start=True, stop=True)\
                              .then_inc(s["logits"], 1)
                    pe.wait_ge(s["probs"], 1)
                    for i in range(NT):
                        mm = pe.transpose(PS[0:EC, i // 4, (i % 4) * P:(i % 4 + 1) * P], LG[:, i, :], t.ident[:, :])
                        if i % 4 == 3:
                            mm.then_inc(s["turned"], 1)
                    pe.wait_ge(s["picked"], 1)
                    pe.transpose(PS[:, 0, 0:EC], vals[:, :], t.ident[0:EC, 0:EC])
                    pe.transpose(PS[:, 0, EC:2 * EC], idxf[:, :], t.ident[0:EC, 0:EC]).then_inc(s["picked_t"], 1)

                @block.scalar
                def _(act):
                    with act.Fori(0, NT // 2) as k:
                        for p in two:
                            act.wait_ge(s["tr"], k * 2 + p + 3)
                            act.activation(tt[p][:, :], PS[:, p, 0:P], ACT.Copy).then_inc(s["tt"], 1)
                    act.wait_ge(s["exp_in"], 1)
                    act.activation(LG[:, :, :], LG[:, :, :], ACT.Exp).then_inc(s["exp"], 1)

                @block.vector
                def _(dve):
                    dve.wait_ge(s["weights"], 32)
                    with dve.Fori(0, NT // 2) as k:
                        for p in two:
                            i = k * 2 + p
                            if p == 0:
                                dve.wait_ge(s["tr"], k * 2 + 2)
                            dve.tensor_scalar(U[:, i, :], t.H[:, i, :], t.MEAN[:, bass.ds(i, 1)],
                                              t.RSTD[:, bass.ds(i, 1)], ALU.subtract, ALU.mult)
                        dve.drain()
                        for p in two:
                            dve.tensor_copy(stage[p][:, :], U[:, k * 2 + p, :]).then_inc(s["staged"], 1)
                    dve.wait_ge(s["logits"], NT)
                    dve.tensor_tensor(LG[:, :, :], logits.rearrange("p (i e) -> p i e", e=EC),
                                      br[:, :].unsqueeze(1).broadcast_to([P, NT, EC]), ALU.add)
                    dve.drain()
                    dve.tensor_reduce(sm[:, :], LG[:, :, :], AX.X, ALU.max)
                    dve.drain()
                    over = sm[:, :].unsqueeze(2).broadcast_to([P, NT, EC])
                    dve.tensor_tensor(LG[:, :, :], LG[:, :, :], over, ALU.subtract).then_inc(s["exp_in"], 1)
                    dve.wait_ge(s["exp"], 1)
                    dve.tensor_reduce(sm[:, :], LG[:, :, :], AX.X, ALU.add)
                    dve.drain()
                    dve.reciprocal(sm[:, :], sm[:, :])
                    dve.drain()
                    dve.tensor_tensor(LG[:, :, :], LG[:, :, :], over, ALU.mult).then_inc(s["probs"], 1)
                    for b in range(8):
                        dve.wait_ge(s["turned"], b + 1)
                        dve.tensor_copy(row[:, b * 512:(b + 1) * 512], PS[0:EC, b, :])
                    dve.drain()
                    for r in range(ECK // 8):
                        v8 = vals[:, 8 * r:8 * r + 8]
                        dve.max(v8, row[:, :])
                        dve.drain()
                        dve.max_index(idx[:, 8 * r:8 * r + 8], v8, row[:, :])
                        dve.drain()
                        dve.match_replace(row[:, :], v8, row[:, :], -1.0)
                        dve.drain()
                    dve.tensor_copy(idxf[:, :], idx[:, :]).then_inc(s["picked"], 1)
                    dve.wait_ge(s["picked_t"], 1)
                    dve.tensor_copy(vals_t[:, :], PS[:, 0, 0:EC])
                    dve.tensor_copy(idx_u[:, :], PS[:, 0, EC:2 * EC])

        XG = sb("xg", [P, EC, D])
        wu = [sb(f"wu{i}", [P, ECF]) for i in two]
        wd = [sb(f"wd{i}", [P, ECG, 3, D]) for i in two]
        xg, xt = [sb(f"xgs{i}", [P, ECG, D]) for i in two], [sb(f"xt{i}", [P, ECG * P]) for i in two]
        hid = [sb(f"hid{i}", [P, 3, ECG * P]) for i in two]
        y = [sb(f"y{i}", [P, ECG, D]) for i in two]
        with nc.Block() as block:

            @block.sync
            def _(sp):
                with sp.Fori(0, NG // 2) as k:
                    for p in two:
                        g = k * 2 + p
                        sp.wait_ge(s["hid"], g * 3 + 3)
                        sp.dma_start(wu[p][:, :], a["ec_up"][bass.ds(g, 1)].rearrange("g h f -> h (g f)"))\
                          .then_inc(s[f"up{p}"], 16)
                        sp.wait_ge(s["out_ps"], g + 1)
                        down = a["ec_down"][bass.ds(g * ECG, ECG)]
                        for j, (f, n) in enumerate(ECT):
                            sp.dma_start(wd[p][0:n, :, j, :], down[:, f:f + n, :].rearrange("j f c -> f j c"))\
                              .then_inc(s[f"down{p}"], 16)

            @block.gpsimd
            def _(pool):
                def gather(e):
                    pool.indirect_dma_start(out=XG[:, e, :], out_offset=None, in_=UD,
                                            in_offset=bass.IndirectOffsetOnAxis(ap=idx_u[:, e:e + 1], axis=0))\
                        .then_inc(s[f"gathered{e // ECG}"], 16)

                def add(e):
                    if e:
                        pool.wait_ge(s["scattered"], 16 * e)
                        if e % ECG == 0:
                            pool.nop().then_inc(s["freed"], 1)
                    pool.wait_ge(s["y"], 2 + e // ECG + 1)
                    pool.indirect_dma_start(out=rows, out_offset=bass.IndirectOffsetOnAxis(ap=idx_u[:, e:e + 1], axis=0),
                                            in_=y[e // ECG % 2][:, e % ECG, :], in_offset=None,
                                            compute_op=ALU.add).then_inc(s["scattered"], 16)

                AHEAD = 3 * ECG
                pool.nop().then_inc(s["freed"], 2)
                for e in range(AHEAD):
                    gather(e)
                for e in range(EC):
                    add(e)
                    if e + AHEAD < EC:
                        gather(e + AHEAD)
                pool.wait_ge(s["scattered"], 16 * EC)

            @block.tensor
            def _(pe):
                pe.nop().then_inc(s["out_ps"], 2)
                with pe.Fori(0, NG // 2) as k:
                    for p in two:
                        g = k * 2 + p
                        pe.wait_ge(s["xg_staged"], g + 1)
                        for j in range(ECG):
                            mm = pe.transpose(PS[:, p, j * P:(j + 1) * P], xg[p][:, j, :], t.ident[:, :])
                        mm.then_inc(s["xtr"], 1)
                        pe.wait_ge(s["xt"], g + 1)
                        pe.wait_ge(s[f"up{p}"], k * 16 + 16)
                        for j, (f, n) in enumerate(ECT):
                            pe.wait_ge(s["hid"], g * 3 + j + 4)
                            pe.matmul(PS[0:n, 2 + j, :], wu[p][:, f:f + n], xt[p][:, :], start=True, stop=True)\
                              .then_inc(s["up_ps"], 1)
                        pe.wait_ge(s["hid"], g * 3 + 9)
                        pe.wait_ge(s[f"down{p}"], k * 48 + 48)
                        pe.wait_ge(s["y"], g + 1)
                        for e in range(ECG):
                            for j, (f, n) in enumerate(ECT):
                                mm = pe.matmul(PS[:, 5 + p, e * D:(e + 1) * D], hid[p][0:n, j, e * P:(e + 1) * P],
                                               wd[p][0:n, e, j, :], start=(j == 0), stop=(j == 2))
                        mm.then_inc(s["out_ps"], 1)

            @block.scalar
            def _(act):
                act.nop().then_inc(s["hid"], 6)
                with act.Fori(0, NG // 2) as k:
                    for p in two:
                        g = k * 2 + p
                        act.wait_ge(s["xtr"], g + 1)
                        act.activation(xt[p][:, :], PS[:, p, :], ACT.Copy).then_inc(s["xt"], 1)
                        for j, (f, n) in enumerate(ECT):
                            act.wait_ge(s["up_ps"], g * 3 + j + 1)
                            act.activation(hid[p][0:n, j, :], PS[0:n, 2 + j, :], ACT.Silu,
                                           bias=bup[0:n, bass.ds(g, 1), j]).then_inc(s["hid"], 1)

            @block.vector
            def _(dve):
                dve.nop().then_inc(s["y"], 2)
                for g in range(NG):
                    p = g % 2
                    dve.wait_ge(s[f"gathered{g}"], 16 * ECG)
                    dve.tensor_copy(xg[p][:, :, :], XG[:, g * ECG:(g + 1) * ECG, :])\
                       .then_inc(s["xg_staged"], 1)
                    dve.wait_ge(s["out_ps"], g + 3)
                    dve.wait_ge(s["freed"], g + 1)
                    dve.tensor_tensor(y[p][:, :, :], PS[:, 5 + p, :].rearrange("r (e c) -> r e c", e=ECG),
                                      bdown[:, g * ECG:(g + 1) * ECG, :], ALU.add)
                    dve.drain()
                    dve.tensor_tensor(y[p][:, :, :], y[p][:, :, :],
                                      vals_t[:, g * ECG:(g + 1) * ECG].unsqueeze(2).broadcast_to([P, ECG, D]),
                                      ALU.mult).then_inc(s["y"], 1)


def alloc_shared(nc, t, ctx):
    def sb(name, shape, dt=F32):
        return ctx.enter_context(nc.sbuf_tensor(name, shape, dt))

    t.H = sb("hidden", [P, NT, D])
    t.BN = sb("bn", [P, NT, 6])
    t.MEAN = sb("mean", [P, NT])
    t.RSTD = sb("rstd", [P, NT])
    t.ident = sb("ident", [P, P])
    t.toep = sb("toeplitz", [P, 2, P])
    t.ident16 = sb("ident16", [P, P], BF16)
    t.ln_sems, t.ln_uses = Sems(nc, ctx, "ln", "var_ready root_ready"), 0
    t.mha_sems = Sems(nc, ctx, "mha", ATTENTION_SEMS)
    t.moe_sems = Sems(nc, ctx, "moe", EXPERT_SEMS)
    t.PS = ctx.enter_context(nc.psum_tensor("psum", [P, 8, 512], F32))
    t.XS1 = nc.dram_tensor("expert_in1", [TILES1 * P, D], F32).ap()
    t.XS2 = nc.dram_tensor("expert_in2", [TILES2 * P, D], F32).ap()


def build(nc, a, out, upto=99):
    t = NS()
    with ExitStack() as ctx:
        alloc_shared(nc, t, ctx)
        with ExitStack() as tok:
            t.w1 = tok.enter_context(nc.sbuf_tensor("w1", [NF, 2, NHID * NF], F32))
            t.b1 = tok.enter_context(nc.sbuf_tensor("b1", [NF, NHID], F32))
            t.w2 = tok.enter_context(nc.sbuf_tensor("w2", [NF, NHID, D], F32))
            t.b2 = tok.enter_context(nc.sbuf_tensor("b2", [P, D], F32))
            t.dft = tok.enter_context(nc.sbuf_tensor("dft", [HP, 2, 2, NF], F32))
            setup(nc, t, a, tok)
            tokenizer(nc, t, a)
        def attention_and_experts():
            with ExitStack() as sub:
                t.R = sub.enter_context(nc.sbuf_tensor("attended", [P, NT, D], F32))
                full_attention(nc, t, a, "l0mha")
                experts_layer(nc, t, a, "l0moe")

        steps = [lambda: windowed_attention(nc, t, a, ctx),
                 attention_and_experts,
                 lambda: full_attention(nc, t, a, "l1mha"),
                 lambda: bitlinear_ffn(nc, t, a),
                 lambda: state_space(nc, t, a),
                 lambda: experts_layer(nc, t, a, "l2moe"),
                 lambda: bilinear_attention(nc, t, a),
                 lambda: expert_choice(nc, t, a, out)]
        for step in steps[:upto]:
            step()
        if upto < len(steps):
            with nc.semaphore("dump") as dump, nc.Block() as block:
                @block.sync
                def _(sp):
                    sp.dma_start(out.rearrange("b (h p) c -> p (b h) c", p=P), t.H[:, :, :]).then_inc(dump, 16)
                    sp.wait_ge(dump, 16)


def heads_inside(w):
    return w.reshape(w.shape[:-1] + (NH, HD)).swapaxes(-1, -2).reshape(w.shape)


def on_all(row):
    return np.ascontiguousarray(np.broadcast_to(row, (P,) + row.shape))


def constants():
    n = np.arange(PATCH)
    f = np.arange(NF)
    w = 2 * np.pi * ((n[:, None] * f[None, :]) % PATCH) / PATCH
    sin = np.where((f[None, :] * 2) % PATCH == 0, 0.0, np.sin(w))
    dft = np.stack([np.cos(w), -sin], 1).reshape(2, HP, 2, NF).transpose(1, 0, 2, 3)
    c = {"c_ident": np.eye(P), "c_dft": dft}
    win = np.arange(WT) // WIN
    blocks, win_sel = np.zeros((P, WT)), np.zeros((P, NH + 1, WT))
    for r in range(3 * NH):
        win_sel[r, r % NH] = 1
    for w_ in range(WT // WIN):
        blocks[32 + w_] = win == w_
        win_sel[32 + w_] = np.where(win == w_, 0.0, NEG)
    c["c_blocks"], c["c_win_sel"] = blocks, win_sel
    cnt = np.zeros(L)
    for w_ in range(NW):
        cnt[w_ * HOP:w_ * HOP + WIN] += 1
    c["c_cover"] = (cnt > 0).reshape(2, P).T
    c["c_share"] = (1.0 / np.maximum(cnt, 1)).reshape(2, P).T
    sel = np.zeros((P, NH, P))
    for r in range(3 * NH):
        sel[r, r % NH] = 1
    c["c_sel"] = sel
    c["c_before"] = np.triu(np.ones((P, P)), 1)
    c["c_order"] = np.broadcast_to((NE - np.arange(NE))[None, :, None], (P, NE, NT))
    c["c_chain"] = np.broadcast_to((np.arange(NT) > 0)[None, None, :], (P, NE, NT))
    q = np.sqrt(1 + 2 * np.arange(NSTATE))
    hippo = -(np.tril(q[:, None] * q[None, :]) - np.diag(np.arange(NSTATE)))
    c["c_hippo"] = np.stack([hippo, hippo.T], 1)
    c["c_hippo_inv_t"] = np.linalg.inv(hippo).T
    c["c_flip"] = np.eye(P)[::-1]
    return {k: np.ascontiguousarray(v, dtype=np.float32) for k, v in c.items()}


def arrays(i):
    a = dict(constants())
    a["x"] = i["x"]
    a["tok_w1"] = i["L0_tok_w1"].reshape(2, NF, NHID * NF).transpose(1, 0, 2)
    a["tok_b1"] = i["L0_tok_b1"].reshape(NHID, NF).T
    a["tok_w2"] = i["L0_tok_w2"].reshape(NHID, NF, D).transpose(1, 0, 2)
    a["tok_b2"] = on_all(i["L0_tok_b2"])
    w_in, b_in = i["L0_attn_w_in"], i["L0_attn_b_in"]
    a["win_gb"] = np.stack([i["L0_attn_ln_g"], i["L0_attn_ln_b"]], 1)

    def attention(name, wq, wk, wv, wo, bq, bk, bv, bo):
        a[name + "_wqk"] = np.stack([heads_inside(wq), heads_inside(wk)], 1)
        a[name + "_wvo"] = np.stack([wv, wo], 1)
        a[name + "_bqk"] = np.stack([heads_inside(bq), heads_inside(bk)], 1)
        a[name + "_bvo"] = on_all(np.stack([bv, bo]))

    attention("win", w_in[:D].T, w_in[D:2 * D].T, w_in[2 * D:].T, i["L0_attn_w_out"].T,
              b_in[:D], b_in[D:2 * D], b_in[2 * D:], i["L0_attn_b_out"])
    attention("l0mha", *(i["L0_ffn_" + n] for n in ("Wq", "Wk", "Wv", "Wo", "bq", "bk", "bv", "bo")))
    flat = [i["L1_attn_" + n].transpose(1, 0, 2).reshape(D, D) for n in ("Wq", "Wk", "Wv")]
    attention("l1mha", *flat, i["L1_attn_Wo"], *(i["L1_attn_" + n].reshape(D) for n in ("bq", "bk", "bv")),
              i["L1_attn_bo"])

    def moe(name, g, b, gate_w, gate_b, w1, b1, w2, b2):
        a[name + "_gb"] = np.stack([g, b], 1)
        a[name + "_gate_w"] = gate_w
        a[name + "_gate_b"] = on_all(gate_b)
        a[name + "_w1"] = np.concatenate(
            [w1.transpose(1, 0, 2), b1.reshape(NE, KF, P).transpose(2, 0, 1)], 2)
        a[name + "_w2"] = w2.reshape(NE, KF, P, D).transpose(2, 0, 1, 3)
        a[name + "_b2"] = on_all(b2)

    moe("l0moe", i["L0_ffn_ln1_g"], i["L0_ffn_ln1_b"], i["L0_ffn_gate_W"], i["L0_ffn_gate_b"],
        i["L0_ffn_W1"], i["L0_ffn_b1"], i["L0_ffn_W2"], i["L0_ffn_b2"])
    moe("l2moe", i["L2_ffn_ln_g"], i["L2_ffn_ln_b"], i["L2_ffn_w_r"].T, i["L2_ffn_b_r"],
        i["L2_ffn_W1"], i["L2_ffn_b1"], i["L2_ffn_W2"], i["L2_ffn_b2"])
    a["l0moe_gb"] = on_all(np.stack([i["L0_ffn_ln1_g"], i["L0_ffn_ln1_b"]]))
    a["l2moe_gb"] = on_all(np.stack([i["L2_ffn_ln_g"], i["L2_ffn_ln_b"]]))
    a["bit_up"] = i["L1_ffn_w_up"].T
    a["bit_down"] = i["L1_ffn_w_down"].T.reshape(KF, P, D).transpose(1, 0, 2)
    a["ssm_bc"] = np.stack([i["L2_attn_B_ssm"][:, 0], i["L2_attn_C_ssm"][0]], 1)
    a["ssm_d"] = on_all(i["L2_attn_D_skip"])
    a["ssm_log_dt"] = on_all(i["L2_attn_log_dt"])[:NSTATE]
    a["bil_q"] = i["L3_attn_Q"].transpose(1, 0, 2)
    a["bil_v"] = i["L3_attn_V"].transpose(1, 0, 2).reshape(D, D)
    a["ec_wr"] = i["L3_ffn_W_router"]
    a["ec_br"] = on_all(i["L3_ffn_b_router"])
    a["ec_up"] = i["L3_ffn_W_up"]
    pad = np.zeros((EC // ECG, 3 * P), np.float32)
    pad[:, :ECF] = i["L3_ffn_b_up"]
    a["ec_bup"] = pad.reshape(EC // ECG, 3, P).transpose(2, 0, 1)
    a["ec_down"] = i["L3_ffn_W_down"]
    a["ec_bdown"] = on_all(i["L3_ffn_b_down"])
    return {k: np.ascontiguousarray(v) for k, v in a.items()}


TILES1 = 40
TILES2 = 72


def kernel(**inputs):
    import concourse.bacc as bacc
    from concourse.bass_utils import run_bass_kernel_spmd

    given = arrays({k: np.asarray(v) for k, v in inputs.items()})
    nc = bacc.Bacc("TRN2", target_bir_lowering=False, num_devices=1)
    aps = {k: nc.dram_tensor(f"in_{k}", v.shape, mybir.dt.from_np(v.dtype), kind="ExternalInput").ap()
           for k, v in given.items()}
    out = nc.dram_tensor("out_0", (NB, L, D), F32, kind="ExternalOutput").ap()
    build(nc, aps, out)
    r = run_bass_kernel_spmd(nc, [{f"in_{k}": v for k, v in given.items()}], core_ids=[0])
    return r.results[0]["out_0"]
```

```python
from contextlib import ExitStack

import numpy as np
import concourse.bass as bass
from concourse import mybir
from concourse.alu_op_type import AluOpType as ALU

F32 = mybir.dt.float32
BF16 = mybir.dt.bfloat16
U32 = mybir.dt.uint32
I32 = mybir.dt.int32
ACT = mybir.ActivationFunctionType
AX = mybir.AxisListType

P = 128
NB = 16
L = 256
D = 128
NT = NB * L // P
NH, HD = 8, 16
HS = 32
PATCH, NPATCH, HP = 200, 4, 100
NF = PATCH // 2 + 1
NHID = 8
WIN, HOP = 20, 10
NW = (L - WIN) // HOP + 1
WT = 120
EPS = 1e-5
NE, FF = 8, 512
KF = FF // P
EC, ECF = 32, 341
ECK = NB * L // EC
ECG = 4
ECT = [(0, 128), (128, 128), (256, 85)]
NSTATE = 64
SQUARINGS = 12
MAGIC = 1.5 * 2.0 ** 23
NEG = -1e30
TINY = 1e-37


class NS:
    pass


def window_offset(w):
    return HOP * (w // 2) + WT * (w % 2)


class Sems:

    def __init__(self, nc, ctx, phase, names):
        self.s = {n: ctx.enter_context(nc.semaphore(f"{phase}_{n}")) for n in names.split()}

    def __getitem__(self, name):
        return self.s[name]

    def restart(self, nc):
        with nc.Block() as block:

            @block.gpsimd
            def _(pool):
                for sem in self.s.values():
                    pool.sem_clear(sem)


def ln_scales(nc, t, phase):
    with ExitStack() as ctx:
        s, n = t.ln_sems, t.ln_uses + 1
        t.ln_uses = n
        tmp = ctx.enter_context(nc.sbuf_tensor(f"{phase}_tmp", [P, 4, NT], F32))
        with nc.Block() as block:

            @block.vector
            def _(dve):
                me, mo = t.BN[:, :, 1], t.BN[:, :, 4]
                ve, vo = t.BN[:, :, 2], t.BN[:, :, 5]
                dve.tensor_tensor(tmp[:, 0], me, mo, ALU.subtract)
                dve.tensor_tensor(tmp[:, 1], ve, vo, ALU.add)
                dve.tensor_tensor(t.MEAN[:, :], me, mo, ALU.add)
                dve.drain()
                dve.tensor_tensor(tmp[:, 0], tmp[:, 0], tmp[:, 0], ALU.mult)
                dve.tensor_scalar(tmp[:, 1], tmp[:, 1], 1.0 / D, EPS, ALU.mult, ALU.add)
                dve.tensor_scalar(t.MEAN[:, :], t.MEAN[:, :], 0.5, None, ALU.mult)
                dve.drain()
                dve.scalar_tensor_tensor(tmp[:, 2], tmp[:, 0], 0.25, tmp[:, 1], ALU.mult, ALU.add)\
                   .then_inc(s["var_ready"], 1)
                dve.wait_ge(s["root_ready"], n)
                dve.reciprocal(t.RSTD[:, :], tmp[:, 3])
                dve.drain()
                dve.tensor_tensor(tmp[:, 0], t.RSTD[:, :], t.RSTD[:, :], ALU.mult)
                dve.drain()
                dve.tensor_tensor(tmp[:, 0], tmp[:, 0], tmp[:, 2], ALU.mult)
                dve.drain()
                dve.tensor_scalar(tmp[:, 0], tmp[:, 0], -0.5, 1.5, ALU.mult, ALU.add)
                dve.drain()
                dve.tensor_tensor(t.RSTD[:, :], t.RSTD[:, :], tmp[:, 0], ALU.mult)

            @block.scalar
            def _(act):
                act.wait_ge(s["var_ready"], n)
                act.activation(tmp[:, 3], tmp[:, 2], ACT.Sqrt).then_inc(s["root_ready"], 1)


def setup(nc, t, a, ctx):
    s = Sems(nc, ctx, "setup", "loaded matrices scratch_zeroed")
    t.setup_sems = s
    t.zero = ctx.enter_context(nc.sbuf_tensor("zero_tile", [P, 2048], F32))
    loads = [(t.ident, a["c_ident"]), (t.dft, a["c_dft"]), (t.b1, a["tok_b1"]), (t.b2, a["tok_b2"])]
    with nc.Block() as block:

        @block.sync
        def _(sp):
            for dst, src in loads:
                sp.dma_start(dst[tuple(slice(None) for _ in dst.shape)], src).then_inc(s["loaded"], 16)
            sp.wait_ge(s["loaded"], 16 * len(loads))

        @block.vector
        def _(dve):
            dve.memset(t.zero[:, :], 0.0)
            dve.wait_ge(s["loaded"], 16 * len(loads))
            dve.tensor_copy(t.ident16[:, :], t.ident[:, :])

        @block.scalar
        def _(act):
            act.wait_ge(s["loaded"], 16 * len(loads))
            act.dma_start(t.w1[:, :, :], a["tok_w1"]).then_inc(s["matrices"], 16)
            act.dma_start(t.w2[:, :, :], a["tok_w2"]).then_inc(s["matrices"], 16)


def zero_scratch(t, act, sem):
    n = 0
    for buf in (t.XS1, t.XS2):
        rows = buf.rearrange("(p r) c -> p (r c)", p=P)
        for c in range(0, rows.shape[1], 2048):
            m = min(2048, rows.shape[1] - c)
            act.dma_start(rows[:, c:c + m], t.zero[:, 0:m]).then_inc(sem, 16)
            n += 16
    return n


def tokenizer(nc, t, a):
    N = 2 * L
    with ExitStack() as ctx:
        def sb(name, shape, dt=F32):
            return ctx.enter_context(nc.sbuf_tensor(f"tok_{name}", shape, dt))

        s = Sems(nc, ctx, "tok", "w1_doubled padded loaded0 loaded1 tr xt dft squares sum mag ratio atan feat "
                                 "hid_ps hid out_ps stored")
        rows = [sb(f"rows{i}", [P, 2 * NPATCH * HP]) for i in range(2)]
        xt = [sb(f"xt{i}", [HP, 2, P, NPATCH]) for i in range(2)]
        feat = [sb(f"feat{i}", [NF, 2, N]) for i in range(2)]
        sq = [sb(f"sq{i}", [NF, 2, N]) for i in range(2)]
        den = [sb(f"den{i}", [NF, N]) for i in range(2)]
        rat = [sb(f"rat{i}", [NF, N]) for i in range(2)]
        at = [sb(f"at{i}", [NF, N]) for i in range(2)]
        hid = [sb(f"hid{i}", [NF, NHID, N]) for i in range(2)]
        T = a["x"].shape[2]
        x_rows = a["x"].rearrange("b c t -> (b c) t")
        PS = t.PS

        STEPS = NB // 2

        def each_step(eng, first, body, last):
            first()
            for i in range(2):
                body(i, 0, i)
            with eng.Fori(1, STEPS // 2 - 1) as k:
                for p in range(2):
                    body(k * 2 + p, k, p)
            for i in range(STEPS - 2, STEPS):
                body(i, i // 2, i % 2)
            last()

        def there(i):
            return not isinstance(i, int) or 0 <= i < STEPS

        with nc.Block() as block:

            @block.sync
            def _(sp):
                def load(i, k, p):
                    if there(i - 2):
                        sp.wait_ge(s["tr"], i - 1)
                    sp.dma_start(rows[p][:, 0:T], x_rows[bass.ds(i * P, P), :]).then_inc(s[f"loaded{p}"], 16)

                each_step(sp, lambda: sp.wait_ge(s["padded"], 2), load, lambda: None)

            @block.tensor
            def _(pe):
                def turn(i, k, p):
                    pe.wait_ge(s[f"loaded{p}"], k * 16 + 16)
                    for j in range(2 * NPATCH):
                        mm = pe.transpose(PS[0:HP, j % 2, (j // 2) * P:(j // 2 + 1) * P],
                                          rows[p][:, j * HP:(j + 1) * HP], t.ident[:, :])
                    mm.then_inc(s["tr"], 1)

                def spectrum(i, p):
                    pe.wait_ge(s["xt"], i + 1)
                    if there(i - 1):
                        pe.wait_ge(s["feat"], i)
                    for part in range(2):
                        for half in range(2):
                            mm = pe.matmul(PS[0:NF, 2 + part, :], t.dft[:, half, part, :],
                                           xt[p][:, half].rearrange("h q s -> h (q s)"),
                                           start=(half == 0), stop=(half == 1))
                    mm.then_inc(s["dft"], 1)

                def up(i, p, m):
                    if m == 0:
                        pe.wait_ge(s["feat"], i + 1)
                    if m >= 2 or there(i - 1):
                        pe.wait_ge(s["hid"], i * NHID + m - 1)
                    for f in range(2):
                        mm = pe.matmul(PS[0:NF, 4 + m % 2, :], t.w1[:, f, m * NF:(m + 1) * NF],
                                       feat[p][:, f, :], start=(f == 0), stop=(f == 1))
                    mm.then_inc(s["hid_ps"], 1)

                def down(i, p):
                    pe.wait_ge(s["hid"], i * NHID + NHID)
                    if there(i - 2):
                        pe.wait_ge(s["stored"], i - 1)
                    for q in range(4):
                        for m in range(NHID):
                            mm = pe.matmul(PS[:, 6 + p, q * D:(q + 1) * D],
                                           hid[p][:, m, q * P:(q + 1) * P], t.w2[:, m, :],
                                           start=(m == 0), stop=(m == NHID - 1))
                    mm.then_inc(s["out_ps"], 1)

                def start():
                    turn(0, 0, 0)
                    spectrum(0, 0)
                    pe.wait_ge(s["w1_doubled"], 1)

                def body(i, k, p):
                    if there(i + 1):
                        turn(i + 1, k + p, 1 - p)
                    for m in range(NHID):
                        up(i, p, m)
                        if m == 1:
                            if there(i + 1):
                                spectrum(i + 1, 1 - p)
                            if there(i - 1):
                                down(i - 1, 1 - p)

                each_step(pe, start, body, lambda: down(STEPS - 1, 1))

            @block.scalar
            def _(act):
                zeroed = [0]

                def magnitude(i, p):
                    act.wait_ge(s["dft"], i + 1)
                    act.activation(den[p][:, :], PS[0:NF, 2, :], ACT.Abs)
                    act.activation(sq[p][:, 0], PS[0:NF, 2, :], ACT.Square)
                    act.activation(sq[p][:, 1], PS[0:NF, 3, :], ACT.Square).then_inc(s["squares"], 1)
                    act.wait_ge(s["sum"], i + 1)
                    act.activation(feat[p][:, 0], sq[p][:, 0], ACT.Sqrt).then_inc(s["mag"], 1)

                def angle(i, p):
                    act.wait_ge(s["ratio"], i + 1)
                    act.activation(at[p][:, :], rat[p][:, :], ACT.Arctan).then_inc(s["atan"], 1)

                def start():
                    magnitude(0, 0)
                    angle(0, 0)
                    zeroed[0] = zero_scratch(t, act, t.setup_sems["scratch_zeroed"])

                def body(i, k, p):
                    for m in range(NHID):
                        act.wait_ge(s["hid_ps"], i * NHID + m + 1)
                        act.activation(hid[p][:, m], PS[0:NF, 4 + m % 2, :], ACT.Gelu,
                                       bias=t.b1[:, m:m + 1]).then_inc(s["hid"], 1)
                        if m == 1 and there(i + 1):
                            magnitude(i + 1, 1 - p)
                        if m == 3 and there(i + 1):
                            angle(i + 1, 1 - p)

                each_step(act, start, body, lambda: act.wait_ge(t.setup_sems["scratch_zeroed"], zeroed[0]))

            @block.vector
            def _(dve):
                re, im = PS[0:NF, 2, :], PS[0:NF, 3, :]

                def ratio(i, p):
                    dve.wait_ge(s["tr"], i + 1)
                    for half in range(2):
                        c = dve.tensor_copy(xt[p][:, half].rearrange("h q s -> h s q"),
                                            PS[0:HP, half, :].rearrange("h (s q) -> h s q", s=NPATCH))
                    c.then_inc(s["xt"], 1)
                    dve.wait_ge(s["squares"], i + 1)
                    dve.tensor_tensor(sq[p][:, 0], sq[p][:, 0], sq[p][:, 1], ALU.add).then_inc(s["sum"], 1)
                    dve.wait_ge(s["mag"], i + 1)
                    dve.tensor_tensor(den[p][:, :], den[p][:, :], feat[p][:, 0], ALU.add)
                    dve.drain()
                    dve.tensor_scalar(den[p][:, :], den[p][:, :], TINY, None, ALU.max)
                    dve.drain()
                    dve.reciprocal(den[p][:, :], den[p][:, :])
                    dve.drain()
                    dve.tensor_tensor(rat[p][:, :], im, den[p][:, :], ALU.mult).then_inc(s["ratio"], 1)
                    dve.tensor_scalar(sq[p][:, 1], im, 0.0, -0.5, ALU.is_ge, ALU.add)
                    dve.drain()

                def angle(i, p):
                    dve.wait_ge(s["atan"], i + 1)
                    dve.scalar_tensor_tensor(sq[p][:, 0], at[p][:, :], -2.0 / np.pi, sq[p][:, 1],
                                             ALU.mult, ALU.add)
                    dve.drain()
                    dve.scalar_tensor_tensor(sq[p][:, 1], re, 0.0, sq[p][:, 0], ALU.is_lt, ALU.mult)
                    dve.drain()
                    dve.scalar_tensor_tensor(feat[p][:, 1], sq[p][:, 1], float(np.pi), at[p][:, :],
                                             ALU.mult, ALU.add).then_inc(s["feat"], 1)

                def store(i, p):
                    dve.wait_ge(s["out_ps"], i + 1)
                    dve.tensor_tensor(t.H[:, bass.ds(i * 4, 4), :],
                                      PS[:, 6 + p, :].rearrange("p (q c) -> p q c", q=4),
                                      t.b2[:, :].unsqueeze(1).broadcast_to([P, 4, D]), ALU.add)\
                       .then_inc(s["stored"], 1)
                    dve.drain()
                    for q in range(4):
                        dve.bn_stats(t.BN[:, i * 4 + q, :], t.H[:, i * 4 + q, :])

                def start():
                    for p in range(2):
                        dve.memset(rows[p][:, T:], 0.0).then_inc(s["padded"], 1)
                    ratio(0, 0)
                    dve.wait_ge(t.setup_sems["matrices"], 32)
                    dve.tensor_scalar(t.w1[:, 1, :], t.w1[:, 1, :], 2.0, None, ALU.mult)\
                       .then_inc(s["w1_doubled"], 1)
                    angle(0, 0)

                def body(i, k, p):
                    if there(i + 1):
                        ratio(i + 1, 1 - p)
                        angle(i + 1, 1 - p)
                    if there(i - 1):
                        store(i - 1, 1 - p)

                each_step(dve, start, body, lambda: store(STEPS - 1, 1))


def second_norm(nc, t):
    with nc.Block() as block:

        @block.vector
        def _(dve):
            with dve.Fori(0, NT // 8) as k:
                for p in range(8):
                    i = k * 8 + p
                    dve.tensor_scalar(t.U[:, i, :], t.H[:, i, :], t.MEAN[:, bass.ds(i, 1)],
                                      t.RSTD[:, bass.ds(i, 1)], ALU.subtract, ALU.mult)
                dve.drain()
                for p in range(8):
                    dve.bn_stats(t.BN[:, k * 8 + p, :], t.U[:, k * 8 + p, :])


def load_all(block, pairs, sem):
    @block.sync
    def _(sp):
        for dst, src in pairs:
            sp.dma_start(dst[tuple(slice(None) for _ in dst.shape)], src).then_inc(sem, 16)
        sp.wait_ge(sem, 16 * len(pairs))


def attention_weights(nc, ctx, a, name):
    w = NS()

    def sb(n, shape):
        return ctx.enter_context(nc.sbuf_tensor(f"{name}_{n}", shape, F32))

    w.wqk, w.wvo = sb("wqk", [P, 2, P]), sb("wvo", [P, 2, D])
    w.bqk, w.bvo = sb("bqk", [P, 2]), sb("bvo", [P, 2, D])
    w.loads = [(w.wqk, a[name + "_wqk"]), (w.wvo, a[name + "_wvo"]),
               (w.bqk, a[name + "_bqk"]), (w.bvo, a[name + "_bvo"])]
    return w


def attention_prelude(nc, t, s, nms, zero, values, loads):
    with nc.Block() as block:
        load_all(block, loads, s["weights"])

        @block.vector
        def _(dve):
            if nms is not None:
                dve.memset(nms[tuple(slice(None) for _ in nms.shape)], 0.0)
                dve.memset(zero[:, :], 0.0)
            for p in range(2):
                dve.memset(values[p][:, :, :, :], 0.0)
            dve.drain()
            for p in range(2):
                dve.memset(values[p][:, :, :, HD:HD + 1], 1.0)


QUERY_PARTS = (0, 0, 1, 1, 0, 2)
KEY_PARTS = (0, 1, 0, 1, 2, 0)
STACK = 6 * HD
STACK_DMAS = 2 * 6 * 16


ATTENTION_SEMS = ("weights made u tr ut qk_ps qk parts base stacks0 stacks1 v_ps v st_ps mx nms nt_ps mt "
                  "stt_ps exp av_ps norm ot_ps ot out_ps "
                  "added sums turned")


def each_batch(eng, first, body, last):
    first()
    for b in range(2):
        body(b, 0, b)
    with eng.Fori(1, NB // 2 - 2) as k:
        for p in range(2):
            body(k * 2 + p, k, p)
    for b in range(NB - 4, NB):
        body(b, b // 2, b % 2)
    last()


def exists(b):
    return not isinstance(b, int) or 0 <= b < NB


def windowed_attention(nc, t, a, ctx):
    ln_scales(nc, t, "ln_a")
    with ExitStack() as sub:
        def sb(name, shape, dt=F32):
            return sub.enter_context(nc.sbuf_tensor(f"win_{name}", shape, dt))

        t.U = sb("u", [P, NT, D])
        second_norm(nc, t)
        ln_scales(nc, t, "ln_b")
        SEG = nc.dram_tensor("window_out", [NB * NW * WIN, D], F32).ap()
        with ExitStack() as loop:
            def lb(name, shape, dt=F32):
                return loop.enter_context(nc.sbuf_tensor(f"win_{name}", shape, dt))

            s = Sems(nc, loop, "win", ATTENTION_SEMS + " stored sent0 sent1")
            w = attention_weights(nc, loop, a, "win")
            two = range(2)
            gb, cover = lb("gb", [P, 2]), lb("cover", [P, 2])
            us, own = [lb(f"us{i}", [P, 2, D]) for i in two], [lb(f"own{i}", [P, L]) for i in two]
            ut, qk = [lb(f"ut{i}", [P, L]) for i in two], [lb(f"qk{i}", [P, 2, L]) for i in two]
            parts, rest = [lb(f"parts{i}", [P, 3, 2, L], BF16) for i in two], lb("rest", [P, 2, L])
            qs = [lb(f"qs{i}", [STACK, NH, L], BF16) for i in two]
            ks = [lb(f"ks{i}", [STACK, NH, L], BF16) for i in two]
            v = [lb(f"v{i}", [WT, 4, NH, HS]) for i in two]
            st = lb("st", [P, 2, 4 * WT])
            nm, nmrest, nms = lb("nm", [WT, 4, NH]), lb("nmrest", [WT, 4, NH]), lb("nms", [WT, 4, P], BF16)
            zero = lb("zero", [P, 1])
            mt, blocks, blocksf = lb("mt", [P, 4, WT], BF16), lb("blocks", [P, 4, WT], BF16), lb("blocksf", [P, WT])
            pt = lb("pt", [WT, NH, 4, WT])
            rc, oc, ot = lb("rc", [WT, 4, NH]), lb("oc", [WT, 4, NH, HD]), lb("ot", [P, 4, WT])
            sg = [lb(f"sg{i}", [WT, 4, D]) for i in two]
            self_, sel = lb("self", [P, NH + 1, WT]), lb("sel", [P, NH + 1, WT], BF16)
            attention_prelude(nc, t, s, nms, zero, v, w.loads + [(gb, a["win_gb"]),
                                                           (cover, a["c_cover"]), (self_, a["c_win_sel"]),
                                                           (blocksf, a["c_blocks"])])
            PS = t.PS

            with nc.Block() as block:

                @block.tensor
                def _(pe):
                    def transpose_tokens(b, p):
                        pe.wait_ge(s["u"], b + 1)
                        if exists(b - 2):
                            pe.wait_ge(s["v"], b - 1)
                        for h in range(2):
                            mm = pe.transpose(PS[:, 4 + p, h * P:(h + 1) * P], us[p][:, h, :], t.ident[:, :])
                        mm.then_inc(s["tr"], 1)

                    def project_queries_keys(b, p):
                        pe.wait_ge(s["ut"], b + 1)
                        for g in range(2):
                            mm = pe.matmul(PS[:, 4 + p, g * L:(g + 1) * L], w.wqk[:, g, :], ut[p][:, :],
                                           start=True, stop=True)
                        mm.then_inc(s["qk_ps"], 1)

                    def project_values(b, p):
                        pe.wait_ge(s["qk"], b + 1)
                        for j in range(4):
                            o = window_offset(j)
                            mm = pe.matmul(PS[0:WT, 4 + p, j * D:(j + 1) * D], ut[p][:, o:o + WT],
                                           w.wvo[:, 0, :], start=True, stop=True)
                        mm.then_inc(s["v_ps"], 1)

                    def scores(n, row, shift, stationary, moving):
                        for h in range(2):
                            bank = 2 * (n % 2) + h
                            pe.matmul(PS[0:WT, bank, 0:4 * WT], sel[:, row(2 * n + h), :],
                                      shift[:, :, :].rearrange("p j c -> p (j c)"), start=True, stop=False)
                            for j in range(4):
                                o = window_offset(j)
                                mm = pe.matmul(PS[0:WT, bank, j * WT:(j + 1) * WT],
                                               stationary[:, 2 * n + h, o:o + WT],
                                               moving[:, 2 * n + h, o:o + WT], start=False, stop=(j == 3))
                        return mm

                    def row_scores(b, p, n):
                        if n < 2:
                            pe.wait_ge(s["exp"], b * 4 + 3 + n)
                        else:
                            pe.wait_ge(s["mx"], b * 4 + n - 1)
                        scores(n, lambda h: NH, blocks, qs[p], ks[p]).then_inc(s["st_ps"], 1)

                    def column_scores(b, p, n):
                        if n < 2:
                            pe.wait_ge(s["mx"], b * 4 + 3 + n)
                        else:
                            pe.wait_ge(s["exp"], b * 4 + 3 + n)
                        scores(n, lambda h: h, mt, ks[p], qs[p]).then_inc(s["stt_ps"], 1)

                    def sum_values(b, p, g):
                        if g == 0:
                            pe.wait_ge(s["exp"], b * 4 + 8)
                            pe.wait_ge(s["v"], b + 1)
                            if exists(b - 1):
                                pe.wait_ge(s["stored"], b)
                        for j in range(4):
                            for i in range(4):
                                mm = pe.matmul(PS[HS * i:HS * i + HS, 6 + g, j * WT:(j + 1) * WT],
                                               v[p][:, j, 4 * g + i, :], pt[:, 4 * g + i, j, :],
                                               start=True, stop=True)
                        mm.then_inc(s["av_ps"], 1)

                    def turn_sums(b):
                        pe.wait_ge(s["sums"], b + 1)
                        for j in range(4):
                            for g in range(2):
                                o = (j % 2 * 2 + g) * P
                                mm = pe.transpose(PS[0:WT, 6 + j // 2, o:o + P], st[:, g, j * WT:(j + 1) * WT],
                                                  t.ident[:, :])
                        mm.then_inc(s["turned"], 1)

                    def transpose_sums(b):
                        pe.wait_ge(s["norm"], b + 1)
                        for j in range(4):
                            mm = pe.transpose(PS[:, 6, j * WT:(j + 1) * WT],
                                              oc[:, j].rearrange("q h d -> q (h d)"), t.ident[0:WT, 0:WT])
                        mm.then_inc(s["ot_ps"], 1)

                    def project_output(b, p):
                        pe.wait_ge(s["ot"], b + 1)
                        for j in range(4):
                            o = window_offset(j)
                            pe.matmul(PS[0:WT, 7, j * D:(j + 1) * D], ot[:, j, :], w.wvo[:, 1, :],
                                      start=True, stop=False)
                            mm = pe.matmul(PS[0:WT, 7, j * D:(j + 1) * D], own[p][:, o:o + WT], t.ident[:, :],
                                           start=False, stop=True)
                        mm.then_inc(s["out_ps"], 1)

                    def transpose_maxima(b, p):
                        pe.wait_ge(s["nms"], b + 1)
                        if exists(b + 1):
                            pe.wait_ge(s["qk"], b + 2)
                        for j in range(4):
                            mm = pe.transpose(PS[:, 5 - p, j * (WT // 2):(j + 1) * (WT // 2)].bitcast(BF16),
                                              nms[:, j, :], t.ident16[0:WT, 0:WT])
                        mm.then_inc(s["nt_ps"], 1)

                    def start():
                        pe.wait_ge(s["made"], 1)
                        for b in range(2):
                            transpose_tokens(b, b)
                            project_queries_keys(b, b)
                        project_values(0, 0)

                    def body(b, k, p):
                        pe.wait_ge(s[f"stacks{p}"], k * STACK_DMAS + STACK_DMAS)
                        for n in range(2):
                            row_scores(b, p, n)
                        if exists(b + 2):
                            transpose_tokens(b + 2, p)
                        row_scores(b, p, 2)
                        if exists(b - 1):
                            sum_values(b - 1, 1 - p, 0)
                        row_scores(b, p, 3)
                        if exists(b - 1):
                            sum_values(b - 1, 1 - p, 1)
                        if exists(b + 2):
                            project_queries_keys(b + 2, p)
                        if exists(b - 1):
                            turn_sums(b - 1)
                        transpose_maxima(b, p)
                        pe.wait_ge(s["mt"], b + 1)
                        column_scores(b, p, 0)
                        if exists(b - 1):
                            transpose_sums(b - 1)
                        column_scores(b, p, 1)
                        if exists(b + 1):
                            project_values(b + 1, 1 - p)
                        column_scores(b, p, 2)
                        if exists(b - 1):
                            project_output(b - 1, 1 - p)
                        column_scores(b, p, 3)

                    def end():
                        for g in range(2):
                            sum_values(NB - 1, 1, g)
                        turn_sums(NB - 1)
                        transpose_sums(NB - 1)
                        project_output(NB - 1, 1)

                    each_batch(pe, start, body, end)

                @block.scalar
                def _(act):
                    def tokens(b, p):
                        act.wait_ge(s["tr"], b + 1)
                        act.activation(ut[p][:, :], PS[:, 4 + p, 0:L], ACT.Identity, scale=gb[:, 0:1],
                                       bias=gb[:, 1:2]).then_inc(s["ut"], 1)

                    def queries_keys(b, p):
                        act.wait_ge(s["qk_ps"], b + 1)
                        for g in range(2):
                            i = act.activation(qk[p][:, g, :], PS[:, 4 + p, g * L:(g + 1) * L],
                                               ACT.Identity, bias=w.bqk[:, g:g + 1])
                        i.then_inc(s["qk"], 1)

                    def sums(b):
                        act.wait_ge(s["ot_ps"], b + 1)
                        act.activation(ot[:, :, :].rearrange("p j c -> p (j c)"),
                                       PS[:, 6, 0:4 * WT], ACT.Copy).then_inc(s["ot"], 1)

                    def rows_out(b, p, k):
                        act.wait_ge(s["out_ps"], b + 1)
                        if exists(b - 2):
                            act.wait_ge(s[f"sent{p}"], k * 64)
                        act.activation(sg[p][:, :, :].rearrange("q j c -> q (j c)"),
                                       PS[0:WT, 7, :], ACT.Copy).then_inc(s["stored"], 1)

                    def start():
                        act.nop().then_inc(s["exp"], 4)
                        act.wait_ge(s["made"], 1)
                        for b in range(2):
                            tokens(b, b)
                            queries_keys(b, b)

                    def evict_sums(b):
                        act.wait_ge(s["av_ps"], b * 2 + 2)
                        for g in range(2):
                            i = act.activation(st[:, g, :], PS[:, 6 + g, 0:4 * WT], ACT.Copy)
                        i.then_inc(s["sums"], 1)

                    def body(b, k, p):
                        act.activation(own[p][:, :], ut[p][:, :], ACT.Copy)
                        act.drain()
                        if exists(b + 2):
                            tokens(b + 2, p)
                        if exists(b - 1):
                            evict_sums(b - 1)
                        if exists(b + 2):
                            queries_keys(b + 2, p)
                        act.wait_ge(s["nt_ps"], b + 1)
                        act.activation(mt[0:32, :, :].rearrange("p j c -> p (j c)"),
                                       PS[0:32, 5 - p, 0:2 * WT].bitcast(BF16), ACT.Copy).then_inc(s["mt"], 1)
                        for n in range(4):
                            act.wait_ge(s["stt_ps"], b * 4 + n + 1)
                            bank = 2 * (n % 2)
                            act.activation(pt[:, 2 * n:2 * n + 2].rearrange("q h j c -> q h (j c)"),
                                           PS[0:WT, bank:bank + 2, 0:4 * WT], ACT.Exp, scale=HD ** -0.5)\
                               .then_inc(s["exp"], 1)
                            if n == 0 and exists(b - 1):
                                sums(b - 1)
                        if exists(b - 1):
                            rows_out(b - 1, 1 - p, k - 1 if p == 0 else k)

                    def end():
                        evict_sums(NB - 1)
                        sums(NB - 1)
                        rows_out(NB - 1, 1, NB // 2 - 1)

                    each_batch(act, start, body, end)

                @block.gpsimd
                def _(pool):
                    zeros = zero[:, :].unsqueeze(2).broadcast_to([P, 2, L])

                    def cut(b, p):
                        pool.wait_ge(s["qk"], b + 1)
                        pool.tensor_tensor(parts[p][:, 0], qk[p][:, :, :], zeros, ALU.add)
                        pool.drain()
                        pool.tensor_tensor(rest[:, :, :], qk[p][:, :, :], parts[p][:, 0], ALU.subtract)
                        pool.drain()
                        pool.tensor_tensor(parts[p][:, 1], rest[:, :, :], zeros, ALU.add)
                        pool.drain()
                        pool.tensor_tensor(parts[p][:, 2], rest[:, :, :], parts[p][:, 1], ALU.subtract)\
                            .then_inc(s["parts"], 1)

                    def start():
                        for b in range(2):
                            cut(b, b)

                    def body(b, k, p):
                        if exists(b + 2):
                            cut(b + 2, p)

                    each_batch(pool, start, body, lambda: None)

                @block.sync
                def _(sp):
                    def stack(b, p):
                        sp.wait_ge(s["parts"], b + 1)
                        if exists(b - 2):
                            sp.wait_ge(s["stt_ps"], b * 4 - 4)
                        for g in range(6):
                            rows = slice(g * HD, (g + 1) * HD)
                            sp.dma_start(qs[p][rows, :, :], parts[p][:, QUERY_PARTS[g], 0, :])\
                              .then_inc(s[f"stacks{p}"], 16)
                            sp.dma_start(ks[p][rows, :, :], parts[p][:, KEY_PARTS[g], 1, :])\
                              .then_inc(s[f"stacks{p}"], 16)

                    def store(b, p):
                        sp.wait_ge(s["stored"], b + 1)
                        for j in range(4):
                            base = b * (NW * WIN) + (j % 2) * 2 * WT
                            rows = SEG[bass.ds(base, 2 * WT), :].rearrange(
                                "(i o w) c -> o i w c", o=2, w=WIN)[j // 2]
                            sp.dma_start(rows, sg[p][:, j, :]).then_inc(s[f"sent{p}"], 16)

                    def body(b, k, p):
                        if exists(b + 1):
                            stack(b + 1, 1 - p)
                        if exists(b - 2):
                            store(b - 2, p)

                    def end():
                        store(NB - 2, 0)
                        store(NB - 1, 1)
                        for p in range(2):
                            sp.wait_ge(s[f"sent{p}"], 64 * NB // 2)

                    each_batch(sp, lambda: stack(0, 0), body, end)

                @block.vector
                def _(dve):
                    def normalize(b, p):
                        for h in range(2):
                            i = b * 2 + h
                            u = dve.tensor_scalar(us[p][:, h, :], t.U[:, i, :], t.MEAN[:, bass.ds(i, 1)],
                                                  t.RSTD[:, bass.ds(i, 1)], ALU.subtract, ALU.mult)
                        u.then_inc(s["u"], 1)
                        for h in range(2):
                            x = t.H[:, b * 2 + h, :]
                            dve.scalar_tensor_tensor(x, w.bvo[:, 1, :], cover[:, h:h + 1], x, ALU.mult, ALU.add)

                    def values(b, p):
                        dve.wait_ge(s["v_ps"], b + 1)
                        i = dve.tensor_tensor(
                            v[p][:, :, :, 0:HD],
                            PS[0:WT, 4 + p, :].rearrange("q (j h d) -> q j h d", j=4, h=NH),
                            w.bvo[0:WT, 0, :].rearrange("q (h d) -> q h d", h=NH).unsqueeze(1)
                             .broadcast_to([WT, 4, NH, HD]), ALU.add)
                        i.then_inc(s["v"], 1)

                    def maxima(b, n):
                        dve.wait_ge(s["st_ps"], b * 4 + n + 1)
                        bank = 2 * (n % 2)
                        dve.tensor_reduce(nm[:, :, 2 * n:2 * n + 2].rearrange("q j i -> q i j"),
                                          PS[0:WT, bank:bank + 2, 0:4 * WT].rearrange("q i (j c) -> q i j c", j=4),
                                          AX.X, ALU.max, negate=True).then_inc(s["mx"], 1)

                    def cut_maxima():
                        dve.drain()
                        dve.tensor_copy(nms[:, :, 0:NH], nm[:, :, :])
                        dve.drain()
                        dve.tensor_tensor(nmrest[:, :, :], nm[:, :, :], nms[:, :, 0:NH], ALU.subtract)
                        dve.drain()
                        dve.tensor_copy(nms[:, :, NH:2 * NH], nmrest[:, :, :])
                        dve.drain()
                        dve.tensor_tensor(nms[:, :, 2 * NH:3 * NH], nmrest[:, :, :], nms[:, :, NH:2 * NH],
                                          ALU.subtract).then_inc(s["nms"], 1)

                    def divide(b):
                        dve.wait_ge(s["turned"], b + 1)
                        for y in range(2):
                            av = PS[0:WT, 6 + y, :].rearrange("q (j h e) -> q j h e", j=2, h=NH)
                            dve.reciprocal(rc[:, 2 * y:2 * y + 2, :], av[:, :, :, HD])
                        dve.drain()
                        for y in range(2):
                            av = PS[0:WT, 6 + y, :].rearrange("q (j h e) -> q j h e", j=2, h=NH)
                            i = dve.tensor_tensor(oc[:, 2 * y:2 * y + 2], av[:, :, :, 0:HD],
                                                  rc[:, 2 * y:2 * y + 2, :].unsqueeze(3)
                                                  .broadcast_to([WT, 2, NH, HD]), ALU.mult)
                        i.then_inc(s["norm"], 1)

                    def start():
                        dve.tensor_copy(sel[:, :, :], self_[:, :, :])
                        for j in range(4):
                            dve.tensor_copy(blocks[:, j, :], blocksf[:, :])
                            dve.tensor_copy(mt[:, j, :], blocksf[:, :])
                        dve.drain()
                        dve.nop().then_inc(s["made"], 1)
                        for b in range(2):
                            normalize(b, b)
                        dve.wait_ge(s["tr"], 1)
                        normalize(2, 0)
                        values(0, 0)

                    def body(b, k, p):
                        for n in range(4):
                            maxima(b, n)
                        cut_maxima()
                        if exists(b - 1):
                            divide(b - 1)
                        if exists(b + 1):
                            values(b + 1, 1 - p)
                        if exists(b + 3):
                            normalize(b + 3, 1 - p)

                    each_batch(dve, start, body, lambda: divide(NB - 1))

        merge_windows(nc, t, a, sub, SEG)


def merge_windows(nc, t, a, ctx, SEG):
    first = ctx.enter_context(nc.sbuf_tensor("win_first", [P, NB, 2, D], F32))
    second = ctx.enter_context(nc.sbuf_tensor("win_second", [P, NB, 2, D], F32))
    share = ctx.enter_context(nc.sbuf_tensor("win_share", [P, 2], F32))
    s = Sems(nc, ctx, "merge", "cleared share loaded0 loaded1")
    seg = SEG.rearrange("(s b w) c -> s w b c", b=NB, w=WIN)
    H4 = t.H[:, :, :].rearrange("p (b h) c -> p b h c", h=2)
    U4 = t.U[:, :, :].rearrange("p (b h) c -> p b h c", h=2)
    pieces = [(first, 0, 0, 0, 12, 0, 10), (first, 0, 120, 12, 13, 0, 8),
              (second, 0, 10, 0, 11, 10, 20), (second, 0, 120, 11, 12, 10, 18),
              (first, 1, 0, 12, 13, 8, 10), (first, 1, 2, 13, 24, 0, 10),
              (second, 1, 0, 11, 12, 18, 20), (second, 1, 2, 12, 24, 10, 20)]
    arrived = [16 * sum(q[4] - q[3] for q in pieces if q[1] == h) for h in range(2)]
    with nc.Block() as block:

        @block.gpsimd
        def _(pool):
            pool.memset(first[:, :, :, :], 0.0).then_inc(s["cleared"], 1)
            pool.memset(second[:, :, :, :], 0.0).then_inc(s["cleared"], 1)

        @block.sync
        def _(sp):
            sp.dma_start(share[:, :], a["c_share"]).then_inc(s["share"], 16)
            sp.wait_ge(s["cleared"], 2)
            for buf, h, p0, s0, s1, w0, w1 in pieces:
                for q in range(s0, s1):
                    r = p0 + (q - s0) * (w1 - w0)
                    sp.dma_start(buf[r:r + w1 - w0, :, h, :], seg[q, w0:w1]).then_inc(s[f"loaded{h}"], 16)
            for h in range(2):
                sp.wait_ge(s[f"loaded{h}"], arrived[h])

        @block.vector
        def _(dve):
            dve.tensor_tensor(t.H[:, :, :], t.H[:, :, :], t.U[:, :, :], ALU.add)
            dve.wait_ge(s["share"], 16)
            for h in range(2):
                dve.wait_ge(s[f"loaded{h}"], arrived[h])
                dve.tensor_tensor(first[:, :, h, :], first[:, :, h, :], second[:, :, h, :], ALU.add)
                dve.drain()
                dve.scalar_tensor_tensor(H4[:, :, h, :], first[:, :, h, :], share[:, h:h + 1], H4[:, :, h, :],
                                         ALU.mult, ALU.add)
                dve.drain()
                with dve.Fori(0, NB // 8) as k:
                    for p in range(8):
                        i = (k * 8 + p) * 2 + h
                        dve.bn_stats(t.BN[:, i, :], t.H[:, i, :])


EXPERT_SEMS = ("weights w1 w2 b2 staged tr tt logits exp1 exp2 counts_in counts made "
               "xs0 xs1 picked xtr xt hid_ps pre hid out_ps res sent0 sent1")


def full_attention(nc, t, a, name):
    keep = name == "l0mha"
    ln_scales(nc, t, f"{name}_ln")
    with ExitStack() as ctx:
        def sb(n, shape, dt=F32):
            return ctx.enter_context(nc.sbuf_tensor(f"{name}_{n}", shape, dt))

        s = t.mha_sems
        if not keep:
            s.restart(nc)
        w = attention_weights(nc, ctx, a, name)
        two = range(2)
        us, ut = [sb(f"us{i}", [P, 2, D]) for i in two], [sb(f"ut{i}", [P, L]) for i in two]
        qk = [sb(f"qk{i}", [P, 2, L]) for i in two]
        parts = [sb(f"parts{i}", [P, 3, 2, L], BF16) for i in two]
        rest = sb("rest", [P, 2, L])
        qs = [sb(f"qs{i}", [STACK, NH, L], BF16) for i in two]
        ks = [sb(f"ks{i}", [STACK, NH, L], BF16) for i in two]
        v = [sb(f"v{i}", [P, 2, NH, HS]) for i in two]
        nm, nmrest, nms = sb("nm", [P, 2, NH]), sb("nmrest", [P, 2, NH]), sb("nms", [P, 2, P], BF16)
        mt, zero = sb("mt", [P, L], BF16), sb("zero", [P, 1])
        pt = [sb(f"pt{i}", [P, NH, 2, L]) for i in two]
        st = sb("st", [P, 2, L])
        rc, oc, ot = sb("rc", [P, 2, NH]), sb("oc", [P, 2, NH, HD]), sb("ot", [P, L])
        self_, sel = sb("self", [P, NH, P]), sb("sel", [P, NH, P], BF16)
        attention_prelude(nc, t, s, nms, zero, v, w.loads + [(self_, a["c_sel"])])
        PS = t.PS

        with nc.Block() as block:

            @block.tensor
            def _(pe):
                def transpose_tokens(b, p):
                    pe.wait_ge(s["u"], b + 1)
                    if exists(b - 2):
                        pe.wait_ge(s["v"], b - 1)
                    for h in range(2):
                        mm = pe.transpose(PS[:, 4 + p, h * P:(h + 1) * P], us[p][:, h, :], t.ident[:, :])
                    mm.then_inc(s["tr"], 1)

                def project_queries_keys(b, p):
                    pe.wait_ge(s["ut"], b + 1)
                    for g in range(2):
                        mm = pe.matmul(PS[:, 4 + p, g * L:(g + 1) * L], w.wqk[:, g, :], ut[p][:, :],
                                       start=True, stop=True)
                    mm.then_inc(s["qk_ps"], 1)

                def project_values(b, p):
                    pe.wait_ge(s["qk"], b + 1)
                    for h in range(2):
                        mm = pe.matmul(PS[:, 4 + p, h * D:(h + 1) * D], ut[p][:, h * P:(h + 1) * P],
                                       w.wvo[:, 0, :], start=True, stop=True)
                    mm.then_inc(s["v_ps"], 1)

                def row_scores(b, p, n):
                    if n < 2:
                        pe.wait_ge(s["exp"], b * 4 + 3 + n)
                    else:
                        pe.wait_ge(s["mx"], b * 4 + n - 1)
                    for h in range(2):
                        for tile in range(2):
                            mm = pe.matmul(PS[:, 2 * (n % 2) + h, tile * L:(tile + 1) * L],
                                           qs[p][:, 2 * n + h, tile * P:(tile + 1) * P],
                                           ks[p][:, 2 * n + h, :], start=True, stop=True)
                    mm.then_inc(s["st_ps"], 1)

                def column_scores(b, p, n):
                    if n < 2:
                        pe.wait_ge(s["mx"], b * 4 + 3 + n)
                    else:
                        pe.wait_ge(s["exp"], b * 4 + 3 + n)
                    for h in range(2):
                        bank = 2 * (n % 2) + h
                        pe.matmul(PS[:, bank, :].rearrange("p (j c) -> p j c", j=2), sel[:, 2 * n + h, :],
                                  mt[:, :].unsqueeze(1).broadcast_to([P, 2, L]), start=True, stop=False)
                        for tile in range(2):
                            mm = pe.matmul(PS[:, bank, tile * L:(tile + 1) * L],
                                           ks[p][:, 2 * n + h, tile * P:(tile + 1) * P],
                                           qs[p][:, 2 * n + h, :], start=False, stop=(tile == 1))
                    mm.then_inc(s["stt_ps"], 1)

                def sum_values(b, p, g):
                    if g == 0:
                        pe.wait_ge(s["exp"], b * 4 + 8)
                        pe.wait_ge(s["v"], b + 1)
                        if exists(b - 1):
                            pe.wait_ge(s["added"], b)
                    for tile in range(2):
                        for i in range(4):
                            mm = pe.matmul(PS[HS * i:HS * i + HS, 6 + p, g * L:(g + 1) * L],
                                           v[p][:, tile, 4 * g + i, :], pt[p][:, 4 * g + i, tile, :],
                                           start=(tile == 0), stop=(tile == 1))
                    mm.then_inc(s["av_ps"], 1)

                def turn_sums(b, p):
                    pe.wait_ge(s["sums"], b + 1)
                    for q in range(2):
                        for g in range(2):
                            o = (q * 2 + g) * P
                            mm = pe.transpose(PS[:, 6 + p, o:o + P], st[:, g, q * P:(q + 1) * P], t.ident[:, :])
                    mm.then_inc(s["turned"], 1)

                def transpose_sums(b, p):
                    pe.wait_ge(s["norm"], b + 1)
                    for q in range(2):
                        mm = pe.transpose(PS[:, 6 + p, q * P:(q + 1) * P],
                                          oc[:, q].rearrange("q h d -> q (h d)"), t.ident[:, :])
                    mm.then_inc(s["ot_ps"], 1)

                def project_output(b, p):
                    pe.wait_ge(s["ot"], b + 1)
                    for q in range(2):
                        mm = pe.matmul(PS[:, 6 + p, L + q * D:L + (q + 1) * D], ot[:, q * P:(q + 1) * P],
                                       w.wvo[:, 1, :], start=True, stop=True)
                    mm.then_inc(s["out_ps"], 1)

                def transpose_maxima(b, p):
                    pe.wait_ge(s["nms"], b + 1)
                    if exists(b + 1):
                        pe.wait_ge(s["qk"], b + 2)
                    for j in range(2):
                        mm = pe.transpose(PS[:, 5 - p, j * (P // 2):(j + 1) * (P // 2)].bitcast(BF16),
                                          nms[:, j, :], t.ident16[:, :])
                    mm.then_inc(s["nt_ps"], 1)

                def start():
                    pe.wait_ge(s["made"], 1)
                    for b in range(2):
                        transpose_tokens(b, b)
                        project_queries_keys(b, b)

                def body(b, k, p):
                    last, before = exists(b - 1), exists(b - 2)
                    pe.wait_ge(s[f"stacks{p}"], k * STACK_DMAS + STACK_DMAS)
                    for n in range(2):
                        row_scores(b, p, n)
                    if before:
                        turn_sums(b - 2, p)
                    project_values(b, p)
                    if last:
                        sum_values(b - 1, 1 - p, 0)
                    row_scores(b, p, 2)
                    if exists(b + 2):
                        transpose_tokens(b + 2, p)
                    row_scores(b, p, 3)
                    if exists(b + 2):
                        project_queries_keys(b + 2, p)
                    if last:
                        sum_values(b - 1, 1 - p, 1)
                    transpose_maxima(b, p)
                    if before:
                        transpose_sums(b - 2, p)
                    pe.wait_ge(s["mt"], b + 1)
                    for n in range(4):
                        column_scores(b, p, n)
                        if n == 1 and before:
                            project_output(b - 2, p)

                def end():
                    turn_sums(NB - 2, 0)
                    for g in range(2):
                        sum_values(NB - 1, 1, g)
                    transpose_sums(NB - 2, 0)
                    project_output(NB - 2, 0)
                    turn_sums(NB - 1, 1)
                    transpose_sums(NB - 1, 1)
                    project_output(NB - 1, 1)

                each_batch(pe, start, body, end)

            @block.scalar
            def _(act):
                def tokens(b, p):
                    act.wait_ge(s["tr"], b + 1)
                    act.activation(ut[p][:, :], PS[:, 4 + p, 0:L], ACT.Copy).then_inc(s["ut"], 1)

                def queries_keys(b, p):
                    act.wait_ge(s["qk_ps"], b + 1)
                    for g in range(2):
                        i = act.activation(qk[p][:, g, :], PS[:, 4 + p, g * L:(g + 1) * L],
                                           ACT.Identity, bias=w.bqk[:, g:g + 1])
                    i.then_inc(s["qk"], 1)

                def sums(b, p):
                    act.wait_ge(s["ot_ps"], b + 1)
                    act.activation(ot[:, :], PS[:, 6 + p, 0:L], ACT.Copy).then_inc(s["ot"], 1)

                def start():
                    act.nop().then_inc(s["exp"], 4)
                    for b in range(2):
                        tokens(b, b)
                        queries_keys(b, b)

                def evict_sums(b, p):
                    act.wait_ge(s["av_ps"], b * 2 + 2)
                    act.activation(st[:, :, :].rearrange("p g c -> p (g c)"), PS[:, 6 + p, :], ACT.Copy)\
                       .then_inc(s["sums"], 1)

                def body(b, k, p):
                    if exists(b + 2):
                        tokens(b + 2, p)
                        queries_keys(b + 2, p)
                    act.wait_ge(s["nt_ps"], b + 1)
                    act.activation(mt[:, :], PS[:, 5 - p, 0:P].bitcast(BF16), ACT.Copy).then_inc(s["mt"], 1)
                    if exists(b - 2):
                        sums(b - 2, p)
                    if exists(b - 1):
                        evict_sums(b - 1, 1 - p)
                    for n in range(4):
                        act.wait_ge(s["stt_ps"], b * 4 + n + 1)
                        bank = 2 * (n % 2)
                        act.activation(pt[p][:, 2 * n:2 * n + 2].rearrange("q h j c -> q h (j c)"),
                                       PS[:, bank:bank + 2, :], ACT.Exp, scale=HD ** -0.5).then_inc(s["exp"], 1)

                def end():
                    evict_sums(NB - 1, 1)
                    sums(NB - 2, 0)
                    sums(NB - 1, 1)

                each_batch(act, start, body, end)

            @block.gpsimd
            def _(pool):
                zeros = zero[:, :].unsqueeze(2).broadcast_to([P, 2, L])

                def base_and_parts(b, p):
                    pool.wait_ge(s["u"], b + 1)
                    pool.wait_ge(s["qk"], b + 1)
                    bo = w.bvo[:, 1, :].unsqueeze(1).broadcast_to([P, 2, D])
                    if keep:
                        pool.tensor_tensor(t.R[:, bass.ds(b * 2, 2), :], us[p][:, :, :], bo, ALU.add)\
                            .then_inc(s["base"], 1)
                    else:
                        pool.tensor_tensor(t.H[:, bass.ds(b * 2, 2), :], t.H[:, bass.ds(b * 2, 2), :], bo, ALU.add)\
                            .then_inc(s["base"], 1)
                    pool.tensor_tensor(parts[p][:, 0], qk[p][:, :, :], zeros, ALU.add)
                    pool.drain()
                    pool.tensor_tensor(rest[:, :, :], qk[p][:, :, :], parts[p][:, 0], ALU.subtract)
                    pool.drain()
                    pool.tensor_tensor(parts[p][:, 1], rest[:, :, :], zeros, ALU.add)
                    pool.drain()
                    pool.tensor_tensor(parts[p][:, 2], rest[:, :, :], parts[p][:, 1], ALU.subtract)\
                        .then_inc(s["parts"], 1)

                def start():
                    for b in range(2):
                        base_and_parts(b, b)

                def body(b, k, p):
                    if exists(b + 2):
                        base_and_parts(b + 2, p)

                each_batch(pool, start, body, lambda: None)

            @block.sync
            def _(sp):
                def stack(b, p):
                    sp.wait_ge(s["parts"], b + 1)
                    if exists(b - 2):
                        sp.wait_ge(s["stt_ps"], b * 4 - 4)
                    for g in range(6):
                        rows = slice(g * HD, (g + 1) * HD)
                        sp.dma_start(qs[p][rows, :, :], parts[p][:, QUERY_PARTS[g], 0, :])\
                          .then_inc(s[f"stacks{p}"], 16)
                        sp.dma_start(ks[p][rows, :, :], parts[p][:, KEY_PARTS[g], 1, :])\
                          .then_inc(s[f"stacks{p}"], 16)

                def body(b, k, p):
                    if exists(b + 1):
                        stack(b + 1, 1 - p)

                each_batch(sp, lambda: stack(0, 0), body, lambda: None)

            @block.vector
            def _(dve):
                def normalize(b, p):
                    for h in range(2):
                        i = b * 2 + h
                        u = dve.tensor_scalar(us[p][:, h, :], t.H[:, i, :], t.MEAN[:, bass.ds(i, 1)],
                                              t.RSTD[:, bass.ds(i, 1)], ALU.subtract, ALU.mult)
                    u.then_inc(s["u"], 1)

                def values(b, p):
                    dve.wait_ge(s["v_ps"], b + 1)
                    for h in range(2):
                        i = dve.tensor_tensor(
                            v[p][:, h, :, 0:HD],
                            PS[:, 4 + p, h * D:(h + 1) * D].rearrange("q (h d) -> q h d", h=NH),
                            w.bvo[:, 0, :].rearrange("q (h d) -> q h d", h=NH), ALU.add)
                    i.then_inc(s["v"], 1)

                def maxima(b, n):
                    dve.wait_ge(s["st_ps"], b * 4 + n + 1)
                    bank = 2 * (n % 2)
                    dve.tensor_reduce(nm[:, :, 2 * n:2 * n + 2].rearrange("q j i -> q i j"),
                                      PS[:, bank:bank + 2, :].rearrange("q i (j c) -> q i j c", j=2),
                                      AX.X, ALU.max, negate=True).then_inc(s["mx"], 1)

                def cut_maxima():
                    dve.drain()
                    dve.tensor_copy(nms[:, :, 0:NH], nm[:, :, :])
                    dve.drain()
                    dve.tensor_tensor(nmrest[:, :, :], nm[:, :, :], nms[:, :, 0:NH], ALU.subtract)
                    dve.drain()
                    dve.tensor_copy(nms[:, :, NH:2 * NH], nmrest[:, :, :])
                    dve.drain()
                    dve.tensor_tensor(nms[:, :, 2 * NH:3 * NH], nmrest[:, :, :], nms[:, :, NH:2 * NH],
                                      ALU.subtract).then_inc(s["nms"], 1)

                def divide(b, p):
                    dve.wait_ge(s["turned"], b + 1)
                    av = PS[:, 6 + p, :].rearrange("q (j h e) -> q j h e", j=2, h=NH)
                    dve.reciprocal(rc[:, :, :], av[:, :, :, HD])
                    dve.drain()
                    for q in range(2):
                        i = dve.tensor_tensor(oc[:, q], av[:, q, :, 0:HD],
                                              rc[:, q, :].unsqueeze(2).broadcast_to([P, NH, HD]), ALU.mult)
                    i.then_inc(s["norm"], 1)

                def add_attention(b, p):
                    dve.wait_ge(s["out_ps"], b + 1)
                    dve.wait_ge(s["base"], b + 1)
                    out = PS[:, 6 + p, L:L + 2 * D].rearrange("q (j c) -> q j c", j=2)
                    x = t.R if keep else t.H
                    dve.tensor_tensor(x[:, bass.ds(b * 2, 2), :], out, x[:, bass.ds(b * 2, 2), :], ALU.add)\
                       .then_inc(s["added"], 1)
                    dve.drain()
                    for q in range(2):
                        dve.bn_stats(t.BN[:, b * 2 + q, :], x[:, b * 2 + q, :])

                def start():
                    dve.tensor_copy(sel[:, :, :], self_[:, :, :]).then_inc(s["made"], 1)
                    dve.nop().then_inc(s["added"], 1)
                    for b in range(2):
                        normalize(b, b)
                    dve.wait_ge(s["tr"], 1)
                    dve.wait_ge(s["base"], 1)
                    normalize(2, 0)

                def body(b, k, p):
                    for n in range(2):
                        maxima(b, n)
                    values(b, p)
                    for n in range(2, 4):
                        maxima(b, n)
                    cut_maxima()
                    if exists(b - 2):
                        divide(b - 2, p)
                    if exists(b + 3):
                        dve.wait_ge(s["base"], b + 2)
                        normalize(b + 3, 1 - p)
                    if exists(b - 2):
                        add_attention(b - 2, p)

                def end():
                    for b in (NB - 2, NB - 1):
                        divide(b, b % 2)
                        add_attention(b, b % 2)

                each_batch(dve, start, body, end)


def experts_layer(nc, t, a, name):
    first_layer = name == "l0moe"
    ntop = 1 if first_layer else 2
    tiles = TILES1 if first_layer else TILES2
    XS = t.XS1 if first_layer else t.XS2
    gelu = ACT.Gelu_apprx_tanh if first_layer else ACT.Gelu
    YS = nc.dram_tensor(f"{name}_out", [tiles * P, D], F32).ap()
    ln_scales(nc, t, f"{name}_ln")
    with ExitStack() as ctx:
        def sb(n, shape, dt=F32):
            return ctx.enter_context(nc.sbuf_tensor(f"{name}_{n}", shape, dt))

        s = t.moe_sems
        rows_moved = Sems(nc, ctx, name, "scattered gathered0 gathered1 gathered2 gathered3")
        if not first_layer:
            s.restart(nc)
        gb, gw, gbias = sb("gb", [P, 2, D]), sb("gate_w", [P, NE]), sb("gate_b", [P, NE])
        before, order, chain = sb("before", [P, P]), sb("order", [P, NE, NT]), sb("chain", [P, NE, NT])
        ones, trow = sb("ones", [P, P]), sb("trow", [1, NE, tiles])
        w1, w2, b2 = sb("w1", [P, NE, FF + KF]), sb("w2", [P, NE, KF, D]), sb("b2", [P, NE, D])
        pos = [sb(f"pos{i}", [P, NT], U32) for i in range(ntop)]
        gate = [sb(f"gate{i}", [P, NT]) for i in range(ntop)]
        te = sb("te", [1, tiles], I32)
        small = [(gb, a[name + "_gb"]), (gw, a[name + "_gate_w"]), (gbias, a[name + "_gate_b"]),
                 (before, a["c_before"]), (order, a["c_order"]), (chain, a["c_chain"])]
        PS = t.PS
        if not first_layer:
            t.U = sb("u", [P, NT, D])
            second_norm(nc, t)
            ln_scales(nc, t, f"{name}_ln2")
        src = t.R if first_layer else t.U

        with ExitStack() as sub:
            def tb(n, shape, dt=F32):
                return sub.enter_context(nc.sbuf_tensor(f"{name}_{n}", shape, dt))

            T = tb("t", [P, NT, D])
            tt = [tb(f"tt{i}", [P, 4, P]) for i in range(2)]
            LG, E1, M = tb("lg", [P, NE, NT]), tb("e1", [P, NE, NT]), tb("m", [P, NE, NT])
            OH = [tb(f"oh{i}", [P, NE, NT]) for i in range(ntop)]
            CN, RK = tb("cn", [P, NE, NT]), tb("rk", [P, NE, NT])
            best, sm = tb("best", [P, NT]), tb("sm", [P, NT])
            nt_, en = tb("ntiles", [P, NE]), tb("ends", [P, NE])
            cmp_ = tb("cmp", [1, NE, tiles])

            with nc.Block() as block:
                load_all(block, small, s["weights"])

                @block.scalar
                def _(act):
                    act.wait_ge(s["weights"], 16 * len(small))
                    act.dma_start(w1[:, :, :], a[name + "_w1"]).then_inc(s["w1"], 16)
                    act.dma_start(w2[:, :, :, :], a[name + "_w2"]).then_inc(s["w2"], 16)
                    act.dma_start(b2[:, :, :], a[name + "_b2"]).then_inc(s["b2"], 16)
                    for g in range(NT // 4):
                        act.wait_ge(s["tr"], g + 1)
                        act.activation(tt[g % 2][:, :, :].rearrange("c i r -> c (i r)"), PS[:, g % 2, :],
                                       ACT.Copy).then_inc(s["tt"], 1)
                    act.wait_ge(s["exp1"], 1)
                    act.activation(E1[:, :, :], LG[:, :, :], ACT.Exp).then_inc(s["exp2"], 1)

                @block.gpsimd
                def _(pool):
                    pool.memset(ones[:, :], 1.0).then_inc(s["made"], 1)
                    pool.iota(trow[:, :, :], [[0, NE], [1, tiles]], base=0, channel_multiplier=0,
                              allow_small_or_imprecise_dtypes=True).then_inc(s["made"], 1)

                @block.tensor
                def _(pe):
                    pe.wait_ge(s["weights"], 16 * len(small))
                    for g in range(NT // 4 + 1):
                        if g < NT // 4:
                            pe.wait_ge(s["staged"], g // 2 + 1)
                            if g >= 2:
                                pe.wait_ge(s["tt"], g - 1)
                            for i in range(4):
                                mm = pe.transpose(PS[:, g % 2, i * P:(i + 1) * P], T[:, 4 * g + i, :], t.ident[:, :])
                            mm.then_inc(s["tr"], 1)
                        if g:
                            pe.wait_ge(s["tt"], g)
                            for i in range(4):
                                o = (4 * g - 4 + i) * NE
                                mm = pe.matmul(PS[:, 2, o:o + NE], tt[(g - 1) % 2][:, i, :], gw[:, :],
                                               start=True, stop=True)
                            mm.then_inc(s["logits"], 1)
                    pe.wait_ge(s["made"], 2)
                    pe.wait_ge(s["counts_in"], 1)
                    oh = CN[:, :, :].rearrange("p e i -> p (e i)")
                    pe.matmul(PS[:, 4, 0:NE * NT], ones[:, :], oh, start=True, stop=True)
                    pe.matmul(PS[:, 5, 0:NE * NT], before[:, :], oh, start=True, stop=True)\
                      .then_inc(s["counts"], 1)

                @block.vector
                def _(dve):
                    dve.wait_ge(s["weights"], 16 * len(small))
                    with dve.Fori(0, NT // 8) as k:
                        for p in range(8):
                            i = k * 8 + p
                            dve.tensor_scalar(T[:, i, :], src[:, i, :], t.MEAN[:, bass.ds(i, 1)],
                                              t.RSTD[:, bass.ds(i, 1)], ALU.subtract, ALU.mult)
                        dve.drain()
                        eight = T[:, bass.ds(k * 8, 8), :]
                        dve.tensor_tensor(eight, eight, gb[:, 0, :].unsqueeze(1).broadcast_to([P, 8, D]), ALU.mult)
                        dve.drain()
                        dve.tensor_tensor(eight, eight, gb[:, 1, :].unsqueeze(1).broadcast_to([P, 8, D]), ALU.add)\
                           .then_inc(s["staged"], 1)
                    dve.wait_ge(s["logits"], NT // 4)
                    dve.tensor_tensor(LG[:, :, :].rearrange("p e i -> p i e"),
                                      PS[:, 2, 0:NT * NE].rearrange("p (i e) -> p i e", e=NE),
                                      gbias[:, :].unsqueeze(1).broadcast_to([P, NT, NE]), ALU.add)
                    dve.drain()

                    def over_experts(x):
                        return x.rearrange("p e i -> p i e")

                    def on_experts(x):
                        return x.unsqueeze(1).broadcast_to([P, NE, NT])

                    dve.tensor_reduce(best[:, :], over_experts(LG[:, :, :]), AX.X, ALU.max)
                    dve.drain()
                    dve.tensor_tensor(LG[:, :, :], LG[:, :, :], on_experts(best[:, :]), ALU.subtract)
                    dve.drain()

                    def first_at_least(onehot, floor):
                        dve.tensor_tensor(M[:, :, :], LG[:, :, :], floor, ALU.is_ge)
                        dve.drain()
                        dve.tensor_tensor(M[:, :, :], M[:, :, :], order[:, :, :], ALU.mult)
                        dve.drain()
                        dve.tensor_reduce(sm[:, :], over_experts(M[:, :, :]), AX.X, ALU.max)
                        dve.drain()
                        dve.tensor_tensor(onehot[:, :, :], order[:, :, :], on_experts(sm[:, :]), ALU.is_equal)
                        dve.drain()

                    dve.memset(best[:, :], 0.0)
                    dve.drain()
                    first_at_least(OH[0], on_experts(best[:, :]))
                    if first_layer:
                        dve.nop().then_inc(s["exp1"], 1)
                        dve.wait_ge(s["exp2"], 1)
                        dve.tensor_reduce(sm[:, :], over_experts(E1[:, :, :]), AX.X, ALU.add)
                        dve.drain()
                        dve.reciprocal(gate[0][:, :], sm[:, :])
                        dve.tensor_copy(CN[:, :, :], OH[0][:, :, :]).then_inc(s["counts_in"], 1)
                    else:
                        dve.scalar_tensor_tensor(LG[:, :, :], OH[0][:, :, :], NEG, LG[:, :, :], ALU.mult, ALU.add)
                        dve.drain()
                        dve.tensor_reduce(best[:, :], over_experts(LG[:, :, :]), AX.X, ALU.max)
                        dve.drain()
                        first_at_least(OH[1], on_experts(best[:, :]))
                        dve.tensor_tensor(CN[:, :, :], OH[0][:, :, :], OH[1][:, :, :], ALU.add)\
                           .then_inc(s["counts_in"], 1)
                        dve.tensor_tensor(LG[:, :, :], LG[:, :, :], OH[1][:, :, :], ALU.mult)
                        dve.drain()
                        dve.tensor_copy(LG[:, 0, :], best[:, :]).then_inc(s["exp1"], 1)
                        dve.wait_ge(s["exp2"], 1)
                        dve.tensor_scalar(sm[:, :], E1[:, 0, :], 1.0, None, ALU.add)
                        dve.drain()
                        dve.reciprocal(gate[0][:, :], sm[:, :])
                        dve.drain()
                        dve.tensor_tensor(gate[1][:, :], gate[0][:, :], E1[:, 0, :], ALU.mult)
                    dve.wait_ge(s["counts"], 1)
                    flat = "p e i -> p (e i)"
                    dve.tensor_tensor_scan(RK[:, :, :].rearrange(flat), chain[:, :, :].rearrange(flat),
                                           PS[:, 4, 0:NE * NT], 0.0, ALU.mult, ALU.add)
                    dve.drain()
                    dve.wait_ge(s["made"], 2)
                    dve.tensor_scalar(nt_[:, :], RK[:, :, NT - 1], 127.0, 1.0 / P, ALU.add, ALU.mult)
                    dve.drain()
                    dve.tensor_scalar(nt_[:, :], nt_[:, :], -127.0 / 256, MAGIC, ALU.add, ALU.add)
                    dve.drain()
                    dve.tensor_scalar(nt_[:, :], nt_[:, :], -MAGIC, None, ALU.add)
                    dve.drain()
                    dve.tensor_tensor_scan(en[:, :], ones[:, 0:NE], nt_[:, :], 0.0, ALU.mult, ALU.add)
                    dve.tensor_tensor(RK[:, :, :], RK[:, :, :],
                                      PS[:, 4, 0:NE * NT].rearrange("p (e i) -> p e i", e=NE), ALU.subtract)
                    dve.drain()
                    dve.tensor_tensor(RK[:, :, :], RK[:, :, :],
                                      PS[:, 5, 0:NE * NT].rearrange("p (e i) -> p e i", e=NE), ALU.add)
                    dve.tensor_tensor(nt_[:, :], en[:, :], nt_[:, :], ALU.subtract)
                    dve.drain()
                    dve.tensor_scalar(nt_[:, :], nt_[:, :], float(P), None, ALU.mult)
                    dve.drain()
                    dve.tensor_tensor(RK[:, :, :], RK[:, :, :],
                                      nt_[:, :].unsqueeze(2).broadcast_to([P, NE, NT]), ALU.add)
                    dve.drain()
                    for j in range(ntop):
                        dve.tensor_tensor(M[:, :, :], RK[:, :, :], OH[j][:, :, :], ALU.mult)
                        dve.drain()
                        dve.tensor_reduce(sm[:, :], over_experts(M[:, :, :]), AX.X, ALU.add)
                        dve.drain()
                        dve.tensor_copy(pos[j][:, :], sm[:, :])
                        dve.drain()
                    dve.tensor_tensor(cmp_[:, :, :], trow[:, :, :],
                                      en[0:1, :].unsqueeze(2).broadcast_to([1, NE, tiles]), ALU.is_ge)
                    dve.drain()
                    dve.tensor_reduce(trow[:, 0, :], cmp_[:, 0:NE - 1, :].rearrange("p e r -> p r e"), AX.X, ALU.add)
                    dve.drain()
                    dve.tensor_copy(te[:, :], trow[:, 0, :])

            with nc.Block() as block:
                if first_layer:
                    convolution_kernel(nc, t, a, sub, block)

                @block.gpsimd
                def _(pool):
                    for j in range(ntop):
                        for i in range(NT):
                            pool.indirect_dma_start(
                                out=XS, out_offset=bass.IndirectOffsetOnAxis(ap=pos[j][:, i:i + 1], axis=0),
                                in_=T[:, i, :], in_offset=None).then_inc(rows_moved["scattered"], 16)
                    pool.wait_ge(rows_moved["scattered"], 16 * ntop * NT)

        with ExitStack() as sub:
            def tb(n, shape, dt=F32):
                return sub.enter_context(nc.sbuf_tensor(f"{name}_{n}", shape, dt))

            two = range(2)
            xs, xt = [tb(f"xs{i}", [P, D]) for i in two], [tb(f"xt{i}", [P, P]) for i in two]
            ws = [tb(f"ws{i}", [P, FF + KF]) for i in two]
            hp, hid = [tb(f"hp{i}", [P, KF, P]) for i in two], [tb(f"hid{i}", [P, KF, P]) for i in two]
            res = [tb(f"res{i}", [P, D]) for i in two]

            def each_tile(eng, first, body, last):
                first()
                for i in range(2):
                    body(i, 0, i)
                with eng.Fori(1, tiles // 2 - 1) as k:
                    for p in range(2):
                        body(k * 2 + p, k, p)
                for i in range(tiles - 2, tiles):
                    body(i, i // 2, i % 2)
                last()

            def there(i):
                return not isinstance(i, int) or 0 <= i < tiles

            def expert_of(eng, i):
                return eng.value_load(te[0:1, bass.ds(i, 1)], min_val=0, max_val=NE - 1)

            with nc.Block() as block:

                @block.sync
                def _(sp):
                    def body(i, k, p):
                        if there(i - 2):
                            sp.wait_ge(s["xtr"], i - 1)
                        sp.dma_start(xs[p][:, :], XS[bass.ds(i * P, P), :]).then_inc(s[f"xs{p}"], 16)

                    each_tile(sp, lambda: None, body, lambda: None)

                @block.tensor
                def _(pe):
                    def turn(i, k, p):
                        pe.wait_ge(s[f"xs{p}"], k * 16 + 16)
                        pe.transpose(PS[:, p, 0:P], xs[p][:, :], t.ident[:, :]).then_inc(s["xtr"], 1)

                    def up(i, p):
                        pe.wait_ge(s["picked"], i + 1)
                        for j in range(KF):
                            mm = pe.matmul(PS[:, 2 + p, j * P:(j + 1) * P], ws[p][:, j * P:(j + 1) * P],
                                           xt[p][:, :], start=True, stop=True)
                        mm.then_inc(s["hid_ps"], 1)

                    def down(i, p):
                        e = expert_of(pe, i)
                        pe.wait_ge(s["hid"], i + 1)
                        if there(i - 2):
                            pe.wait_ge(s["res"], i - 1)
                        for j in range(KF):
                            mm = pe.matmul(PS[:, 4 + p, 0:D], hid[p][:, j, :], w2[:, e, j, :],
                                           start=(j == 0), stop=(j == KF - 1))
                        mm.then_inc(s["out_ps"], 1)

                    def start():
                        pe.wait_ge(s["w2"], 16)
                        turn(0, 0, 0)

                    def body(i, k, p):
                        if there(i + 1):
                            turn(i + 1, k + p, 1 - p)
                        up(i, p)
                        if there(i - 1):
                            down(i - 1, 1 - p)

                    each_tile(pe, start, body, lambda: down(tiles - 1, 1))

                @block.scalar
                def _(act):
                    def store(i, p):
                        act.wait_ge(s["res"], i + 1)
                        act.dma_start(YS[bass.ds(i * P, P), :], res[p][:, :]).then_inc(s[f"sent{p}"], 16)

                    def body(i, k, p):
                        act.wait_ge(s["pre"], i + 1)
                        act.activation(hid[p][:, :, :], hp[p][:, :, :], gelu).then_inc(s["hid"], 1)
                        if there(i - 1):
                            store(i - 1, 1 - p)

                    def end():
                        store(tiles - 1, 1)
                        for p in range(2):
                            act.wait_ge(s[f"sent{p}"], 16 * (tiles // 2))

                    each_tile(act, lambda: None, body, end)

                @block.vector
                def _(dve):
                    def pick(i, p):
                        e = expert_of(dve, i)
                        dve.drain()
                        dve.wait_ge(s["xtr"], i + 1)
                        dve.tensor_copy(xt[p][:, :], PS[:, p, 0:P])
                        dve.tensor_copy(ws[p][:, :], w1[:, e, :]).then_inc(s["picked"], 1)

                    def add_bias(i, p):
                        dve.wait_ge(s["hid_ps"], i + 1)
                        dve.tensor_tensor(hp[p][:, :, :], PS[:, 2 + p, :].rearrange("f (j r) -> f j r", j=KF),
                                          ws[p][:, FF:FF + KF].unsqueeze(2).broadcast_to([P, KF, P]), ALU.add)\
                           .then_inc(s["pre"], 1)

                    def finish(i, k, p):
                        e = expert_of(dve, i)
                        dve.wait_ge(s["out_ps"], i + 1)
                        if there(i - 2):
                            dve.wait_ge(s[f"sent{p}"], k * 16)
                        dve.tensor_tensor(res[p][:, :], PS[:, 4 + p, 0:D], b2[:, e, :], ALU.add)\
                           .then_inc(s["res"], 1)

                    def start():
                        dve.wait_ge(s["b2"], 16)
                        dve.wait_ge(s["w1"], 16)
                        pick(0, 0)

                    def body(i, k, p):
                        if there(i + 1):
                            pick(i + 1, 1 - p)
                        add_bias(i, p)
                        if there(i - 1):
                            finish(i - 1, k - 1 + p, 1 - p)

                    each_tile(dve, start, body, lambda: finish(tiles - 1, tiles // 2 - 1, 1))

        CH = 4
        n = NT // CH
        with ExitStack() as sub:
            got = [sub.enter_context(nc.sbuf_tensor(f"{name}_got{j}", [P, NT, D], F32)) for j in range(ntop)]
            with nc.Block() as block:

                @block.gpsimd
                def _(pool):
                    for c in range(CH):
                        for i in range(c * n, (c + 1) * n):
                            for j in range(ntop):
                                pool.indirect_dma_start(
                                    out=got[j][:, i, :], out_offset=None, in_=YS,
                                    in_offset=bass.IndirectOffsetOnAxis(ap=pos[j][:, i:i + 1], axis=0))\
                                    .then_inc(rows_moved[f"gathered{c}"], 16)
                    for c in range(CH):
                        pool.wait_ge(rows_moved[f"gathered{c}"], 16 * ntop * n)

                @block.vector
                def _(dve):
                    if not first_layer:
                        dve.tensor_tensor(t.H[:, :, :], t.H[:, :, :], t.U[:, :, :], ALU.add)
                        dve.drain()
                    for c in range(CH):
                        tiles_ = slice(c * n, (c + 1) * n)
                        dve.wait_ge(rows_moved[f"gathered{c}"], 16 * ntop * n)
                        for j in range(ntop):
                            dve.tensor_tensor(got[j][:, tiles_, :], got[j][:, tiles_, :],
                                              gate[j][:, tiles_].unsqueeze(2).broadcast_to([P, n, D]), ALU.mult)
                        dve.drain()
                        for j in range(ntop):
                            dve.tensor_tensor(t.H[:, tiles_, :], t.H[:, tiles_, :], got[j][:, tiles_, :], ALU.add)
                            dve.drain()
                        with dve.Fori(0, n) as i:
                            dve.bn_stats(t.BN[:, i + c * n, :], t.H[:, i + c * n, :])


def bitlinear_ffn(nc, t, a):
    ln_scales(nc, t, "bit_ln")
    with ExitStack() as ctx:
        def sb(n, shape, dt=F32):
            return ctx.enter_context(nc.sbuf_tensor(f"bit_{n}", shape, dt))

        s = Sems(nc, ctx, "bit", "weights ones sums sum_ps ident xq tr xt up_ps h hr hq htr ht out_ps added")
        up, down = sb("up", [P, FF]), sb("down", [P, KF, D])
        upq, downq = sb("upq", [P, FF], BF16), sb("downq", [P, KF, D], BF16)
        identb = sb("ident", [P, P], BF16)
        ones, sums, ws, wi = sb("ones", [P, P]), sb("sums", [P, 2]), sb("ws", [P, 2]), sb("wi", [P, 2])
        two = range(2)
        U, XQ, XT = sb("u", [P, NT, D]), sb("xq", [P, NT, D], BF16), sb("xt", [P, NT, P], BF16)
        am0, xsc0, osc0 = sb("token_am", [P, NT]), sb("token_xsc", [P, NT]), sb("token_osc", [P, NT])
        am, xsc, osc = [sb(f"am{i}", [P, 2]) for i in two], sb("xsc", [P, 2]), [sb(f"osc{i}", [P, 2]) for i in two]
        h, hr = [sb(f"h{i}", [P, 2, FF]) for i in two], [sb(f"hr{i}", [P, 2, FF]) for i in two]
        hq, ht = [sb(f"hq{i}", [P, 2, FF], BF16) for i in two], [sb(f"ht{i}", [P, 2, FF], BF16) for i in two]
        xts = [sb(f"xts{i}", [P, 2, P], BF16) for i in two]
        PS = t.PS
        PB = PS[:, :, :].bitcast(BF16)

        with nc.Block() as block:
            load_all(block, [(up, a["bit_up"]), (down, a["bit_down"])], s["weights"])

            @block.tensor
            def _(pe):
                pe.wait_ge(s["sums"], 1)
                pe.matmul(PS[:, 0, 0:2], ones[:, :], sums[:, :], start=True, stop=True).then_inc(s["sum_ps"], 1)
                for g in range(4):
                    pe.wait_ge(s["xq"], g + 1)
                    for i in range(8):
                        mm = pe.transpose(PB[:, 4 + g, i * P:(i + 1) * P], XQ[:, 8 * g + i, :], identb[:, :])
                    mm.then_inc(s["tr"], 1)

            @block.scalar
            def _(act):
                for g in range(4):
                    act.wait_ge(s["tr"], g + 1)
                    act.activation(XT[:, 8 * g:8 * g + 8, :].rearrange("p i c -> p (i c)"), PB[:, 4 + g, :],
                                   ACT.Copy)

            @block.vector
            def _(dve):
                dve.memset(ones[:, :], 1.0)
                dve.tensor_copy(identb[:, :], t.ident[:, :])
                dve.wait_ge(s["weights"], 32)
                dve.tensor_reduce(sums[:, 0:1], up[:, :], AX.X, ALU.add, apply_absolute_value=True)
                dve.tensor_reduce(sums[:, 1:2], down[:, :, :], AX.XY, ALU.add, apply_absolute_value=True)
                dve.drain()
                dve.nop().then_inc(s["sums"], 1)
                dve.wait_ge(s["sum_ps"], 1)
                dve.tensor_scalar(ws[:, :], PS[:, 0, 0:2], 1.0 / (D * FF), EPS, ALU.mult, ALU.max)
                dve.drain()
                dve.reciprocal(wi[:, :], ws[:, :])
                dve.drain()
                for n, (w, q) in enumerate(((up[:, :], upq[:, :]), (down[:, :, :], downq[:, :, :]))):
                    dve.tensor_scalar(w, w, wi[:, n:n + 1], MAGIC, ALU.mult, ALU.add)
                    dve.drain()
                    dve.tensor_scalar(w, w, -MAGIC, 1.0, ALU.add, ALU.min)
                    dve.drain()
                    dve.tensor_scalar(q, w, -1.0, None, ALU.max)
                with dve.Fori(0, NT) as i:
                    dve.tensor_scalar(U[:, i, :], t.H[:, i, :], t.MEAN[:, bass.ds(i, 1)],
                                      t.RSTD[:, bass.ds(i, 1)], ALU.subtract, ALU.mult)
                dve.drain()
                dve.tensor_reduce(am0[:, :], U[:, :, :], AX.X, ALU.max, apply_absolute_value=True)
                dve.drain()
                dve.tensor_scalar(am0[:, :], am0[:, :], EPS, None, ALU.max)
                dve.drain()
                dve.reciprocal(xsc0[:, :], am0[:, :])
                dve.tensor_scalar(osc0[:, :], am0[:, :], 1.0 / 127, ws[:, 0:1], ALU.mult, ALU.mult)
                dve.drain()
                dve.tensor_scalar(xsc0[:, :], xsc0[:, :], 127.0, None, ALU.mult)
                dve.drain()
                for g in range(4):
                    n = slice(8 * g, 8 * g + 8)
                    dve.tensor_tensor(U[:, n, :], U[:, n, :], xsc0[:, n].unsqueeze(2).broadcast_to([P, 8, D]),
                                      ALU.mult)
                    dve.drain()
                    dve.tensor_scalar(XQ[:, n, :], U[:, n, :], MAGIC, -MAGIC, ALU.add, ALU.add)\
                       .then_inc(s["xq"], 1)

        with nc.Block() as block:

            @block.tensor
            def _(pe):
                def up(b, p):
                    pe.wait_ge(s["xt"], b + 1)
                    if exists(b - 2):
                        pe.wait_ge(s["h"], b - 1)
                    for j in range(2):
                        mm = pe.matmul(PS[:, 2 * p + j, :], xts[p][:, j, :], upq[:, :], start=True, stop=True)
                    mm.then_inc(s["up_ps"], 1)

                def turn(b, p):
                    pe.wait_ge(s["hq"], b + 1)
                    for j in range(2):
                        for f in range(KF):
                            o = (j * KF + f) * P
                            mm = pe.transpose(PB[:, 4 + p, o:o + P], hq[p][:, j, f * P:(f + 1) * P], identb[:, :])
                    mm.then_inc(s["htr"], 1)

                def down(b, p):
                    pe.wait_ge(s["ht"], b + 1)
                    if exists(b - 2):
                        pe.wait_ge(s["added"], b - 1)
                    for j in range(2):
                        for f in range(KF):
                            mm = pe.matmul(PS[:, 6 + p, j * D:(j + 1) * D], ht[p][:, j, f * P:(f + 1) * P],
                                           downq[:, f, :], start=(f == 0), stop=(f == KF - 1))
                    mm.then_inc(s["out_ps"], 1)

                def body(b, k, p):
                    if exists(b + 1):
                        up(b + 1, 1 - p)
                    turn(b, p)
                    down(b, p)

                each_batch(pe, lambda: up(0, 0), body, lambda: None)

            @block.scalar
            def _(act):
                def relu(b, p):
                    act.wait_ge(s["up_ps"], b + 1)
                    for j in range(2):
                        i = act.activation(h[p][:, j, :], PS[:, 2 * p + j, :], ACT.Relu,
                                           scale=osc0[:, bass.ds(b * 2 + j, 1)])
                    i.then_inc(s["h"], 1)

                def body(b, k, p):
                    if exists(b + 1):
                        relu(b + 1, 1 - p)
                    act.wait_ge(s["htr"], b + 1)
                    act.activation(ht[p][:, :, :].rearrange("p j f -> p (j f)"), PB[:, 4 + p, :], ACT.Copy)\
                       .then_inc(s["ht"], 1)

                each_batch(act, lambda: relu(0, 0), body, lambda: None)

            @block.gpsimd
            def _(pool):
                def stage(b, p):
                    pool.tensor_copy(xts[p][:, :, :], XT[:, bass.ds(b * 2, 2), :]).then_inc(s["xt"], 1)

                def body(b, k, p):
                    pool.wait_ge(s["h"], b + 1)
                    if exists(b + 2):
                        stage(b + 2, p)
                    pool.tensor_scalar(hr[p][:, 0, :], h[p][:, 0, :], MAGIC, -MAGIC, ALU.add, ALU.add)\
                        .then_inc(s["hr"], 1)

                def start():
                    for b in range(2):
                        stage(b, b)

                each_batch(pool, start, body, lambda: None)

            @block.vector
            def _(dve):
                def quantize(b, p):
                    dve.wait_ge(s["h"], b + 1)
                    dve.tensor_scalar(hr[p][:, 1, :], h[p][:, 1, :], MAGIC, -MAGIC, ALU.add, ALU.add)
                    dve.tensor_reduce(am[p][:, :], h[p][:, :, :], AX.X, ALU.max)
                    dve.drain()
                    dve.tensor_scalar(am[p][:, :], am[p][:, :], MAGIC, -MAGIC, ALU.add, ALU.add)
                    dve.drain()
                    dve.tensor_scalar(am[p][:, :], am[p][:, :], 127.0, EPS, ALU.min, ALU.max)
                    dve.drain()
                    dve.reciprocal(xsc[:, :], am[p][:, :])
                    dve.tensor_scalar(osc[p][:, :], am[p][:, :], 1.0 / 127, ws[:, 1:2], ALU.mult, ALU.mult)
                    dve.drain()
                    dve.tensor_scalar(xsc[:, :], xsc[:, :], 127.0, None, ALU.mult)
                    dve.drain()
                    for j in (1, 0):
                        if j == 0:
                            dve.wait_ge(s["hr"], b + 1)
                        dve.tensor_scalar(hr[p][:, j, :], hr[p][:, j, :], 127.0, xsc[:, j:j + 1],
                                          ALU.min, ALU.mult)
                    dve.drain()
                    dve.tensor_scalar(hq[p][:, :, :], hr[p][:, :, :], MAGIC, -MAGIC, ALU.add, ALU.add)\
                       .then_inc(s["hq"], 1)

                def add(b, p):
                    dve.wait_ge(s["out_ps"], b + 1)
                    for j in range(2):
                        i = b * 2 + j
                        x = dve.scalar_tensor_tensor(t.H[:, i, :], PS[:, 6 + p, j * D:(j + 1) * D],
                                                     osc[p][:, j:j + 1], t.H[:, i, :], ALU.mult, ALU.add)
                    x.then_inc(s["added"], 1)
                    dve.drain()
                    for j in range(2):
                        dve.bn_stats(t.BN[:, b * 2 + j, :], t.H[:, b * 2 + j, :])

                def body(b, k, p):
                    quantize(b, p)
                    if exists(b - 1):
                        add(b - 1, 1 - p)

                each_batch(dve, lambda: None, body, lambda: add(NB - 1, 1))


def convolution_kernel(nc, t, a, ctx, block):
    N = NSTATE

    def sb(n, shape, dt=F32):
        return ctx.enter_context(nc.sbuf_tensor(f"ssm_{n}", shape, dt))

    s = Sems(nc, ctx, "ssm", "loaded dt pe dve kernel zeros hankel")
    A, E, G = sb("a", [N, 2, N]), sb("e", [N, 2, N]), sb("g", [N, 2, N])
    inv_t, bc, ldt, dt = sb("inv_t", [N, N]), sb("bc", [N, 2]), sb("ldt", [N, 1]), sb("dt", [N, 1])
    flip = sb("flip", [P, P])
    V, C, eb = sb("v", [N, 16]), sb("c", [N, 16]), sb("eb", [N, 1])
    K, zeros = sb("k", [16, 16]), sb("zeros", [1, L])
    hankel = sb("hankel", [P, 2, P])
    KZ = nc.dram_tensor("ssm_kernel", [2 * L], F32).ap()
    loads = [(A, a["c_hippo"]), (inv_t, a["c_hippo_inv_t"]), (bc, a["ssm_bc"]), (ldt, a["ssm_log_dt"]),
             (flip, a["c_flip"])]
    PS = t.PS
    doublings = [(V, m) for m in (1, 2, 4, 8)] + [(C, m) for m in (1, 2, 4, 8)]
    TERMS = 8

    @block.sync
    def _(sp):
        for dst, src in loads:
            sp.dma_start(dst[tuple(slice(None) for _ in dst.shape)], src).then_inc(s["loaded"], 16)
        sp.wait_ge(s["zeros"], 1)
        sp.dma_start(KZ[L:2 * L].unsqueeze(0), zeros[:, :]).then_inc(s["kernel"], 16)
        sp.wait_ge(s["dve"], TERMS + SQUARINGS + 3 + 2 * len(doublings))
        sp.dma_start(KZ[0:L].rearrange("(i j) -> i j", i=16), K[:, :]).then_inc(s["kernel"], 16)
        sp.wait_ge(s["kernel"], 32)
        for n in range(2):
            sp.dma_start(hankel[:, n, :], bass.AP(KZ.tensor, P * (1 - n), [[1, P], [1, P]]))\
              .then_inc(s["hankel"], 16)

    @block.scalar
    def _(act):
        act.wait_ge(s["loaded"], 16 * len(loads))
        act.activation(dt[:, :], ldt[:, :], ACT.Exp).then_inc(s["dt"], 1)

    @block.tensor
    def _(pe):
        done = [0]

        def after_dve():
            done[0] += 1
            pe.wait_ge(s["dve"], done[0])

        def pair(x, y):
            after_dve()
            pe.matmul(PS[0:N, 0, 0:N], x[:, 1, :], y[:, 0, :], start=True, stop=True)
            pe.matmul(PS[0:N, 0, N:2 * N], x[:, 0, :], y[:, 1, :], start=True, stop=True)\
              .then_inc(s["pe"], 1)

        for _ in range(TERMS - 1):
            pair(A, G)
        pair(A, G)
        for _ in range(SQUARINGS):
            pair(E, E)
        after_dve()
        pe.matmul(PS[0:N, 0, 0:1], E[:, 1, :], bc[:, 0:1], start=True, stop=True).then_inc(s["pe"], 1)
        after_dve()
        pe.matmul(PS[0:N, 0, 0:1], inv_t[:, :], eb[:, :], start=True, stop=True).then_inc(s["pe"], 1)
        for n, (x, m) in enumerate(doublings):
            after_dve()
            side = E[:, 1, :] if x is V else E[:, 0, :]
            pe.matmul(PS[0:N, 0, 0:m], side, x[:, 0:m], start=True, stop=True).then_inc(s["pe"], 1)
            if n < len(doublings) - 1:
                pair(E, E)
        after_dve()
        pe.matmul(PS[0:16, 0, 0:16], C[:, :], V[:, :], start=True, stop=True).then_inc(s["pe"], 1)
        pe.wait_ge(s["hankel"], 32)
        for n in range(2):
            mm = pe.matmul(PS[:, 1, n * P:(n + 1) * P], hankel[:, n, :], flip[:, :], start=True, stop=True)
        mm.then_inc(s["pe"], 1)

    @block.vector
    def _(dve):
        done = [0]

        def after_pe():
            done[0] += 1
            dve.wait_ge(s["pe"], done[0])

        dve.memset(zeros[:, :], 0.0).then_inc(s["zeros"], 1)
        dve.wait_ge(s["dt"], 1)
        dve.tensor_scalar(A[:, :, :], A[:, :, :], dt[:, :], 2.0 ** -SQUARINGS, ALU.mult, ALU.mult)
        dve.tensor_copy(G[:, 0, :], t.ident[0:N, 0:N])
        dve.tensor_copy(G[:, 1, :], t.ident[0:N, 0:N])
        dve.drain()
        dve.nop().then_inc(s["dve"], 1)
        product = PS[0:N, 0, 0:2 * N].rearrange("p (h c) -> p h c", h=2)
        eye = t.ident[0:N, 0:N].unsqueeze(1).broadcast_to([N, 2, N])
        for n in range(TERMS, 1, -1):
            after_pe()
            dve.scalar_tensor_tensor(G[:, :, :], product, 1.0 / n, eye, ALU.mult, ALU.add)\
               .then_inc(s["dve"], 1)
        after_pe()
        dve.tensor_copy(E[:, :, :], product).then_inc(s["dve"], 1)

        def double():
            after_pe()
            dve.scalar_tensor_tensor(E[:, :, :], E[:, :, :], 2.0, product, ALU.mult, ALU.add)\
               .then_inc(s["dve"], 1)

        for _ in range(SQUARINGS):
            double()
        after_pe()
        dve.tensor_copy(eb[:, :], PS[0:N, 0, 0:1]).then_inc(s["dve"], 1)
        after_pe()
        dve.tensor_copy(V[:, 0:1], PS[0:N, 0, 0:1])
        dve.tensor_copy(C[:, 0:1], bc[:, 1:2])
        dve.drain()
        dve.nop().then_inc(s["dve"], 1)
        for n, (x, m) in enumerate(doublings):
            after_pe()
            dve.tensor_tensor(x[:, m:2 * m], x[:, 0:m], PS[0:N, 0, 0:m], ALU.add).then_inc(s["dve"], 1)
            if n < len(doublings) - 1:
                double()
        after_pe()
        dve.tensor_copy(K[:, :], PS[0:16, 0, 0:16]).then_inc(s["dve"], 1)
        after_pe()
        dve.tensor_copy(t.toep[:, :, :], PS[:, 1, 0:2 * P].rearrange("p (n c) -> p n c", n=2))


def state_space(nc, t, a):
    ln_scales(nc, t, "ssm_ln")
    with ExitStack() as ctx:
        s = Sems(nc, ctx, "conv", "skip u conv")
        skip = ctx.enter_context(nc.sbuf_tensor("ssm_skip", [P, 1], F32))
        U = ctx.enter_context(nc.sbuf_tensor("ssm_u", [P, NT, D], F32))
        PS = t.PS
        U4 = U[:, :, :].rearrange("p (b h) c -> p b h c", h=2)

        with nc.Block() as block:

            @block.sync
            def _(sp):
                sp.dma_start(skip[:, :], a["ssm_d"]).then_inc(s["skip"], 16)

            @block.tensor
            def _(pe):
                for g in range(4):
                    pe.wait_ge(s["u"], 8 * g + 8)
                    rhs = [U4[:, 4 * g:4 * g + 4, h, :] for h in range(2)]
                    pe.matmul(PS[:, 2 * g, :], t.toep[:, 0, :], rhs[0], start=True, stop=True)
                    pe.matmul(PS[:, 2 * g + 1, :], t.toep[:, 1, :], rhs[0], start=True, stop=False)
                    pe.matmul(PS[:, 2 * g + 1, :], t.toep[:, 0, :], rhs[1], start=False, stop=True)\
                      .then_inc(s["conv"], 1)

            @block.vector
            def _(dve):
                H4 = t.H[:, :, :].rearrange("p (b h) c -> p b h c", h=2)
                with dve.Fori(0, NT) as i:
                    dve.tensor_scalar(U[:, i, :], t.H[:, i, :], t.MEAN[:, bass.ds(i, 1)],
                                      t.RSTD[:, bass.ds(i, 1)], ALU.subtract, ALU.mult).then_inc(s["u"], 1)
                dve.drain()
                dve.wait_ge(s["skip"], 16)
                dve.scalar_tensor_tensor(t.H[:, :, :], U[:, :, :], skip[:, 0:1], t.H[:, :, :], ALU.mult, ALU.add)
                dve.drain()
                for g in range(4):
                    dve.wait_ge(s["conv"], g + 1)
                    for h in range(2):
                        dve.tensor_tensor(H4[:, 4 * g:4 * g + 4, h, :], H4[:, 4 * g:4 * g + 4, h, :],
                                          PS[:, 2 * g + h, :].rearrange("p (b c) -> p b c", b=4), ALU.add)
                dve.drain()
                with dve.Fori(0, NT // 8) as k:
                    for p in range(8):
                        dve.bn_stats(t.BN[:, k * 8 + p, :], t.H[:, k * 8 + p, :])


def bilinear_attention(nc, t, a):
    ln_scales(nc, t, "bil_ln")
    with ExitStack() as ctx:
        def sb(n, shape, dt=F32):
            return ctx.enter_context(nc.sbuf_tensor(f"bil_{n}", shape, dt))

        s = Sems(nc, ctx, "bil", "weights u tr ut v_ps v tq_ps tq st_ps mx exp pr_ps pr av_ps sums turned norm")
        s.restart(nc)
        wq, wv = sb("wq", [P, NH, D]), sb("wv", [P, D])
        two = range(2)
        us, ut = [sb(f"us{i}", [P, 2, D]) for i in two], [sb(f"ut{i}", [P, L]) for i in two]
        v, st = [sb(f"v{i}", [P, 2, NH, HS]) for i in two], sb("st", [P, 2, L])
        tq = [sb(f"tq{i}", [P, NH, L]) for i in two]
        nm = sb("nm", [P, NH, 2])
        pr = [sb(f"pr{i}", [P, 2, L]) for i in range(4)]
        pt = [sb(f"pt{i}", [P, NH, 2, L]) for i in two]
        rc, oc = sb("rc", [P, 2, NH]), sb("oc", [P, 2, NH, HD])
        attention_prelude(nc, t, s, None, None, v, [(wq, a["bil_q"]), (wv, a["bil_v"])])
        PS = t.PS
        LAG = 2
        A_BANK, SUMS = 6, 7

        def first(b, h, back):
            return isinstance(b, int) and b * NH + h < back

        with nc.Block() as block:

            @block.tensor
            def _(pe):
                def transpose_tokens(b, p):
                    pe.wait_ge(s["u"], b + 1)
                    if exists(b - 1):
                        pe.wait_ge(s["v"], b)
                    for h in range(2):
                        mm = pe.transpose(PS[:, A_BANK, h * P:(h + 1) * P], us[p][:, h, :], t.ident[:, :])
                    mm.then_inc(s["tr"], 1)

                def project_queries(b, p, n):
                    if n == 0:
                        pe.wait_ge(s["ut"], b + 1)
                    else:
                        pe.wait_ge(s["tq"], b * 4 + n)
                    for h in range(2):
                        mm = pe.matmul(PS[:, A_BANK, h * L:(h + 1) * L], wq[:, 2 * n + h, :], ut[p][:, :],
                                       start=True, stop=True)
                    mm.then_inc(s["tq_ps"], 1)

                def project_values(b, p):
                    pe.wait_ge(s["tq"], b * 4 + 4)
                    for h in range(2):
                        mm = pe.matmul(PS[:, A_BANK, h * D:(h + 1) * D], ut[p][:, h * P:(h + 1) * P],
                                       wv[:, :], start=True, stop=True)
                    mm.then_inc(s["v_ps"], 1)

                def scores(b, p, h):
                    if not first(b, h, 4):
                        pe.wait_ge(s["exp"], b * NH + h - 3)
                    if h == 0:
                        pe.wait_ge(s["tq"], b * 4 + 4)
                    for q in range(2):
                        mm = pe.matmul(PS[:, h % 4, q * L:(q + 1) * L], tq[p][:, h, q * P:(q + 1) * P],
                                       ut[p][:, :], start=True, stop=True)
                    mm.then_inc(s["st_ps"], 1)

                def turn(b, h):
                    pe.wait_ge(s["exp"], b * NH + h + 1)
                    if not first(b, h, 2):
                        pe.wait_ge(s["pr"], b * NH + h - 1)
                    for q in range(2):
                        for tile in range(2):
                            o = tile * L + q * P
                            mm = pe.transpose(PS[:, 4 + h % 2, o:o + P], pr[h % 4][:, q, tile * P:(tile + 1) * P],
                                              t.ident[:, :])
                    mm.then_inc(s["pr_ps"], 1)

                def sum_values(b, p, g):
                    if g == 0:
                        pe.wait_ge(s["pr"], b * NH + NH)
                        pe.wait_ge(s["v"], b + 1)
                        if exists(b - 1):
                            pe.wait_ge(s["norm"], b)
                    for tile in range(2):
                        for i in range(4):
                            mm = pe.matmul(PS[HS * i:HS * i + HS, SUMS, g * L:(g + 1) * L],
                                           v[p][:, tile, 4 * g + i, :], pt[p][:, 4 * g + i, tile, :],
                                           start=(tile == 0), stop=(tile == 1))
                    mm.then_inc(s["av_ps"], 1)

                def turn_sums(b):
                    pe.wait_ge(s["sums"], b + 1)
                    for q in range(2):
                        for g in range(2):
                            o = (q * 2 + g) * P
                            mm = pe.transpose(PS[:, SUMS, o:o + P], st[:, g, q * P:(q + 1) * P], t.ident[:, :])
                    mm.then_inc(s["turned"], 1)

                def start():
                    transpose_tokens(0, 0)
                    for n in range(4):
                        project_queries(0, 0, n)
                    project_values(0, 0)

                def body(b, k, p):
                    for h in range(NH):
                        scores(b, p, h)
                        if h >= LAG:
                            turn(b, h - LAG)
                        if h == 0 and exists(b + 1):
                            transpose_tokens(b + 1, 1 - p)
                        if h in (2, 3) and exists(b - 1):
                            sum_values(b - 1, 1 - p, h - 2)
                        if h == 6 and exists(b - 1):
                            turn_sums(b - 1)
                        if h in (1, 3, 5, 6) and exists(b + 1):
                            project_queries(b + 1, 1 - p, (1, 3, 5, 6).index(h))
                    for h in range(NH - LAG, NH):
                        if h == NH - 1 and exists(b + 1):
                            project_values(b + 1, 1 - p)
                        turn(b, h)

                def end():
                    for g in range(2):
                        sum_values(NB - 1, 1, g)
                    turn_sums(NB - 1)

                each_batch(pe, start, body, end)

            @block.scalar
            def _(act):
                def tokens(b, p):
                    act.wait_ge(s["tr"], b + 1)
                    act.activation(ut[p][:, :], PS[:, A_BANK, 0:L], ACT.Copy).then_inc(s["ut"], 1)

                def queries(b, p, n):
                    act.wait_ge(s["tq_ps"], b * 4 + n + 1)
                    act.activation(tq[p][:, 2 * n:2 * n + 2, :].rearrange("p h c -> p (h c)"),
                                   PS[:, A_BANK, :], ACT.Copy).then_inc(s["tq"], 1)

                def evict_sums(b):
                    act.wait_ge(s["av_ps"], b * 2 + 2)
                    act.activation(st[:, :, :].rearrange("p g c -> p (g c)"), PS[:, SUMS, :], ACT.Copy)\
                       .then_inc(s["sums"], 1)

                def start():
                    tokens(0, 0)
                    for n in range(4):
                        queries(0, 0, n)

                def body(b, k, p):
                    for h in range(NH):
                        act.wait_ge(s["mx"], b * NH + h + 1)
                        for q in range(2):
                            i = act.activation(pr[h % 4][:, q, :], PS[:, h % 4, q * L:(q + 1) * L], ACT.Exp,
                                               bias=nm[:, h, q:q + 1])
                        i.then_inc(s["exp"], 1)
                        if h == 0 and exists(b + 1):
                            tokens(b + 1, 1 - p)
                        if h in (1, 3, 5, 6) and exists(b + 1):
                            queries(b + 1, 1 - p, (1, 3, 5, 6).index(h))
                        if h == 4 and exists(b - 1):
                            evict_sums(b - 1)

                each_batch(act, start, body, lambda: evict_sums(NB - 1))

            @block.vector
            def _(dve):
                def normalize(b, p):
                    for h in range(2):
                        i = b * 2 + h
                        u = dve.tensor_scalar(us[p][:, h, :], t.H[:, i, :], t.MEAN[:, bass.ds(i, 1)],
                                              t.RSTD[:, bass.ds(i, 1)], ALU.subtract, ALU.mult)
                    u.then_inc(s["u"], 1)

                def values(b, p):
                    dve.wait_ge(s["v_ps"], b + 1)
                    dve.tensor_copy(v[p][:, :, :, 0:HD], PS[:, A_BANK, 0:2 * D].rearrange(
                        "q (j h d) -> q j h d", j=2, h=NH)).then_inc(s["v"], 1)

                def maxima(b, h):
                    dve.wait_ge(s["st_ps"], b * NH + h + 1)
                    dve.tensor_reduce(nm[:, h, :], PS[:, h % 4, :].rearrange("q (j c) -> q j c", j=2),
                                      AX.X, ALU.max, negate=True).then_inc(s["mx"], 1)

                def evict(b, p, h):
                    dve.wait_ge(s["pr_ps"], b * NH + h + 1)
                    dve.tensor_copy(pt[p][:, h].rearrange("q j c -> q (j c)"), PS[:, 4 + h % 2, :])\
                       .then_inc(s["pr"], 1)

                def add_attention(b):
                    dve.wait_ge(s["turned"], b + 1)
                    av = PS[:, SUMS, :].rearrange("q (j h e) -> q j h e", j=2, h=NH)
                    dve.reciprocal(rc[:, :, :], av[:, :, :, HD])
                    dve.drain()
                    dve.tensor_tensor(oc[:, :, :, :], av[:, :, :, 0:HD],
                                      rc[:, :, :].unsqueeze(3).broadcast_to([P, 2, NH, HD]), ALU.mult)\
                       .then_inc(s["norm"], 1)
                    dve.drain()
                    x = t.H[:, bass.ds(b * 2, 2), :]
                    dve.tensor_tensor(x, x, oc[:, :].rearrange("q j h d -> q j (h d)"), ALU.add)
                    dve.drain()
                    for q in range(2):
                        dve.bn_stats(t.BN[:, b * 2 + q, :], t.H[:, b * 2 + q, :])

                def start():
                    for b in range(2):
                        normalize(b, b)
                    values(0, 0)

                def body(b, k, p):
                    for h in range(NH):
                        maxima(b, h)
                        if h >= LAG:
                            evict(b, p, h - LAG)
                        if h == 1 and exists(b - 2):
                            add_attention(b - 2)
                    for h in range(NH - LAG, NH):
                        if h == NH - 1 and exists(b + 1):
                            values(b + 1, 1 - p)
                        evict(b, p, h)
                    if exists(b + 2):
                        normalize(b + 2, p)

                def end():
                    for b in (NB - 2, NB - 1):
                        add_attention(b)

                each_batch(dve, start, body, end)


def expert_choice(nc, t, a, out):
    ln_scales(nc, t, "ec_ln")
    rows = out.rearrange("b l c -> (b l) c")
    NG = EC // ECG
    with ExitStack() as ctx:
        def sb(n, shape, dt=F32):
            return ctx.enter_context(nc.sbuf_tensor(f"ec_{n}", shape, dt))

        s = Sems(nc, ctx, "ec", "weights staged tr tt logits exp_in exp probs turned in_rows picked picked_t idx "
                                "u_sent h_sent gathered0 gathered1 gathered2 gathered3 gathered4 gathered5 "
                                "gathered6 gathered7 xg_staged xtr xt up_ps hid out_ps y scattered freed "
                                "up0 up1 down0 down1 late table table_sent decoded0 decoded1")
        s.restart(nc)
        UD = nc.dram_tensor("ec_tokens", [NT * P, D], F32).ap()
        TABLE = nc.dram_tensor("ec_candidates", [EC * 4 * ECK, 1], U32).ap()
        wr, br = sb("wr", [P, EC]), sb("br", [P, EC])
        bup, bdown = sb("bup", [P, NG, 3]), sb("bdown", [P, EC, D])
        vals_t, place_u, idx_u = sb("vals_t", [P, EC]), sb("place_u", [P, EC], U32), sb("idx_u", [P, EC], U32)
        PS = t.PS
        two = range(2)

        with ExitStack() as sub:
            def tb(n, shape, dt=F32):
                return sub.enter_context(nc.sbuf_tensor(f"ec_{n}", shape, dt))

            U = tb("u", [P, NT, D])
            tt = [tb(f"tt{i}", [P, 4, P]) for i in two]
            logits = PS[:, 2:4, :].rearrange("p a b -> p (a b)")
            LG, sm = tb("lg", [P, NT, EC]), tb("sm", [P, NT])
            quarters, qvals, qidx = tb("quarters", [P, NT * P // 4]), tb("qvals", [P, ECK]), tb("qidx", [P, ECK], U32)
            idxf, tokens, base = tb("idxf", [P, ECK]), tb("cand_token", [P, ECK], U32), tb("cand_base", [P, 2])
            row, vals, idx = tb("row", [EC, 4 * ECK]), tb("vals", [EC, ECK]), tb("idx", [EC, ECK], U32)
            placef = tb("placef", [EC, ECK])

            with nc.Block() as block:

                @block.sync
                def _(sp):
                    sp.dma_start(wr[:, :], a["ec_wr"]).then_inc(s["weights"], 16)
                    sp.dma_start(br[:, :], a["ec_br"]).then_inc(s["weights"], 16)
                    sp.dma_start(base[:, :], a["c_ec_base"]).then_inc(s["weights"], 16)
                    sp.dma_start(bup[:, :, :], a["ec_bup"]).then_inc(s["late"], 16)
                    sp.dma_start(bdown[:, :, :], a["ec_bdown"]).then_inc(s["late"], 16)
                    sp.dma_start(rows.rearrange("(i p) c -> p i c", p=P), t.H[:, :, :]).then_inc(s["h_sent"], 16)
                    sp.wait_ge(s["staged"], NT // 8)
                    sp.dma_start(UD.rearrange("(i p) c -> p i c", p=P), U[:, :, :]).then_inc(s["u_sent"], 16)
                    sp.wait_ge(s["u_sent"], 16)
                    sp.wait_ge(s["table"], 1)
                    for q in range(4):
                        sp.dma_start(TABLE.rearrange("(e q r) o -> q e (r o)", q=4, r=ECK)[q],
                                     tokens[EC * q:EC * q + EC, :]).then_inc(s["table_sent"], 16)
                    sp.wait_ge(s["table_sent"], 64)
                    sp.wait_ge(s["h_sent"], 16)
                    sp.wait_ge(s["late"], 32)

                @block.tensor
                def _(pe):
                    pe.wait_ge(s["weights"], 48)
                    for g in range(NT // 4 + 1):
                        if g < NT // 4:
                            pe.wait_ge(s["staged"], g // 2 + 1)
                            if g >= 2:
                                pe.wait_ge(s["tt"], g - 1)
                            for i in range(4):
                                mm = pe.transpose(PS[:, g % 2, i * P:(i + 1) * P], U[:, 4 * g + i, :], t.ident[:, :])
                            mm.then_inc(s["tr"], 1)
                        if g:
                            pe.wait_ge(s["tt"], g)
                            for i in range(4):
                                o = (4 * g - 4 + i) * EC
                                mm = pe.matmul(logits[:, o:o + EC], tt[(g - 1) % 2][:, i, :], wr[:, :],
                                               start=True, stop=True)
                            mm.then_inc(s["logits"], 1)
                    pe.wait_ge(s["probs"], 1)
                    for i in range(NT):
                        mm = pe.transpose(PS[0:EC, i // 4, (i % 4) * P:(i % 4 + 1) * P], LG[:, i, :], t.ident[:, :])
                        if i % 4 == 3:
                            mm.then_inc(s["turned"], 1)
                    pe.wait_ge(s["picked"], 1)
                    pe.transpose(PS[:, 0, 0:EC], vals[:, :], t.ident[0:EC, 0:EC])
                    pe.transpose(PS[:, 0, EC:2 * EC], placef[:, :], t.ident[0:EC, 0:EC]).then_inc(s["picked_t"], 1)

                @block.scalar
                def _(act):
                    for g in range(NT // 4):
                        act.wait_ge(s["tr"], g + 1)
                        act.activation(tt[g % 2][:, :, :].rearrange("c i r -> c (i r)"), PS[:, g % 2, :],
                                       ACT.Copy).then_inc(s["tt"], 1)
                    act.wait_ge(s["exp_in"], 1)
                    act.activation(LG[:, :, :], LG[:, :, :], ACT.Exp).then_inc(s["exp"], 1)

                @block.vector
                def _(dve):
                    dve.wait_ge(s["weights"], 48)
                    with dve.Fori(0, NT // 8) as k:
                        for p in range(8):
                            i = k * 8 + p
                            u = dve.tensor_scalar(U[:, i, :], t.H[:, i, :], t.MEAN[:, bass.ds(i, 1)],
                                                  t.RSTD[:, bass.ds(i, 1)], ALU.subtract, ALU.mult)
                        u.then_inc(s["staged"], 1)
                    dve.wait_ge(s["logits"], NT // 4)
                    dve.tensor_tensor(LG[:, :, :], logits.rearrange("p (i e) -> p i e", e=EC),
                                      br[:, :].unsqueeze(1).broadcast_to([P, NT, EC]), ALU.add)
                    dve.drain()
                    dve.tensor_reduce(sm[:, :], LG[:, :, :], AX.X, ALU.max)
                    dve.drain()
                    over = sm[:, :].unsqueeze(2).broadcast_to([P, NT, EC])
                    dve.tensor_tensor(LG[:, :, :], LG[:, :, :], over, ALU.subtract).then_inc(s["exp_in"], 1)
                    dve.wait_ge(s["exp"], 1)
                    dve.tensor_reduce(sm[:, :], LG[:, :, :], AX.X, ALU.add)
                    dve.drain()
                    dve.reciprocal(sm[:, :], sm[:, :])
                    dve.drain()
                    dve.tensor_tensor(LG[:, :, :], LG[:, :, :], over, ALU.mult).then_inc(s["probs"], 1)
                    for b in range(8):
                        dve.wait_ge(s["turned"], b + 1)
                        q, o = b // 2, b % 2 * 512
                        dve.tensor_copy(quarters[EC * q:EC * q + EC, o:o + 512], PS[0:EC, b, :])
                    dve.drain()

                    def best(values, index, row):
                        for r in range(ECK // 8):
                            v8 = values[:, 8 * r:8 * r + 8]
                            dve.max(v8, row[:, :])
                            dve.drain()
                            dve.max_index(index[:, 8 * r:8 * r + 8], v8, row[:, :])
                            dve.drain()
                            dve.match_replace(row[:, :], v8, row[:, :], -1.0)
                            dve.drain()

                    best(qvals, qidx, quarters)
                    dve.tensor_copy(idxf[:, :], qidx[:, :])
                    for q in range(4):
                        dve.tensor_copy(row[:, q * ECK:(q + 1) * ECK], qvals[EC * q:EC * q + EC, :])
                    dve.drain()
                    dve.tensor_scalar(tokens[:, :], idxf[:, :], base[:, 0:1], None, ALU.add).then_inc(s["table"], 1)
                    best(vals, idx, row)
                    dve.tensor_copy(placef[:, :], idx[:, :])
                    dve.drain()
                    dve.tensor_scalar(placef[:, :], placef[:, :], base[0:EC, 1:2], None, ALU.add)\
                       .then_inc(s["picked"], 1)
                    dve.wait_ge(s["picked_t"], 1)
                    dve.tensor_copy(vals_t[:, :], PS[:, 0, 0:EC])
                    dve.tensor_copy(place_u[:, :], PS[:, 0, EC:2 * EC])

        XG = sb("xg", [P, EC, D])
        wu = [sb(f"wu{i}", [P, ECF]) for i in two]
        wd = [sb(f"wd{i}", [P, ECG, 3, D]) for i in two]
        xg, xt = [sb(f"xgs{i}", [P, ECG, D]) for i in two], [sb(f"xt{i}", [P, ECG * P]) for i in two]
        hid = [sb(f"hid{i}", [P, 3, ECG * P]) for i in two]
        y = [sb(f"y{i}", [P, ECG, D]) for i in two]
        with nc.Block() as block:

            @block.sync
            def _(sp):
                with sp.Fori(0, NG // 2) as k:
                    for p in two:
                        g = k * 2 + p
                        sp.wait_ge(s["hid"], g * 3 + 3)
                        sp.dma_start(wu[p][:, :], a["ec_up"][bass.ds(g, 1)].rearrange("g h f -> h (g f)"))\
                          .then_inc(s[f"up{p}"], 16)
                        sp.wait_ge(s["out_ps"], g + 1)
                        down = a["ec_down"][bass.ds(g * ECG, ECG)]
                        for j, (f, n) in enumerate(ECT):
                            sp.dma_start(wd[p][0:n, :, j, :], down[:, f:f + n, :].rearrange("j f c -> f j c"))\
                              .then_inc(s[f"down{p}"], 16)

            @block.gpsimd
            def _(pool):
                def gather(e):
                    pool.indirect_dma_start(out=XG[:, e, :], out_offset=None, in_=UD,
                                            in_offset=bass.IndirectOffsetOnAxis(ap=idx_u[:, e:e + 1], axis=0))\
                        .then_inc(s[f"gathered{e // ECG}"], 16)

                def add(e):
                    if e:
                        pool.wait_ge(s["scattered"], 16 * e)
                        if e % ECG == 0:
                            pool.nop().then_inc(s["freed"], 1)
                    pool.wait_ge(s["y"], 2 + e // ECG + 1)
                    pool.indirect_dma_start(out=rows, out_offset=bass.IndirectOffsetOnAxis(ap=idx_u[:, e:e + 1], axis=0),
                                            in_=y[e // ECG % 2][:, e % ECG, :], in_offset=None,
                                            compute_op=ALU.add).then_inc(s["scattered"], 16)

                def decode(e, sem):
                    pool.indirect_dma_start(out=idx_u[:, e:e + 1], out_offset=None, in_=TABLE,
                                            in_offset=bass.IndirectOffsetOnAxis(ap=place_u[:, e:e + 1], axis=0))\
                        .then_inc(sem, 16)

                AHEAD = 3 * ECG
                pool.nop().then_inc(s["freed"], 2)
                for e in range(AHEAD):
                    decode(e, s["decoded0"])
                pool.wait_ge(s["decoded0"], 16 * AHEAD)
                for e in range(AHEAD):
                    gather(e)
                for e in range(AHEAD, EC):
                    decode(e, s["decoded1"])
                pool.wait_ge(s["decoded1"], 16 * (EC - AHEAD))
                for e in range(EC):
                    add(e)
                    if e + AHEAD < EC:
                        gather(e + AHEAD)
                pool.wait_ge(s["scattered"], 16 * EC)

            @block.tensor
            def _(pe):
                pe.nop().then_inc(s["out_ps"], 2)
                with pe.Fori(0, NG // 2) as k:
                    for p in two:
                        g = k * 2 + p
                        pe.wait_ge(s["xg_staged"], g + 1)
                        for j in range(ECG):
                            mm = pe.transpose(PS[:, p, j * P:(j + 1) * P], xg[p][:, j, :], t.ident[:, :])
                        mm.then_inc(s["xtr"], 1)
                        pe.wait_ge(s["xt"], g + 1)
                        pe.wait_ge(s[f"up{p}"], k * 16 + 16)
                        for j, (f, n) in enumerate(ECT):
                            pe.wait_ge(s["hid"], g * 3 + j + 4)
                            pe.matmul(PS[0:n, 2 + j, :], wu[p][:, f:f + n], xt[p][:, :], start=True, stop=True)\
                              .then_inc(s["up_ps"], 1)
                        pe.wait_ge(s["hid"], g * 3 + 9)
                        pe.wait_ge(s[f"down{p}"], k * 48 + 48)
                        pe.wait_ge(s["y"], g + 1)
                        for e in range(ECG):
                            for j, (f, n) in enumerate(ECT):
                                mm = pe.matmul(PS[:, 5 + p, e * D:(e + 1) * D], hid[p][0:n, j, e * P:(e + 1) * P],
                                               wd[p][0:n, e, j, :], start=(j == 0), stop=(j == 2))
                        mm.then_inc(s["out_ps"], 1)

            @block.scalar
            def _(act):
                act.nop().then_inc(s["hid"], 6)
                with act.Fori(0, NG // 2) as k:
                    for p in two:
                        g = k * 2 + p
                        act.wait_ge(s["xtr"], g + 1)
                        act.activation(xt[p][:, :], PS[:, p, :], ACT.Copy).then_inc(s["xt"], 1)
                        for j, (f, n) in enumerate(ECT):
                            act.wait_ge(s["up_ps"], g * 3 + j + 1)
                            act.activation(hid[p][0:n, j, :], PS[0:n, 2 + j, :], ACT.Silu,
                                           bias=bup[0:n, bass.ds(g, 1), j]).then_inc(s["hid"], 1)

            @block.vector
            def _(dve):
                dve.nop().then_inc(s["y"], 2)
                for g in range(NG):
                    p = g % 2
                    dve.wait_ge(s[f"gathered{g}"], 16 * ECG)
                    dve.tensor_copy(xg[p][:, :, :], XG[:, g * ECG:(g + 1) * ECG, :])\
                       .then_inc(s["xg_staged"], 1)
                    dve.wait_ge(s["out_ps"], g + 3)
                    dve.wait_ge(s["freed"], g + 1)
                    dve.tensor_tensor(y[p][:, :, :], PS[:, 5 + p, :].rearrange("r (e c) -> r e c", e=ECG),
                                      bdown[:, g * ECG:(g + 1) * ECG, :], ALU.add)
                    dve.drain()
                    dve.tensor_tensor(y[p][:, :, :], y[p][:, :, :],
                                      vals_t[:, g * ECG:(g + 1) * ECG].unsqueeze(2).broadcast_to([P, ECG, D]),
                                      ALU.mult).then_inc(s["y"], 1)


def alloc_shared(nc, t, ctx):
    def sb(name, shape, dt=F32):
        return ctx.enter_context(nc.sbuf_tensor(name, shape, dt))

    t.H = sb("hidden", [P, NT, D])
    t.BN = sb("bn", [P, NT, 6])
    t.MEAN = sb("mean", [P, NT])
    t.RSTD = sb("rstd", [P, NT])
    t.ident = sb("ident", [P, P])
    t.toep = sb("toeplitz", [P, 2, P])
    t.ident16 = sb("ident16", [P, P], BF16)
    t.ln_sems, t.ln_uses = Sems(nc, ctx, "ln", "var_ready root_ready"), 0
    t.mha_sems = Sems(nc, ctx, "mha", ATTENTION_SEMS)
    t.moe_sems = Sems(nc, ctx, "moe", EXPERT_SEMS)
    t.PS = ctx.enter_context(nc.psum_tensor("psum", [P, 8, 512], F32))
    t.XS1 = nc.dram_tensor("expert_in1", [TILES1 * P, D], F32).ap()
    t.XS2 = nc.dram_tensor("expert_in2", [TILES2 * P, D], F32).ap()


def build(nc, a, out):
    t = NS()
    with ExitStack() as ctx:
        alloc_shared(nc, t, ctx)
        with ExitStack() as tok:
            t.w1 = tok.enter_context(nc.sbuf_tensor("w1", [NF, 2, NHID * NF], F32))
            t.b1 = tok.enter_context(nc.sbuf_tensor("b1", [NF, NHID], F32))
            t.w2 = tok.enter_context(nc.sbuf_tensor("w2", [NF, NHID, D], F32))
            t.b2 = tok.enter_context(nc.sbuf_tensor("b2", [P, D], F32))
            t.dft = tok.enter_context(nc.sbuf_tensor("dft", [HP, 2, 2, NF], F32))
            setup(nc, t, a, tok)
            tokenizer(nc, t, a)

        def attention_and_experts():
            with ExitStack() as sub:
                t.R = sub.enter_context(nc.sbuf_tensor("attended", [P, NT, D], F32))
                full_attention(nc, t, a, "l0mha")
                experts_layer(nc, t, a, "l0moe")

        steps = [lambda: windowed_attention(nc, t, a, ctx),
                 attention_and_experts,
                 lambda: full_attention(nc, t, a, "l1mha"),
                 lambda: bitlinear_ffn(nc, t, a),
                 lambda: state_space(nc, t, a),
                 lambda: experts_layer(nc, t, a, "l2moe"),
                 lambda: bilinear_attention(nc, t, a),
                 lambda: expert_choice(nc, t, a, out)]
        for step in steps:
            step()


def heads_inside(w):
    return w.reshape(w.shape[:-1] + (NH, HD)).swapaxes(-1, -2).reshape(w.shape)


def on_all(row):
    return np.ascontiguousarray(np.broadcast_to(row, (P,) + row.shape))


def constants():
    n = np.arange(PATCH)
    f = np.arange(NF)
    w = 2 * np.pi * ((n[:, None] * f[None, :]) % PATCH) / PATCH
    sin = np.where((f[None, :] * 2) % PATCH == 0, 0.0, np.sin(w))
    dft = np.stack([np.cos(w), -sin], 1).reshape(2, HP, 2, NF).transpose(1, 0, 2, 3)
    c = {"c_ident": np.eye(P), "c_dft": dft}
    win = np.arange(WT) // WIN
    blocks, win_sel = np.zeros((P, WT)), np.zeros((P, NH + 1, WT))
    for r in range(3 * NH):
        win_sel[r, r % NH] = 1
    for w_ in range(WT // WIN):
        blocks[32 + w_] = win == w_
        win_sel[32 + w_] = np.where(win == w_, 0.0, NEG)
    c["c_blocks"], c["c_win_sel"] = blocks, win_sel
    cnt = np.zeros(L)
    for w_ in range(NW):
        cnt[w_ * HOP:w_ * HOP + WIN] += 1
    c["c_cover"] = (cnt > 0).reshape(2, P).T
    c["c_share"] = (1.0 / np.maximum(cnt, 1)).reshape(2, P).T
    sel = np.zeros((P, NH, P))
    for r in range(3 * NH):
        sel[r, r % NH] = 1
    c["c_sel"] = sel
    c["c_before"] = np.triu(np.ones((P, P)), 1)
    c["c_order"] = np.broadcast_to((NE - np.arange(NE))[None, :, None], (P, NE, NT))
    c["c_chain"] = np.broadcast_to((np.arange(NT) > 0)[None, None, :], (P, NE, NT))
    r = np.arange(P)
    c["c_ec_base"] = np.stack([r // EC * (NT * P // 4), r % EC * 4 * ECK], 1)
    q = np.sqrt(1 + 2 * np.arange(NSTATE))
    hippo = -(np.tril(q[:, None] * q[None, :]) - np.diag(np.arange(NSTATE)))
    c["c_hippo"] = np.stack([hippo, hippo.T], 1)
    c["c_hippo_inv_t"] = np.linalg.inv(hippo).T
    c["c_flip"] = np.eye(P)[::-1]
    return {k: np.ascontiguousarray(v, dtype=np.float32) for k, v in c.items()}


def arrays(i):
    a = dict(constants())
    a["x"] = i["x"]
    a["tok_w1"] = i["L0_tok_w1"].reshape(2, NF, NHID * NF).transpose(1, 0, 2)
    a["tok_b1"] = i["L0_tok_b1"].reshape(NHID, NF).T
    a["tok_w2"] = i["L0_tok_w2"].reshape(NHID, NF, D).transpose(1, 0, 2)
    a["tok_b2"] = on_all(i["L0_tok_b2"])
    w_in, b_in = i["L0_attn_w_in"], i["L0_attn_b_in"]
    a["win_gb"] = np.stack([i["L0_attn_ln_g"], i["L0_attn_ln_b"]], 1)

    def attention(name, wq, wk, wv, wo, bq, bk, bv, bo):
        a[name + "_wqk"] = np.stack([heads_inside(wq), heads_inside(wk)], 1)
        a[name + "_wvo"] = np.stack([wv, wo], 1)
        a[name + "_bqk"] = np.stack([heads_inside(bq), heads_inside(bk)], 1)
        a[name + "_bvo"] = on_all(np.stack([bv, bo]))

    attention("win", w_in[:D].T, w_in[D:2 * D].T, w_in[2 * D:].T, i["L0_attn_w_out"].T,
              b_in[:D], b_in[D:2 * D], b_in[2 * D:], i["L0_attn_b_out"])
    attention("l0mha", *(i["L0_ffn_" + n] for n in ("Wq", "Wk", "Wv", "Wo", "bq", "bk", "bv", "bo")))
    flat = [i["L1_attn_" + n].transpose(1, 0, 2).reshape(D, D) for n in ("Wq", "Wk", "Wv")]
    attention("l1mha", *flat, i["L1_attn_Wo"], *(i["L1_attn_" + n].reshape(D) for n in ("bq", "bk", "bv")),
              i["L1_attn_bo"])

    def moe(name, g, b, gate_w, gate_b, w1, b1, w2, b2):
        a[name + "_gb"] = np.stack([g, b], 1)
        a[name + "_gate_w"] = gate_w
        a[name + "_gate_b"] = on_all(gate_b)
        a[name + "_w1"] = np.concatenate(
            [w1.transpose(1, 0, 2), b1.reshape(NE, KF, P).transpose(2, 0, 1)], 2)
        a[name + "_w2"] = w2.reshape(NE, KF, P, D).transpose(2, 0, 1, 3)
        a[name + "_b2"] = on_all(b2)

    moe("l0moe", i["L0_ffn_ln1_g"], i["L0_ffn_ln1_b"], i["L0_ffn_gate_W"], i["L0_ffn_gate_b"],
        i["L0_ffn_W1"], i["L0_ffn_b1"], i["L0_ffn_W2"], i["L0_ffn_b2"])
    moe("l2moe", i["L2_ffn_ln_g"], i["L2_ffn_ln_b"], i["L2_ffn_w_r"].T, i["L2_ffn_b_r"],
        i["L2_ffn_W1"], i["L2_ffn_b1"], i["L2_ffn_W2"], i["L2_ffn_b2"])
    a["l0moe_gb"] = on_all(np.stack([i["L0_ffn_ln1_g"], i["L0_ffn_ln1_b"]]))
    a["l2moe_gb"] = on_all(np.stack([i["L2_ffn_ln_g"], i["L2_ffn_ln_b"]]))
    a["bit_up"] = i["L1_ffn_w_up"].T
    a["bit_down"] = i["L1_ffn_w_down"].T.reshape(KF, P, D).transpose(1, 0, 2)
    a["ssm_bc"] = np.stack([i["L2_attn_B_ssm"][:, 0], i["L2_attn_C_ssm"][0]], 1)
    a["ssm_d"] = on_all(i["L2_attn_D_skip"])
    a["ssm_log_dt"] = on_all(i["L2_attn_log_dt"])[:NSTATE]
    a["bil_q"] = i["L3_attn_Q"].transpose(1, 0, 2)
    a["bil_v"] = i["L3_attn_V"].transpose(1, 0, 2).reshape(D, D)
    a["ec_wr"] = i["L3_ffn_W_router"]
    a["ec_br"] = on_all(i["L3_ffn_b_router"])
    a["ec_up"] = i["L3_ffn_W_up"]
    pad = np.zeros((EC // ECG, 3 * P), np.float32)
    pad[:, :ECF] = i["L3_ffn_b_up"]
    a["ec_bup"] = pad.reshape(EC // ECG, 3, P).transpose(2, 0, 1)
    a["ec_down"] = i["L3_ffn_W_down"]
    a["ec_bdown"] = on_all(i["L3_ffn_b_down"])
    return {k: np.ascontiguousarray(v) for k, v in a.items()}


TILES1 = 40
TILES2 = 72


def kernel(**inputs):
    import concourse.bacc as bacc
    from concourse.bass_utils import run_bass_kernel_spmd

    given = arrays({k: np.asarray(v) for k, v in inputs.items()})
    nc = bacc.Bacc("TRN2", target_bir_lowering=False, num_devices=1)
    aps = {k: nc.dram_tensor(f"in_{k}", v.shape, mybir.dt.from_np(v.dtype), kind="ExternalInput").ap()
           for k, v in given.items()}
    out = nc.dram_tensor("out_0", (NB, L, D), F32, kind="ExternalOutput").ap()
    build(nc, aps, out)
    r = run_bass_kernel_spmd(nc, [{f"in_{k}": v for k, v in given.items()}], core_ids=[0])
    return r.results[0]["out_0"]
```
